# Optimizing a Trainium2 kernel written in Bass

```python
import numpy as np
import jax
import jax.numpy as jnp

def _softmax(x, axis=-1):
    return jax.nn.softmax(x, axis=axis)

def _gelu(x):
    return jax.nn.gelu(x, approximate=True)

def _silu(x):
    return jax.nn.silu(x)

def _sigmoid(x):
    return jax.nn.sigmoid(x)

def _layernorm(x, axis=-1, eps=1e-05):
    m = jnp.mean(x, axis=axis, keepdims=True)
    v = jnp.var(x, axis=axis, keepdims=True)
    return (x - m) / jnp.sqrt(v + eps)

def _scatter_add(tgt, idx, src, axis=0):
    return tgt.at[idx].add(src)

def _segment_sum(src, seg, n):
    return jax.ops.segment_sum(src, seg, n)
kernel_name = 'mk_flamingo_gated_d2_seqx_r8_e455d4'

def setup_inputs(seed: int=0):
    np.random.seed(seed)
    _w = jnp.asarray

    def _rec_inputs():
        import jax
        import jax.numpy as jnp
        _rk = jax.random.key(seed)
        x = -0.0003929 + 0.9999 * jax.random.normal(jax.random.fold_in(_rk, 1), (16, 256, 128), jnp.float32)
        _lenS = 256 - jax.random.randint(jax.random.fold_in(_rk, 7), (16,), 0, max(1, 256 // 4) + 1, jnp.int32)
        _lenS2 = 64 - jax.random.randint(jax.random.fold_in(_rk, 8), (16,), 0, max(1, 64 // 4) + 1, jnp.int32)
        _ctx_1024P = jax.random.normal(jax.random.fold_in(_rk, 11), (16, 16, 128), jnp.float32)
        _ctx_1024c = jax.random.dirichlet(jax.random.fold_in(_rk, 511), 0.3 * jnp.ones((16,), jnp.float32), (16, 64))
        _ctx_1024t = jnp.einsum('bsk,bkd->bsd', _ctx_1024c, _ctx_1024P)
        _ctx_1024t = _ctx_1024t * jax.lax.rsqrt(jnp.mean(jnp.square(_ctx_1024t)) + 1e-12) * 0.953939
        ctx_1024 = -0.000514642 + 1.00011 * (_ctx_1024t + 0.3 * jax.random.normal(jax.random.fold_in(_rk, 611), (16, 64, 128), jnp.float32))
        _validS = jnp.arange(256)[None, :] < _lenS[:, None]
        _validS2 = jnp.arange(64)[None, :] < _lenS2[:, None]
        _causal = jnp.tril(jnp.ones((256, 256), dtype=bool))
        mask_BxS2_bk0 = jnp.logical_not(jnp.broadcast_to(_validS2[:, :], (16, 64)))
        mask_BxSxS2_ff1 = jnp.where(jnp.ones((16, 256, 64), dtype=bool), 1.0, 0.0).astype(jnp.float32)
        mask_BxS2_ff1 = jnp.where(jnp.ones((16, 64), dtype=bool), 1.0, 0.0).astype(jnp.float32)
        _g = jax.random.normal(jax.random.fold_in(_rk, 9001), (2, 2), jnp.float32)
        _g = jnp.sign(_g) * jnp.maximum(jnp.abs(_g), 1.0) + (_g == 0) * 1.0
        g_xattn = _g[0]
        g_ffn = _g[1]
        return (x, ctx_1024, mask_BxS2_bk0, mask_BxSxS2_ff1, mask_BxS2_ff1, g_xattn, g_ffn)
    x, ctx_1024, mask_BxS2_bk0, mask_BxSxS2_ff1, mask_BxS2_ff1, g_xattn, g_ffn = _rec_inputs()

    def _L0_xattn_setup():
        import jax, jax.numpy as jnp
        import numpy as np
        DIM = 128
        HEADS = 16
        HEAD_DIM = DIM // HEADS
        B, N, S = (4, 512, 64)
        key = jax.random.key(seed)
        ks = jax.random.split(key, 9)
        scale = DIM ** (-0.5)
        return {'x': jax.random.normal(ks[0], (B, N, DIM), dtype=jnp.float32), 'context': jax.random.normal(ks[1], (B, S, DIM), dtype=jnp.float32), 'context_mask': jax.random.uniform(ks[2], (B, S)) < 0.2, 'q_w': jax.random.normal(ks[3], (DIM, DIM), dtype=jnp.float32) * scale, 'q_b': jnp.zeros((DIM,), dtype=jnp.float32), 'kv_w': jax.random.normal(ks[4], (DIM, 2 * DIM), dtype=jnp.float32) * scale, 'kv_b': jnp.zeros((2 * DIM,), dtype=jnp.float32), 'proj_w': jax.random.normal(ks[5], (DIM, DIM), dtype=jnp.float32) * scale, 'proj_b': jnp.zeros((DIM,), dtype=jnp.float32)}
    _L0_xattn_all = _L0_xattn_setup()
    _L0_xattn_in = {k: v for k, v in _L0_xattn_all.items() if k in ('q_w', 'q_b', 'kv_w', 'kv_b', 'proj_w', 'proj_b')}
    del _L0_xattn_all

    def _L0_ffn_setup():
        import jax, jax.numpy as jnp
        import numpy as np
        B, T, D = (2, 256, 128)
        F = 512
        E = 8
        key = jax.random.key(seed)
        k0, k1, k2, k3 = jax.random.split(key, 4)
        x = jax.random.normal(k0, (B, T, D), dtype=jnp.float32)
        Wg = jax.random.normal(k1, (E, D), dtype=jnp.float32) * 0.02
        W1 = jax.random.normal(k2, (E, D, F), dtype=jnp.float32) * 0.02
        W2 = jax.random.normal(k3, (E, F, D), dtype=jnp.float32) * 0.02
        return {'x': x, 'Wg': Wg, 'W1': W1, 'W2': W2}
    _L0_ffn_all = _L0_ffn_setup()
    _L0_ffn_in = {k: v for k, v in _L0_ffn_all.items() if k in ('Wg', 'W1', 'W2')}
    del _L0_ffn_all

    def _L1_xattn_setup():
        import jax, jax.numpy as jnp
        import numpy as np
        key = jax.random.key(seed)
        ks = jax.random.split(key, 5)
        B, S, D = (8, 256, 128)
        return {'query': jax.random.normal(ks[0], (B, S, D), dtype=jnp.float32), 'key': jax.random.normal(ks[1], (B, S, D), dtype=jnp.float32), 'value': jax.random.normal(ks[2], (B, S, D), dtype=jnp.float32), 'cell_mask': jnp.ones((B, S, S), dtype=jnp.float32), 'seq_mask': jnp.ones((B, S), dtype=jnp.float32), 'W_k': jax.random.normal(ks[3], (D, D), dtype=jnp.float32) * (1.0 / np.sqrt(D)), 'b_k': jnp.zeros((D,), dtype=jnp.float32), 'W_o': jax.random.normal(ks[4], (D, D), dtype=jnp.float32) * (1.0 / np.sqrt(D)), 'b_o': jnp.zeros((D,), dtype=jnp.float32)}
    _L1_xattn_all = _L1_xattn_setup()
    _L1_xattn_in = {k: v for k, v in _L1_xattn_all.items() if k in ('W_k', 'b_k', 'W_o', 'b_o')}
    del _L1_xattn_all

    def _L1_ffn_setup():
        import jax, jax.numpy as jnp
        import numpy as np
        N, T, D = (4, 512, 128)
        NUM_EXPERTS = 8
        EXPERT_CAP = 2.0
        MLP_RATIO = 4
        HIDDEN = MLP_RATIO * D
        key = jax.random.key(seed)
        k1, k2, k3, k4 = jax.random.split(key, 4)
        x = jax.random.normal(k1, (N, T, D), dtype=jnp.float32)
        gate_w = jax.random.truncated_normal(k2, -2.0, 2.0, (D, NUM_EXPERTS), dtype=jnp.float32) * 0.02
        w1 = jax.random.normal(k3, (NUM_EXPERTS, D, HIDDEN), dtype=jnp.float32) * 0.02
        w2 = jax.random.normal(k4, (NUM_EXPERTS, HIDDEN, D), dtype=jnp.float32) * 0.02
        return {'x': x, 'gate_w': gate_w, 'w1': w1, 'w2': w2}
    _L1_ffn_all = _L1_ffn_setup()
    _L1_ffn_in = {k: v for k, v in _L1_ffn_all.items() if k in ('gate_w', 'w1', 'w2')}
    del _L1_ffn_all
    return {'x': x, 'ctx_1024': ctx_1024, 'mask_BxS2_bk0': mask_BxS2_bk0, 'mask_BxSxS2_ff1': mask_BxSxS2_ff1, 'mask_BxS2_ff1': mask_BxS2_ff1, 'g_xattn': g_xattn, 'g_ffn': g_ffn, 'L0_xattn_q_w': _L0_xattn_in['q_w'], 'L0_xattn_q_b': _L0_xattn_in['q_b'], 'L0_xattn_kv_w': _L0_xattn_in['kv_w'], 'L0_xattn_kv_b': _L0_xattn_in['kv_b'], 'L0_xattn_proj_w': _L0_xattn_in['proj_w'], 'L0_xattn_proj_b': _L0_xattn_in['proj_b'], 'L0_ffn_Wg': _L0_ffn_in['Wg'], 'L0_ffn_W1': _L0_ffn_in['W1'], 'L0_ffn_W2': _L0_ffn_in['W2'], 'L1_xattn_W_k': _L1_xattn_in['W_k'], 'L1_xattn_b_k': _L1_xattn_in['b_k'], 'L1_xattn_W_o': _L1_xattn_in['W_o'], 'L1_xattn_b_o': _L1_xattn_in['b_o'], 'L1_ffn_gate_w': _L1_ffn_in['gate_w'], 'L1_ffn_w1': _L1_ffn_in['w1'], 'L1_ffn_w2': _L1_ffn_in['w2']}

def reference(x, ctx_1024, mask_BxS2_bk0, mask_BxSxS2_ff1, mask_BxS2_ff1, g_xattn, g_ffn, L0_xattn_q_w, L0_xattn_q_b, L0_xattn_kv_w, L0_xattn_kv_b, L0_xattn_proj_w, L0_xattn_proj_b, L0_ffn_Wg, L0_ffn_W1, L0_ffn_W2, L1_xattn_W_k, L1_xattn_b_k, L1_xattn_W_o, L1_xattn_b_o, L1_ffn_gate_w, L1_ffn_w1, L1_ffn_w2):
    import jax
    import jax.numpy as jnp

    def _L0_xattn_ref(x, context, context_mask, q_w, q_b, kv_w, kv_b, proj_w, proj_b):
        import jax, jax.numpy as jnp
        import numpy as np
        DIM = 128
        HEADS = 16
        HEAD_DIM = DIM // HEADS
        B, N, S = (4, 512, 64)
        b, n, c = x.shape
        s = context.shape[1]
        h, d = (HEADS, HEAD_DIM)
        scale = d ** (-0.5)
        q = (x @ q_w + q_b).reshape(b, n, h, d)
        kv = (context @ kv_w + kv_b).reshape(b, s, 2, h, d)
        k = kv[:, :, 0]
        v = kv[:, :, 1]
        attn = jnp.einsum('bnhd,bshd->bhns', q, k) * scale
        attn = jnp.where(context_mask[:, None, None, :], -jnp.inf, attn)
        attn = jax.nn.softmax(attn, axis=-1)
        out = jnp.einsum('bhns,bshd->bnhd', attn, v).reshape(b, n, c)
        return out @ proj_w + proj_b

    def _L0_ffn_ref(x, Wg, W1, W2):
        import jax, jax.numpy as jnp
        import numpy as np
        B, T, D = (2, 256, 128)
        F = 512
        E = 8
        b, t, d = x.shape
        h = x.reshape(-1, d)
        logits = h @ Wg.T
        scores, idx = jax.lax.top_k(logits, 2)
        scores = jax.nn.softmax(scores.astype(jnp.float32), axis=-1).astype(x.dtype)
        up = jnp.einsum('nd,edf->enf', h, W1)
        act = jax.nn.silu(up)
        out = jnp.einsum('enf,efd->ned', act, W2)
        sel = jnp.take_along_axis(out, idx[:, :, None], axis=1)
        y = jnp.sum(scores[:, :, None] * sel, axis=1)
        return y.reshape(b, t, d)

    def _L1_xattn_ref(query, key, value, cell_mask, seq_mask, W_k, b_k, W_o, b_o):
        import jax, jax.numpy as jnp
        import numpy as np
        k_proj = jnp.einsum('bkd,qd->bkq', key, W_k) + b_k
        scores = jnp.einsum('bqd,bkd->bqk', query, k_proj)
        scores = scores + jnp.log(cell_mask) + jnp.log(seq_mask)[:, None, :]
        p_attn = jax.nn.softmax(scores, axis=-1)
        x = jnp.einsum('bqk,bkd->bqd', p_attn, value)
        return jnp.einsum('bqd,od->bqo', x, W_o) + b_o

    def _L1_ffn_ref(x, gate_w, w1, w2):
        import jax, jax.numpy as jnp
        import numpy as np
        N, T, D = (4, 512, 128)
        NUM_EXPERTS = 8
        EXPERT_CAP = 2.0
        MLP_RATIO = 4
        HIDDEN = MLP_RATIO * D
        x = x.astype(jnp.float32)
        n, t, d = x.shape
        k = int(EXPERT_CAP * t / NUM_EXPERTS)
        scores = jnp.einsum('ntd,de->nte', x, gate_w)
        probs = jax.nn.softmax(scores, axis=-1)
        probs = jnp.transpose(probs, (0, 2, 1))
        g, m = jax.lax.top_k(probs, k)
        xin = jax.vmap(lambda xb, mb: xb[mb])(x, m)
        h = jax.nn.gelu(jnp.einsum('nekd,edf->nekf', xin, w1))
        h = jnp.einsum('nekf,efd->nekd', h, w2)
        weighted = g[..., None] * h
        flat_idx = (m + jnp.arange(n, dtype=m.dtype)[:, None, None] * t).reshape(-1)
        out = jnp.zeros((n * t, d), dtype=jnp.float32).at[flat_idx].add(weighted.reshape(-1, d))
        out = out.reshape(n, t, d)
        return out.astype(jnp.bfloat16)
    x = x + jnp.tanh(g_xattn[0]) * _L0_xattn_ref(_layernorm(x, axis=-1), ctx_1024, mask_BxS2_bk0, L0_xattn_q_w, L0_xattn_q_b, L0_xattn_kv_w, L0_xattn_kv_b, L0_xattn_proj_w, L0_xattn_proj_b)
    x = x + jnp.tanh(g_ffn[0]) * _L0_ffn_ref(_layernorm(x, axis=-1), L0_ffn_Wg, L0_ffn_W1, L0_ffn_W2)
    x = x + jnp.tanh(g_xattn[1]) * _L1_xattn_ref(_layernorm(x, axis=-1), ctx_1024, ctx_1024, mask_BxSxS2_ff1, mask_BxS2_ff1, L1_xattn_W_k, L1_xattn_b_k, L1_xattn_W_o, L1_xattn_b_o)
    x = x + jnp.tanh(g_ffn[1]) * _L1_ffn_ref(_layernorm(x, axis=-1), L1_ffn_gate_w, L1_ffn_w1, L1_ffn_w2)
    return x

_drawn_inputs = setup_inputs


def setup_inputs(seed=0):
    import zlib

    import numpy as np

    out = dict(_drawn_inputs(seed))
    spreads = {'g_ffn': (-1.0, 0.6),
     'L0_xattn_q_b': (0.0, 0.298),
     'L0_xattn_kv_b': (0.0, 0.1),
     'L0_xattn_proj_b': (0.0, 0.1),
     'L1_xattn_b_k': (0.0, 0.8),
     'L1_xattn_b_o': (0.0, 0.1)}
    factors = {'L1_ffn_gate_w': 8.0, 'L1_ffn_w1': 8.0, 'L1_ffn_w2': 8.0}
    for name, (base, spread) in spreads.items():
        noise = np.random.default_rng([zlib.crc32(name.encode()), seed]).standard_normal(out[name].shape)
        drawn = base * np.exp(spread * noise) if base else spread * noise
        out[name] = jnp.asarray(drawn.astype(out[name].dtype))
    for name, factor in factors.items():
        out[name] = (out[name] * factor).astype(out[name].dtype)
    return out
```

```python
from contextlib import ExitStack

import concourse.bass as bass
from concourse import mybir

F32 = mybir.dt.float32
BF16 = mybir.dt.bfloat16
U8 = mybir.dt.uint8
U32 = mybir.dt.uint32
ALU = mybir.AluOpType
ACT = mybir.ActivationFunctionType
AX = mybir.AxisListType

P = 128
B, N, D = 16, 256, 128
S = 64
H, DH = 16, 8
E, F = 8, 512
FC = F // P
TPB = N // P
T = B * TPB
PAIRS = H // 2
GROUPS = 4
HPG = H // GROUPS
CT = 4
CHUNKS = T // CT
CW = CT * P
CAP = 2 * N // E
HB = B // 2
SCALE = float(DH) ** -0.5
EPS = 1e-5
MASKED = -1e30
LEAST = 1e-18


def wait(engine, sem, value):
    if isinstance(value, int) and value <= 0:
        return
    engine.wait_ge(sem, value)


def hold(engine, sem, value, held):
    if isinstance(value, int) and value <= 0:
        return
    engine.wait_ge(sem, value)
    engine.sem_inc(held, 1)


class Chain:

    def __init__(self, engine, sem):
        self.engine, self.sem, self.base, self.k = engine, sem, 0, 0

    def start(self, base, k=0):
        self.base, self.k = base, k

    def done(self, instruction):
        self.k += 1
        return instruction.then_inc(self.sem, 1)

    def link(self, instruction):
        self.done(instruction)
        self.engine.wait_ge(self.sem, self.base + self.k)


def build(nc, a, out, phases=4):
    with ExitStack() as ctx:
        def sb(name, shape, dt=F32):
            return ctx.enter_context(nc.sbuf_tensor(name, shape, dt))

        def sem(name):
            return ctx.enter_context(nc.semaphore(name))

        x = sb("x", [P, T, D])
        mean_var = sb("mean_var", [P, T, 2])
        rstd = sb("rstd", [P, T])
        shift = sb("shift", [P, T])
        ident = sb("ident", [P, P])
        head_rows = sb("head_rows", [P, H])
        head_pick = sb("head_pick", [H, PAIRS, P])
        head_pick16 = sb("head_pick16", [H, PAIRS, P], BF16)
        slot_no = sb("slot_no", [P, CAP])
        lanes = sb("lanes", [P, E])
        ones = sb("ones", [1, P])
        ones16 = sb("ones16", [1, P], BF16)
        eps = sb("eps", [P, 1])
        gates = sb("gates", [P, 4])
        tg = sb("tg", [P, 4])
        q_w = sb("q_w", [P, D])
        kv_w = sb("kv_w", [P, 2 * D])
        proj_w = sb("proj_w", [P, D])
        wk_t = sb("wk_t", [P, D])
        wo_t = sb("wo_t", [P, D])
        route = sb("route", [P, 2, E])
        q_b = sb("q_b", [P, 1])
        q_bs = sb("q_bs", [P, 1])
        k_b = sb("k_b", [P, 1])
        bk1 = sb("bk1", [P, 1])
        v_b = sb("v_b", [P, D])
        proj_b = sb("proj_b", [1, D])
        bo1 = sb("bo1", [P, D])
        w_up1 = sb("w_up1", [P, E, F])
        w_down1 = sb("w_down1", [P, E, FC, D])
        mask4 = sb("mask4", [P, B // 4], U32)
        key_bias = sb("key_bias", [P, B])
        mask_row4 = sb("mask_row4", [1, B * S // 4], U32)
        key_row = sb("key_row", [1, B, S], BF16)
        vals0 = sb("vals0", [P, B, PAIRS, 2 * (DH + 1)])
        z = sb("z", [P, CT, D])
        zt = sb("zt", [P, N])
        q = sb("q", [P, 2, N])
        neg_max = sb("neg_max", [P, TPB, H])
        nmt = sb("nmt", [H, N], BF16)
        inv = sb("inv", [P, TPB, H])
        on = sb("on", [P, TPB, D])
        ot = sb("ot", [P, N])
        stats = sb("stats", [P, CT, 6])
        mv = sb("mv", [P, CT, 2])
        k1 = sb("k1", [P, B, S])
        v1 = sb("v1", [S, B, D])
        s1 = sb("s1", [P, TPB, S])
        nm1 = sb("nm1", [P, TPB])
        e1 = sb("e1", [P, TPB, S])
        sum1 = sb("sum1", [P, TPB])
        p1 = sb("p1", [P, TPB, S])
        pt1 = sb("pt1", [S, N])
        lg = sb("lg", [P, T, E])
        gate = sb("gate", [P, T, E])
        top8 = sb("top8", [P, T, 8])
        idx8 = sb("idx8", [P, T, 8], mybir.dt.uint32)
        pick = sb("pick", [P, 2, T])
        part = sb("part", [P, 2, T])
        scr = sb("scr", [P, T, E])
        left = sb("left", [P, N])
        best8 = sb("best8", [P, 8])
        took = sb("took", [P, N])
        rank = sb("rank", [P, N])
        zero_n = sb("zero_n", [P, N])
        slot_t = sb("slot_t", [P, TPB, B, E])
        y_slots = sb("y_slots", [P, FC, D])
        o16 = sb("o16", [P, TPB, D], BF16)

        area_k = sb("area_k", [P, 4096])
        area_h = sb("area_h", [P, 4096])
        area_z = sb("area_z", [P, 4096])
        area_m = sb("area_m", [P, 3072])
        area_w = sb("area_w", [P, 8192])
        k0 = area_k[:, 0:B * S].rearrange("p (b s) -> p b s", b=B)
        k0s = area_k[:, B * S:B * S + 2 * H * S].rearrange("p (u h s) -> p u h s", u=2, h=H)
        xg = area_k[:, :].rearrange("p (e b s) -> p e b s", e=E, s=CAP)
        ctx_t = area_h[:, 0:B * S].rearrange("p (b s) -> p b s", b=B)
        pt0 = area_h[:, 0:PAIRS * N].rearrange("p (h n) -> p h n", h=PAIRS)
        hid = area_h[:, :].rearrange("p (u f n) -> p u f n", u=2, f=FC)
        cell_zero = area_z[:, 0:T * S].rearrange("p (t s) -> p t s", s=S)
        seq_zero = area_z[:, T * S:T * S + B * S].rearrange("p (b s) -> p b s", s=S)
        zt_all = area_z[:, :]
        yt = area_z[:, :].rearrange("p (b e s) -> p b e s", b=HB, e=E)
        cell = area_m[:, 0:T * S].rearrange("p (t s) -> p t s", s=S)
        seq = area_m[:, T * S:T * S + B * S].rearrange("p (b s) -> p b s", s=S)
        sel = area_m[:, 0:1024].rearrange("p (j e s) -> p j e s", j=TPB, e=E)
        selg = area_m[:, 1024:2048].rearrange("p (j e s) -> p j e s", j=TPB, e=E)
        up0 = area_w[:, 0:4096].rearrange("p (e f) -> p e f", e=E)
        down0 = area_w[:, 4096:8192].rearrange("p (e c d) -> p e c d", e=E, c=FC)
        sgt = area_w[:, :].rearrange("p (b m) -> p b m", b=HB)

        bank = [ctx.enter_context(nc.psum_tensor(f"bank{i}", [P, 512], F32)) for i in range(4)]
        big = [ctx.enter_context(nc.psum_tensor(f"big{i}", [P, 1024], F32)) for i in range(2)]

        names = """ld_const ld_ctx ld_w ld_x ld_e0 ld_mask ld_e1 ld_r stored
            pe_setup act_setup dve_setup pool_setup masks_ready
            a_keys a_z a_tz a_zt a_qm a_q a_s a_max a_tm a_mt a_p2 a_exp a_av a_on a_to a_ot a_pj
            ln_sqrt x_done dve pool held_dve held_act held_pe
            r_z r_tz r_zt r_lg r_d r_exp
            b_gate b_up b_act b_y b_add
            c_z c_tz c_zt c_s c_sub c_exp c_p c_tp c_pt c_o
            d_pr d_rows d_slot d_cols d_slots d_z d_sel d_xg d_xge d_sgt d_sgte
            d_up d_act d_y d_yt d_ty d_ys d_out0 d_o d_out""".split()
        s = {n: sem(n) for n in names}

        def load(eng, which, dst, src):
            eng.dma_start(dst, src).then_inc(s[which], 16)

        LOADS = {"ld_const": 5, "ld_ctx": 1, "ld_w": 12, "ld_x": 4, "ld_mask": 4, "ld_e0": 2, "ld_e1": 2, "ld_r": 2}

        def loaded(eng, which):
            eng.wait_ge(s[which], 16 * LOADS[which])

        block = ctx.enter_context(nc.Block())

        @block.sync
        def _(sp):
            load(sp, "ld_ctx", ctx_t, a["ctx_t"])
            load(sp, "ld_w", kv_w[:, :], a["kv_w"])
            x_in = a["x"].rearrange("(t p) d -> p t d", p=P)
            for i in range(4):
                load(sp, "ld_x", x[:, 8 * i:8 * i + 8, :], x_in[:, 8 * i:8 * i + 8, :])
            load(sp, "ld_w", k_b[:, :], a["kv_b"][0:D].rearrange("(p a) -> p a", a=1))
            load(sp, "ld_w", v_b[:, :], bcast_rows(a["kv_b"][D:2 * D]))
            load(sp, "ld_const", ident[:, :], a["ident"])
            load(sp, "ld_const", head_rows[:, :], a["head_rows"])
            load(sp, "ld_const", head_pick[:, :, :], a["head_pick"])
            load(sp, "ld_const", slot_no[:, :], a["slot_no"])
            load(sp, "ld_const", lanes[:, :], a["lanes"])
            load(sp, "ld_mask", mask4[:, :], a["mask_t"])
            load(sp, "ld_mask", mask_row4[:, :], a["mask_row"])
            load(sp, "ld_w", q_w[:, :], a["q_w"])
            load(sp, "ld_w", q_b[:, :], a["q_b"].rearrange("(p a) -> p a", a=1))
            load(sp, "ld_w", proj_w[:, :], a["proj_w"])
            load(sp, "ld_w", proj_b[:, :], a["proj_b"].rearrange("(a d) -> a d", a=1))
            load(sp, "ld_w", gates[:, 0:2], bcast_rows(a["g_xattn"]))
            load(sp, "ld_w", gates[:, 2:4], bcast_rows(a["g_ffn"]))
            load(sp, "ld_w", wk_t[:, :], a["wk_t"])
            load(sp, "ld_w", wo_t[:, :], a["wo_t"])
            load(sp, "ld_w", bk1[:, :], a["b_k"].rearrange("(p a) -> p a", a=1))
            load(sp, "ld_r", bo1[:, :], bcast_rows(a["b_o"]))
            load(sp, "ld_r", route[:, :, :], a["route"])
            load(sp, "ld_mask", cell, a["cell"].rearrange("(t p) s -> p t s", p=P))
            load(sp, "ld_mask", area_m[:, T * S:T * S + B * S], bcast_rows(a["seq"]))
            load(sp, "ld_e0", area_w[:, 0:4096], a["w_up0"])
            load(sp, "ld_e0", area_w[:, 4096:8192], a["w_down0"])
            load(sp, "ld_e1", w_up1[:, :, :], a["w_up1"])
            load(sp, "ld_e1", w_down1[:, :, :], a["w_down1"])
            if phases < 4:
                sp.wait_ge(s["x_done"], phases)
                sp.dma_start(out.rearrange("(t p) d -> p t d", p=P), x[:, :, :]).then_inc(s["stored"], 16)
                sp.wait_ge(s["stored"], 16)
                return
            x_out = out.rearrange("(t p) d -> p t d", p=P)
            for b in range(B):
                sp.wait_ge(s["d_out"], b + 1)
                sp.dma_start(x_out[:, TPB * b:TPB * b + TPB, :], x[:, TPB * b:TPB * b + TPB, :]).then_inc(s["stored"], 16)
            sp.wait_ge(s["stored"], 16 * B)

        @block.gpsimd
        def _(pool):
            ch = Chain(pool, s["pool"])
            ch.done(pool.memset(ones[:, :], 1.0))
            ch.done(pool.memset(ones16[:, :], 1.0))
            ch.done(pool.memset(eps[:, :], EPS))
            ch.link(pool.memset(vals0[:, :, :, :], 0.0))
            ch.done(pool.memset(vals0[0:S, :, :, DH:DH + 1], 1.0))
            pool.memset(vals0[S:P, :, :, 2 * DH + 1:2 * DH + 2], 1.0).then_inc(s["pool_setup"], 1)

            def keys(c, u):
                pool.tensor_tensor(k0s[:, u, :, :], k0[:, bass.ds(c, 1), :].broadcast_to([P, H, S]),
                                   head_rows[:, :].unsqueeze(2).broadcast_to([P, H, S]), ALU.mult).then_inc(s["a_keys"], 1)

            pool.wait_ge(s["dve_setup"], 6)
            keys(0, 0)
            keys(1, 1)
            with pool.Fori(2, B - 1, 2) as c:
                for u in range(2):
                    pool.wait_ge(s["a_p2"], 2 * (c + u) - 2)
                    keys(c + u, u)
            loaded(pool, "ld_mask")
            ch.done(pool.tensor_scalar(cell_zero, cell, 0.0, MASKED, ALU.is_le, ALU.mult))
            ch.link(pool.tensor_scalar(seq_zero, seq, 0.0, MASKED, ALU.is_le, ALU.mult))
            ch.done(pool.tensor_scalar(cell, cell, LEAST, None, ALU.max))
            pool.tensor_scalar(seq, seq, LEAST, None, ALU.max).then_inc(s["pool_setup"], 1)
            if phases < 2:
                return
            pool.wait_ge(s["masks_ready"], 2)
            ch.done(pool.tensor_tensor(cell, cell, cell_zero, ALU.add))
            ch.link(pool.tensor_tensor(seq, seq, seq_zero, ALU.add))
            cell_b = cell.rearrange("p (b t) s -> p b t s", t=TPB)
            for t in range(TPB):
                pool.wait_ge(s["pool"], ch.k)
                pool.tensor_tensor(cell_b[:, :, t, :], cell_b[:, :, t, :], seq, ALU.add).then_inc(s["pool_setup"], 1)

        @block.scalar
        def _(act):
            act.preload_act_table(ACT.Exp)
            act.wait_ge(s["ld_w"], 16 * LOADS["ld_w"])
            act.activation(tg[:, :], gates[:, :], ACT.Tanh)
            act.activation(q_bs[:, :], q_b[:, :], ACT.Copy, scale=SCALE).then_inc(s["act_setup"], 1)

            def layer_rstd(n):
                act.wait_ge(s["ln_sqrt"], n)
                act.activation(rstd[:, :], mean_var[:, :, 1], ACT.Sqrt, bias=eps[:, 0:1]).then_inc(s["act_setup"], 1)

            act.wait_ge(s["pool_setup"], 1)
            layer_rstd(1)
            act.preload_act_table(ACT.Exp)

            def evac_zt(c):
                wait(act, s["a_tz"], c + 1)
                act.activation(zt[:, :], bank[0][:, 0:N], ACT.Copy).then_inc(s["a_zt"], 1)

            def evac_q(c, u):
                wait(act, s["a_qm"], c + 1)
                act.activation(q[:, u, :], bank[1][:, 0:N], ACT.Identity, bias=q_bs[:, 0:1], scale=SCALE)\
                    .then_inc(s["a_q"], 1)

            def exps(c, h):
                hold(act, s["a_p2"], 2 * c + h + 1, s["held_act"])
                act.activation(area_h[:, h * 1024:(h + 1) * 1024], big[h][:, :], ACT.Exp,
                               bias=key_bias[:, bass.ds(c, 1)]).then_inc(s["a_exp"], 1)

            def a_iter(c, u, now=True, last=True, nxt=True):
                if now:
                    wait(act, s["a_tm"], c + 1)
                    act.activation(nmt[:, :], bank[0][0:H, 0:N], ACT.Copy).then_inc(s["a_mt"], 1)
                    exps(c, 0)
                if last:
                    wait(act, s["a_to"], c)
                    act.activation(ot[:, :], bank[0][:, 0:N], ACT.Copy).then_inc(s["a_ot"], 1)
                if nxt:
                    evac_zt(c + 1)
                    evac_q(c + 1, 1 - u)
                if now:
                    exps(c, 1)

            evac_zt(0)
            evac_q(0, 0)
            act.wait_ge(s["dve_setup"], 2)
            a_iter(0, 0, last=False)
            with act.Fori(1, B - 2, 2) as c:
                a_iter(c, 1)
                a_iter(c + 1, 0)
            a_iter(B - 1, 1, nxt=False)
            a_iter(B, 0, now=False, nxt=False)

            if phases < 2:
                return
            act.wait_ge(s["pool_setup"], 2)
            act.activation(cell, cell, ACT.Ln).then_inc(s["masks_ready"], 1)
            act.activation(seq, seq, ACT.Ln).then_inc(s["masks_ready"], 1)

            def hidden(n, u, func, done):
                for f in range(FC):
                    act.wait_ge(s[done[0]], FC * n + f + 1)
                    src = big[f // 2][:, (f % 2) * CW:(f % 2 + 1) * CW]
                    act.activation(hid[:, u, f, :], src, func).then_inc(s[done[1]], 1)

            def route_evac(r):
                for c in range(CHUNKS):
                    act.wait_ge(s["r_tz"], CHUNKS * r + c + 1)
                    act.activation(zt_all[:, CW * c:CW * c + CW], bank[c % 2][:, :], ACT.Copy).then_inc(s["r_zt"], 1)

            layer_rstd(2)
            act.wait_ge(s["pool_setup"], 2 + TPB)
            act.preload_act_table(ACT.Silu)
            route_evac(0)
            act.wait_ge(s["r_d"], 1)
            act.activation(part[:, 0, :], pick[:, 0, :], ACT.Tanh, scale=0.5).then_inc(s["r_exp"], 1)
            with act.Fori(0, CHUNKS) as c:
                for e in range(E):
                    hidden(E * c + e, e % 2, ACT.Silu, ("b_up", "b_act"))
            if phases < 3:
                return

            layer_rstd(3)
            act.preload_act_table(ACT.Exp)

            def c_zt(c):
                act.wait_ge(s["c_tz"], c + 1)
                act.activation(zt[:, :], bank[0][:, 0:N], ACT.Copy).then_inc(s["c_zt"], 1)

            def c_iter(c, nxt=True):
                if nxt:
                    c_zt(c + 1)
                act.wait_ge(s["c_sub"], c + 1)
                act.activation(e1[:, :, :], s1[:, :, :], ACT.Exp).then_inc(s["c_exp"], 1)
                act.wait_ge(s["c_tp"], c + 1)
                act.activation(pt1[:, :], bank[1][0:S, 0:N], ACT.Copy).then_inc(s["c_pt"], 1)

            c_zt(0)
            with act.Fori(0, B - 1) as c:
                c_iter(c)
            c_iter(B - 1, nxt=False)
            if phases < 4:
                return

            layer_rstd(4)
            act.preload_act_table(ACT.Exp)
            route_evac(1)
            act.wait_ge(s["r_d"], 2)
            act.activation(scr[:, :, :], lg[:, :, :], ACT.Exp).then_inc(s["r_exp"], 1)
            act.preload_act_table(ACT.Gelu_apprx_tanh)
            for half in range(2):
                with act.Fori(0, HB) as i:
                    b = HB * half + i
                    act.wait_ge(s["d_xg"], b + 1)
                    act.activation(xg[:, :, bass.ds(i, 1), :].squeeze(2),
                                   bank[0][:, :].rearrange("p (e s) -> p e s", e=E), ACT.Copy).then_inc(s["d_xge"], 1)
                for e in range(E):
                    hidden(E * half + e, e % 2, ACT.Gelu_apprx_tanh, ("d_up", "d_act"))
                for i in range(HB):
                    b = HB * half + i
                    act.wait_ge(s["d_ty"], b + 1)
                    act.activation(y_slots[:, :, :], bank[0][:, :].rearrange("p (k d) -> p k d", k=FC), ACT.Copy)\
                        .then_inc(s["d_ys"], 1)

        @block.tensor
        def _(pe):
            mm = pe.matmul
            pe.wait_ge(s["ld_ctx"], 16)
            pe.wait_ge(s["ld_w"], 16 * LOADS["ld_w"])
            for h in range(2):
                mm(bank[h][:, :], kv_w[:, 0:D], ctx_t[:, 8 * h:8 * h + 8, :], start=True, stop=True)\
                    .then_inc(s["pe_setup"], 1)
            for h in range(2):
                mm(bank[2 + h][:, :], wk_t[:, :], ctx_t[:, 8 * h:8 * h + 8, :], start=True, stop=True)\
                    .then_inc(s["pe_setup"], 1)
            for b in range(B):
                for k in range(2):
                    ins = mm(big[b // 8][S * k:S * k + S, (b % 8) * D:(b % 8 + 1) * D], ctx_t[:, b, :], kv_w[:, D:2 * D],
                             start=True, stop=True)
                if b % 8 == 7:
                    ins.then_inc(s["pe_setup"], 1)
            for b in range(B):
                if b % 8 == 0:
                    pe.wait_ge(s["dve_setup"], 3 + b // 8)
                ins = mm(big[b // 8][0:S, (b % 8) * D:(b % 8 + 1) * D], ctx_t[:, b, :], wo_t[:, :], start=True, stop=True)
                if b % 8 == 7:
                    ins.then_inc(s["pe_setup"], 1)

            def transposes(dst, src, n, done, rows=P, cols=P):
                for t in range(n):
                    ins = pe.transpose(dst[0:cols, t * P:(t + 1) * P], src[:, t, :], ident[:, :])
                ins.then_inc(done, 1)

            pe.wait_ge(s["ld_const"], 16 * LOADS["ld_const"])

            def tz(c):
                wait(pe, s["a_z"], c + 1)
                transposes(bank[0], z[:, 0:TPB, :], TPB, s["a_tz"])

            def q_product(c):
                wait(pe, s["a_zt"], c + 1)
                mm(bank[1][:, 0:N], q_w[:, :], zt[:, :], start=True, stop=True).then_inc(s["a_qm"], 1)

            def pass1(c, u):
                wait(pe, s["a_q"], c + 1)
                wait(pe, s["a_keys"], c + 1)
                for t in range(TPB):
                    wait(pe, s["a_exp"], 2 * c - 1 + t)
                    for g in range(GROUPS):
                        dst = big[t][:, g * HPG * S:(g + 1) * HPG * S]
                        mm(dst, q[:, u, t * P:(t + 1) * P], k0s[:, u, HPG * g:HPG * g + HPG, :], start=True, stop=False)
                        ins = mm(dst, ones16[:, :], key_row[:, bass.ds(c, 1), :].broadcast_to([1, HPG, S]),
                                 start=False, stop=True)
                    ins.then_inc(s["a_s"], 1)

            def values(c):
                wait(pe, s["a_exp"], 2 * c + 2)
                for t in range(TPB):
                    for h in range(PAIRS):
                        w = 2 * (DH + 1)
                        o = (t * PAIRS + h) * w
                        ins = mm(bank[2][:, o:o + w], pt0[:, h, t * P:(t + 1) * P], vals0[:, bass.ds(c, 1), h, :],
                                 start=True, stop=True)
                ins.then_inc(s["a_av"], 1)

            def pass2(c, u, h):
                wait(pe, s["a_max"], 2 * c + h + 1)
                wait(pe, s["a_keys"], c + 1)
                for k in range(4):
                    pair = 4 * h + k
                    dst = big[h][:, k * N:(k + 1) * N]
                    mm(dst, k0s[:, u, 2 * pair:2 * pair + 2, :], q[:, u, :], start=True, stop=False)
                    ins = mm(dst, head_pick16[:, pair, :], nmt[:, :], start=False, stop=True)
                ins.then_inc(s["a_p2"], 1)

            def a_iter(c, u, now=True, last=True, nxt=True):
                if now:
                    pass1(c, u)
                if last:
                    values(c - 1)
                if now:
                    wait(pe, s["a_max"], 2 * c + 2)
                    wait(pe, s["a_zt"], c + 1)
                    transposes(bank[0], neg_max, TPB, s["a_tm"], cols=H)
                    wait(pe, s["a_mt"], c + 1)
                    pass2(c, u, 0)
                if last:
                    wait(pe, s["a_on"], c)
                    transposes(bank[0], on, TPB, s["a_to"])
                    wait(pe, s["a_ot"], c)
                if nxt:
                    tz(c + 1)
                    q_product(c + 1)
                if now:
                    pass2(c, u, 1)
                if last:
                    for t in range(TPB):
                        dst = bank[3][:, t * P:(t + 1) * P]
                        mm(dst, ot[:, t * P:(t + 1) * P], proj_w[:, :], start=True, stop=False)
                        ins = mm(dst, ones[:, :], proj_b[:, :], start=False, stop=True)
                    ins.then_inc(s["a_pj"], 1)

            pe.wait_ge(s["dve_setup"], 8)
            tz(0)
            q_product(0)
            a_iter(0, 0, last=False)
            with pe.Fori(1, B - 2, 2) as c:
                a_iter(c, 1)
                a_iter(c + 1, 0)
            a_iter(B - 1, 1, nxt=False)
            a_iter(B, 0, now=False, nxt=False)
            if phases < 2:
                return

            def route_products(r, col):
                for c in range(CHUNKS):
                    pe.wait_ge(s["r_z"], CHUNKS * r + c + 1)
                    if c >= 2:
                        pe.wait_ge(s["r_zt"], CHUNKS * r + c - 1)
                    transposes(bank[c % 2], z, CT, s["r_tz"])
                    pe.wait_ge(s["r_zt"], CHUNKS * r + c + 1)
                    for t in range(CT):
                        k = col(CT * c + t)
                        ins = mm(bank[2][:, k:k + E], zt_all[:, CW * c + P * t:CW * c + P * t + P], route[:, r, :],
                                 start=True, stop=True)
                ins.then_inc(s["r_lg"], 1)

            loaded(pe, "ld_e0")
            loaded(pe, "ld_r")
            route_products(0, lambda t: E * t)

            def up(n, w, e, tokens, sems, free):
                for f in range(FC):
                    wait(pe, s[sems[1]], FC * (n - 1) + f + 1 if free else 0)
                    mm(big[f // 2][:, (f % 2) * CW:(f % 2 + 1) * CW], w[:, e, f * P:(f + 1) * P], tokens,
                       start=True, stop=True).then_inc(s[sems[0]], 1)

            def b_up(n, c, e, free=True):
                up(n, up0, e, zt_all[:, bass.ds(CW * c, CW)], ("b_up", "b_act"), free)

            def b_down(n, e, free=True):
                pe.wait_ge(s["b_act"], FC * (n + 1))
                y = bank[2 + e % 2]
                if free:
                    pe.wait_ge(s["b_add"], n - 1)
                for t in range(CT):
                    for f in range(FC):
                        ins = mm(y[:, t * D:(t + 1) * D], hid[:, e % 2, f, t * P:(t + 1) * P], down0[:, e, f, :],
                                 start=(f == 0), stop=(f == FC - 1))
                ins.then_inc(s["b_y"], 1)

            def b_iter(c, first=False, last=False):
                for e in range(E):
                    if not (last and e == E - 1):
                        b_up(E * c + e + 1, c + (e == E - 1), (e + 1) % E)
                    b_down(E * c + e, e, not (first and e < 2))

            pe.wait_ge(s["b_gate"], 1)
            b_up(0, 0, 0, free=False)
            b_iter(0, first=True)
            with pe.Fori(1, CHUNKS - 1) as c:
                b_iter(c)
            b_iter(CHUNKS - 1, last=True)
            if phases < 3:
                return

            def c_tz(c):
                pe.wait_ge(s["c_z"], c + 1)
                transposes(bank[0], z[:, 0:TPB, :], TPB, s["c_tz"])

            def c_scores(c, free=True):
                pe.wait_ge(s["c_zt"], c + 1)
                if free:
                    pe.wait_ge(s["c_sub"], c)
                for t in range(TPB):
                    ins = mm(bank[2][:, t * S:(t + 1) * S], zt[:, t * P:(t + 1) * P], k1[:, bass.ds(c, 1), :],
                             start=True, stop=True)
                ins.then_inc(s["c_s"], 1)

            def c_iter(c, nxt=True):
                if nxt:
                    c_tz(c + 1)
                    c_scores(c + 1)
                hold(pe, s["c_p"], c + 1, s["held_pe"])
                transposes(bank[1], p1, TPB, s["c_tp"], cols=S)
                pe.wait_ge(s["c_pt"], c + 1)
                for t in range(TPB):
                    ins = mm(bank[3][:, t * D:(t + 1) * D], pt1[:, t * P:(t + 1) * P], v1[:, bass.ds(c, 1), :],
                             start=True, stop=True)
                ins.then_inc(s["c_o"], 1)

            pe.wait_ge(s["b_add"], CHUNKS * E)
            c_tz(0)
            c_scores(0, free=False)
            with pe.Fori(0, B - 1) as c:
                c_iter(c)
            c_iter(B - 1, nxt=False)
            if phases < 4:
                return

            loaded(pe, "ld_e1")
            pe.wait_ge(s["x_done"], 3)
            route_products(1, lambda t: (t % TPB) * B * E + t // TPB * E)
            pe.wait_ge(s["d_pr"], 1)
            for j in range(TPB):
                ins = pe.transpose(bank[0][:, j * P:(j + 1) * P], gate[:, :, :].rearrange("p (j b) e -> p j (b e)", j=TPB)[:, j, :], ident[:, :])
            ins.then_inc(s["d_rows"], 1)
            pe.wait_ge(s["d_slot"], 1)
            for j in range(TPB):
                ins = pe.transpose(bank[1][:, j * P:(j + 1) * P], rank[:, j * P:(j + 1) * P], ident[:, :])
            ins.then_inc(s["d_cols"], 1)
            pe.wait_ge(s["d_slots"], 1)
            for half in range(2):
                def take(i, free):
                    b = HB * half + i
                    pe.wait_ge(s["d_sel"], b + 1)
                    if free:
                        pe.wait_ge(s["d_xge"], b)
                        pe.wait_ge(s["d_sgte"], b)
                    for j in range(TPB):
                        ins = mm(bank[0][:, :], z[:, j, :], sel[:, j, :, :], start=(j == 0), stop=(j == TPB - 1))
                    ins.then_inc(s["d_xg"], 1)
                    for k in range(FC):
                        for j in range(TPB):
                            o = (k * TPB + j) * P
                            ins = pe.transpose(big[0][:, o:o + P], selg[:, j, 2 * k:2 * k + 2, :], ident[:, :])
                    ins.then_inc(s["d_sgt"], 1)

                take(0, half > 0)
                with pe.Fori(1, HB) as i:
                    take(i, True)
                pe.wait_ge(s["d_xge"], HB * (half + 1))
                pe.wait_ge(s["d_sgte"], HB * (half + 1))

                def d_up(e):
                    n = E * half + e
                    up(n, w_up1, e, xg[:, e, :, :], ("d_up", "d_act"), n > 0)

                def d_down(e):
                    n = E * half + e
                    pe.wait_ge(s["d_act"], FC * (n + 1))
                    if n >= 2:
                        pe.wait_ge(s["d_yt"], n - 1)
                    for f in range(FC):
                        ins = mm(bank[2 + e % 2][:, :], w_down1[:, e, f, :], hid[:, e % 2, f, :],
                                 start=(f == 0), stop=(f == FC - 1))
                    ins.then_inc(s["d_y"], 1)

                d_up(0)
                for e in range(E):
                    if e + 1 < E:
                        d_up(e + 1)
                    d_down(e)
                pe.wait_ge(s["d_yt"], E * (half + 1))
                for i in range(HB):
                    b = HB * half + i
                    if b > 0:
                        pe.wait_ge(s["d_ys"], b)
                    for k in range(FC):
                        ins = pe.transpose(bank[0][:, k * P:(k + 1) * P], yt[:, i, 2 * k:2 * k + 2, :], ident[:, :])
                    ins.then_inc(s["d_ty"], 1)
                    pe.wait_ge(s["d_ys"], b + 1)
                    if b > 0:
                        pe.wait_ge(s["d_o"], b)
                    for j in range(TPB):
                        for k in range(FC):
                            o = (k * TPB + j) * P
                            ins = mm(bank[1][:, j * D:(j + 1) * D], sgt[:, i, o:o + P], y_slots[:, k, :],
                                     start=(k == 0), stop=(k == FC - 1))
                    ins.then_inc(s["d_out0"], 1)

        @block.vector
        def _(dve):
            ch = Chain(dve, s["dve"])
            dve.wait_ge(s["ld_const"], 16 * LOADS["ld_const"])
            dve.wait_ge(s["ld_mask"], 16 * LOADS["ld_mask"])
            ch.done(dve.tensor_copy(head_pick16[:, :, :], head_pick[:, :, :]))
            dve.tensor_scalar(key_row[:, :, :], mask_row4[:, :].bitcast(U8).rearrange("p (b s) -> p b s", s=S), MASKED, None,
                              ALU.mult).then_inc(s["dve_setup"], 1)
            dve.tensor_scalar(key_bias[:, :], mask4[:, :].bitcast(U8), MASKED, None, ALU.mult).then_inc(s["dve_setup"], 1)
            dve.wait_ge(s["pool_setup"], 1)
            dve.wait_ge(s["ld_w"], 16 * LOADS["ld_w"])
            for h in range(2):
                dve.wait_ge(s["pe_setup"], 5 + h)
                for k in range(2):
                    r = slice(S * k, S * k + S)
                    for j in range(2):
                        v = big[h][r, 512 * j:512 * j + 512].rearrange("p (b h k d) -> p b h k d", b=4, h=PAIRS, k=2)
                        bias = v_b[r, :].rearrange("p (h k d) -> p h k d", h=PAIRS, k=2)[:, :, k, :]
                        b0 = 8 * h + 4 * j
                        ins = dve.tensor_tensor(vals0[r, b0:b0 + 4, :, k * (DH + 1):k * (DH + 1) + DH], v[:, :, :, k, :],
                                                bias.unsqueeze(1).broadcast_to([S, 4, PAIRS, DH]), ALU.add)
                        if (k, j) == (1, 1):
                            ins.then_inc(s["dve_setup"], 1)
            for h in range(2):
                dve.tensor_scalar(k0[:, 8 * h:8 * h + 8, :], bank[h][:, :].rearrange("p (b s) -> p b s", s=S),
                                  k_b[:, 0:1], None, ALU.add)\
                    .then_inc(s["dve_setup"], 1)
            dve.wait_ge(s["ld_r"], 16 * LOADS["ld_r"])
            for h in range(2):
                ins = dve.tensor_scalar(k1[:, 8 * h:8 * h + 8, :], bank[2 + h][:, :].rearrange("p (b s) -> p b s", s=S),
                                        bk1[:, 0:1], None, ALU.add)
            for h in range(2):
                dve.wait_ge(s["pe_setup"], 7 + h)
                dve.tensor_tensor(v1[:, 8 * h:8 * h + 8, :], big[h][0:S, :].rearrange("p (b d) -> p b d", d=D),
                                  bo1[0:S, :].unsqueeze(1).broadcast_to([S, 8, D]), ALU.add)\
                    .then_inc(s["dve_setup"], 1)

            def tile_stats(t0, n):
                hold(dve, ch.sem, ch.base + ch.k, s["held_dve"])
                for t in range(n):
                    ch.done(dve.bn_stats(stats[:, t, :], x[:, bass.ds(t0 + t, 1), :].squeeze(1)))
                hold(dve, ch.sem, ch.base + ch.k, s["held_dve"])
                for t in range(n):
                    ch.done(dve.bn_aggr(mv[:, t, :], stats[:, t, :]))
                dve.wait_ge(ch.sem, ch.base + ch.k)
                ch.link(dve.tensor_copy(mean_var[:, bass.ds(t0, n), :], mv[:, 0:n, :]))

            def layer_norm(n):
                dve.drain().then_inc(s["ln_sqrt"], 1)
                dve.wait_ge(s["act_setup"], n + 1)
                ch.link(dve.reciprocal(rstd[:, :], rstd[:, :]))
                ch.link(dve.scalar_tensor_tensor(shift[:, :], mean_var[:, :, 0], -1.0, rstd[:, :], ALU.mult, ALU.mult))

            def normalize(t0, n, done):
                for t in range(n):
                    ins = dve.tensor_scalar(z[:, t, :], x[:, bass.ds(t0 + t, 1), :].squeeze(1),
                                            rstd[:, bass.ds(t0 + t, 1)], shift[:, bass.ds(t0 + t, 1)],
                                            ALU.mult, ALU.add)
                ins.then_inc(s[done], 1)

            dve.wait_ge(s["ld_x"], 16 * LOADS["ld_x"])
            for c in range(CHUNKS):
                tile_stats(CT * c, CT)
            dve.wait_ge(s["act_setup"], 1)
            layer_norm(1)

            base = ch.k
            per = TPB + TPB + 1 + 2

            def a_iter(c, now=True, last=True, nxt=True):
                if nxt:
                    wait(dve, s["a_tz"], c + 1)
                    normalize(TPB * (c + 1), TPB, "a_z")
                if now:
                    for t in range(TPB):
                        wait(dve, s["a_s"], TPB * c + t + 1)
                        wait(dve, s["a_tm"], c)
                        dve.tensor_reduce(neg_max[:, t, :], big[t][:, :].rearrange("p (h s) -> p h s", s=S), AX.X,
                                          ALU.max, negate=True).then_inc(s["a_max"], 1)
                if last:
                    wait(dve, s["a_av"], c)
                    o = bank[2][:, 0:TPB * H * (DH + 1)].rearrange("p (t h d) -> p t h d", t=TPB, h=H)
                    ch.link(dve.reciprocal(inv[:, :, :], o[:, :, :, DH]))
                    dve.tensor_tensor(on[:, :, :].rearrange("p t (h d) -> p t h d", h=H), o[:, :, :, 0:DH],
                                      inv[:, :, :].unsqueeze(3).broadcast_to([P, TPB, H, DH]), ALU.mult)\
                        .then_inc(s["a_on"], 1)
                    wait(dve, s["a_pj"], c)
                    xs = x[:, bass.ds(TPB * (c - 1), TPB), :]
                    ch.done(dve.scalar_tensor_tensor(xs, bank[3][:, 0:N].rearrange("p (t d) -> p t d", t=TPB),
                                                     tg[:, 0:1], xs, ALU.mult, ALU.add))
                    tile_stats(TPB * (c - 1), TPB)

            normalize(0, TPB, "a_z")
            a_iter(0, last=False)
            per = 2 + 2 * TPB + 1
            base = ch.k
            with dve.Fori(1, B - 2, 2) as c:
                ch.start(base + per * (c - 1))
                a_iter(c)
                a_iter(c + 1)
                assert ch.k == 2 * per
            ch.start(0, base + per * (B - 2))
            a_iter(B - 1, nxt=False)
            a_iter(B, now=False, nxt=False)
            ch.start(ch.base, ch.k)
            dve.drain().then_inc(s["x_done"], 1)
            if phases < 2:
                return

            def link_all():
                dve.wait_ge(ch.sem, ch.base + ch.k)

            def route_rows(r):
                for c in range(CHUNKS):
                    if r or c:
                        dve.wait_ge(s["r_tz"], CHUNKS * r + c)
                    normalize(CT * c, CT, "r_z")

            layer_norm(2)
            route_rows(0)
            dve.wait_ge(s["r_lg"], 1)
            ch.link(dve.tensor_copy(lg[:, :, :], bank[2][:, 0:T * E].rearrange("p (t e) -> p t e", e=E)))
            for t in range(T):
                ch.done(dve.max(top8[:, t, :], lg[:, t, :]))
            link_all()
            for t in range(T):
                ch.done(dve.max_index(idx8[:, t, :], top8[:, t, :], lg[:, t, :]))
            dve.tensor_tensor(pick[:, 0, :], top8[:, :, 0], top8[:, :, 1], ALU.subtract).then_inc(s["r_d"], 1)
            dve.wait_ge(s["r_exp"], 1)
            for k in range(2):
                ch.done(dve.tensor_scalar(part[:, 1 - k, :], part[:, 0, :], -0.5 if k == 0 else 0.5, 0.5, ALU.mult, ALU.add))
                link_all()
            ch.link(dve.tensor_copy(pick[:, :, :], idx8[:, :, 0:2].rearrange("p t k -> p k t")))
            lanes_all = lanes[:, :].unsqueeze(1).broadcast_to([P, T, E])
            for k, dst in enumerate((gate, scr)):
                ch.link(dve.tensor_tensor(dst[:, :, :], lanes_all, pick[:, k, :].unsqueeze(2).broadcast_to([P, T, E]),
                                          ALU.is_equal))
                ch.link(dve.tensor_tensor(dst[:, :, :], dst[:, :, :], part[:, k, :].unsqueeze(2).broadcast_to([P, T, E]),
                                          ALU.mult))
            ch.link(dve.tensor_tensor(gate[:, :, :], gate[:, :, :], scr[:, :, :], ALU.add))
            dve.tensor_scalar(gate[:, :, :], gate[:, :, :], tg[:, 2:3], None, ALU.mult).then_inc(s["b_gate"], 1)
            dve.wait_ge(s["b_gate"], 1)
            base = ch.k
            per = E * CT + 2 * CT + 1
            with dve.Fori(0, CHUNKS) as c:
                ch.start(base + per * c)
                for e in range(E):
                    dve.wait_ge(s["b_y"], E * c + e + 1)
                    for t in range(CT):
                        xs = x[:, bass.ds(CT * c + t, 1), :].squeeze(1)
                        ins = ch.done(dve.scalar_tensor_tensor(xs, bank[2 + e % 2][:, t * D:(t + 1) * D],
                                                               gate[:, bass.ds(CT * c + t, 1), e], xs, ALU.mult, ALU.add))
                    link_all()
                    dve.sem_inc(s["b_add"], 1)
                tile_stats(CT * c, CT)
                assert ch.k == per
            ch.start(0, base + per * CHUNKS)
            dve.drain().then_inc(s["x_done"], 1)
            if phases < 3:
                return

            layer_norm(3)
            dve.wait_ge(s["pool_setup"], 2 + TPB)

            def c_iter(c, last=True, now=True, nxt=True):
                if now:
                    dve.wait_ge(s["c_s"], c + 1)
                    ch.link(dve.tensor_tensor(s1[:, :, :], bank[2][:, 0:TPB * S].rearrange("p (t s) -> p t s", t=TPB),
                                              cell[:, bass.ds(TPB * c, TPB), :], ALU.add))
                    ch.link(dve.tensor_reduce(nm1[:, :], s1[:, :, :], AX.X, ALU.max, negate=True))
                    dve.tensor_tensor(s1[:, :, :], s1[:, :, :], nm1[:, :].unsqueeze(2).broadcast_to([P, TPB, S]), ALU.add)\
                        .then_inc(s["c_sub"], 1)
                if nxt:
                    dve.wait_ge(s["c_tz"], c + 1)
                    normalize(TPB * (c + 1), TPB, "c_z")
                if last:
                    dve.wait_ge(s["c_o"], c)
                    xs = x[:, bass.ds(TPB * (c - 1), TPB), :]
                    ch.done(dve.scalar_tensor_tensor(xs, bank[3][:, 0:N].rearrange("p (t d) -> p t d", t=TPB),
                                                     tg[:, 1:2], xs, ALU.mult, ALU.add))
                    tile_stats(TPB * (c - 1), TPB)
                if now:
                    dve.wait_ge(s["c_exp"], c + 1)
                    ch.link(dve.reduce_sum(sum1[:, :], e1[:, :, :], AX.X))
                    ch.link(dve.reciprocal(sum1[:, :], sum1[:, :]))
                    dve.tensor_tensor(p1[:, :, :], e1[:, :, :], sum1[:, :].unsqueeze(2).broadcast_to([P, TPB, S]), ALU.mult)\
                        .then_inc(s["c_p"], 1)

            normalize(0, TPB, "c_z")
            c_iter(0, last=False)
            base = ch.k
            per = 4 + 2 + 2 * TPB
            with dve.Fori(1, B - 1) as c:
                ch.start(base + per * (c - 1))
                c_iter(c)
                assert ch.k == per
            ch.start(0, base + per * (B - 2))
            c_iter(B - 1, nxt=False)
            c_iter(B, now=False, nxt=False)
            dve.drain().then_inc(s["x_done"], 1)
            if phases < 4:
                return

            layer_norm(4)
            route_rows(1)
            dve.wait_ge(s["r_lg"], 2)
            ch.link(dve.tensor_copy(lg[:, :, :], bank[2][:, 0:T * E].rearrange("p (t e) -> p t e", e=E)))
            ch.link(dve.tensor_reduce(pick[:, 0, :], lg[:, :, :], AX.X, ALU.max, negate=True))
            dve.tensor_tensor(lg[:, :, :], lg[:, :, :], pick[:, 0, :].unsqueeze(2).broadcast_to([P, T, E]), ALU.add)\
                .then_inc(s["r_d"], 1)
            ch.done(dve.memset(zero_n[:, :], 0.0))
            dve.wait_ge(s["r_exp"], 2)
            ch.link(dve.reduce_sum(pick[:, 0, :], scr[:, :, :], AX.X))
            ch.link(dve.reciprocal(pick[:, 0, :], pick[:, 0, :]))
            dve.tensor_tensor(gate[:, :, :], scr[:, :, :], pick[:, 0, :].unsqueeze(2).broadcast_to([P, T, E]), ALU.mult)\
                .then_inc(s["d_pr"], 1)
            dve.wait_ge(s["d_rows"], 1)
            ch.link(dve.tensor_copy(left[:, :], bank[0][:, 0:N]))
            for _ in range(CAP // 8):
                ch.link(dve.max(best8[:, :], left[:, :]))
                ch.link(dve.match_replace(left[:, :], best8[:, :], left[:, :], -1.0))
            ch.link(dve.tensor_scalar(took[:, :], left[:, :], 0.0, None, ALU.is_lt))
            ch.link(dve.tensor_tensor_scan(rank[:, :], took[:, :], zero_n[:, :], 0.0, ALU.add, ALU.add))
            ch.link(dve.tensor_tensor(rank[:, :], rank[:, :], took[:, :], ALU.mult))
            dve.tensor_scalar(rank[:, :], rank[:, :], -1.0, None, ALU.add).then_inc(s["d_slot"], 1)
            dve.wait_ge(s["d_cols"], 1)
            ch.link(dve.tensor_copy(slot_t[:, :, :, :], bank[1][:, 0:N].rearrange("p (j b e) -> p j b e", j=TPB, b=B)))
            dve.sem_inc(s["d_slots"], 1)
            slot_all = slot_no[:, :].unsqueeze(1).broadcast_to([P, E, CAP])
            gate_t = gate[:, :, :].rearrange("p (j b) e -> p j b e", j=TPB)
            for half in range(2):
                base = ch.k
                with dve.Fori(0, HB) as i:
                    ch.start(base + TPB * i)
                    b = HB * half + i
                    if half:
                        dve.wait_ge(s["d_sgt"], b)
                    normalize(TPB * b, TPB, "d_z")
                    for j in range(TPB):
                        ch.done(dve.tensor_tensor(sel[:, j, :, :], slot_all,
                                                  slot_t[:, j, bass.ds(b, 1), :].squeeze(1).unsqueeze(2).broadcast_to([P, E, CAP]),
                                                  ALU.is_equal))
                    link_all()
                    for j in range(TPB):
                        ins = dve.tensor_tensor(selg[:, j, :, :], sel[:, j, :, :],
                                                gate_t[:, j, bass.ds(b, 1), :].squeeze(1).unsqueeze(2).broadcast_to([P, E, CAP]),
                                                ALU.mult)
                    ins.then_inc(s["d_sel"], 1)
                    dve.wait_ge(s["d_sgt"], b + 1)
                    dve.tensor_copy(sgt[:, bass.ds(i, 1), :].squeeze(1), big[0][:, :]).then_inc(s["d_sgte"], 1)
                ch.start(0, base + TPB * HB)
                for e in range(E):
                    dve.wait_ge(s["d_y"], E * half + e + 1)
                    dve.tensor_copy(yt[:, :, e, :], bank[2 + e % 2][:, :].rearrange("p (b s) -> p b s", b=HB))\
                        .then_inc(s["d_yt"], 1)
                for i in range(HB):
                    b = HB * half + i
                    dve.wait_ge(s["d_out0"], b + 1)
                    if b > 0:
                        dve.wait_ge(s["d_out"], b)
                    ch.link(dve.tensor_copy(o16[:, :, :], bank[1][:, 0:N].rearrange("p (t d) -> p t d", t=TPB)))
                    dve.sem_inc(s["d_o"], 1)
                    xs = x[:, TPB * b:TPB * b + TPB, :]
                    dve.scalar_tensor_tensor(xs, o16[:, :, :], tg[:, 3:4], xs, ALU.mult, ALU.add).then_inc(s["d_out"], 1)


def bcast_rows(src):
    n = src.shape[0]
    return src.rearrange("(a n) -> a n", a=1).broadcast_to([P, n])


_OUT = (B * N, D)


def kernel(**inputs):
    import numpy as np
    import concourse.bacc as bacc
    from concourse.bass_utils import run_bass_kernel_spmd

    g = {k: np.asarray(v) for k, v in inputs.items()}
    flat = np.ascontiguousarray
    mask = g["mask_BxS2_bk0"].view(np.uint8)
    pair = np.arange(H)[:, None, None] == 2 * np.arange(PAIRS)[None, :, None] + (np.arange(P) // S)[None, None, :]
    arrays = {
        "x": flat(g["x"].reshape(B * N, D)),
        "ctx_t": flat(g["ctx_1024"].transpose(2, 0, 1)),
        "mask_t": flat(np.concatenate([mask.T, mask.T])).view(np.uint32),
        "mask_row": flat(mask.reshape(1, B * S)).view(np.uint32),
        "cell": flat(g["mask_BxSxS2_ff1"].reshape(B * N, S)),
        "seq": flat(g["mask_BxS2_ff1"].reshape(B * S)),
        "g_xattn": flat(g["g_xattn"]),
        "g_ffn": flat(g["g_ffn"]),
        "q_w": flat(g["L0_xattn_q_w"]),
        "q_b": flat(g["L0_xattn_q_b"]),
        "kv_w": flat(g["L0_xattn_kv_w"]),
        "kv_b": flat(g["L0_xattn_kv_b"]),
        "proj_w": flat(g["L0_xattn_proj_w"]),
        "proj_b": flat(g["L0_xattn_proj_b"]),
        "wk_t": flat(g["L1_xattn_W_k"].T),
        "b_k": flat(g["L1_xattn_b_k"]),
        "wo_t": flat(g["L1_xattn_W_o"].T),
        "b_o": flat(g["L1_xattn_b_o"]),
        "route": flat(np.stack([g["L0_ffn_Wg"].T, g["L1_ffn_gate_w"]], axis=1)),
        "w_up0": flat(g["L0_ffn_W1"].transpose(1, 0, 2).reshape(D, E * F)),
        "w_down0": flat(g["L0_ffn_W2"].reshape(E, FC, P, D).transpose(2, 0, 1, 3).reshape(P, E * FC * D)),
        "w_up1": flat(g["L1_ffn_w1"].transpose(1, 0, 2)),
        "w_down1": flat(g["L1_ffn_w2"].reshape(E, FC, P, D).transpose(2, 0, 1, 3)),
        "ident": np.eye(P, dtype=np.float32),
        "head_rows": ((np.arange(P) // DH)[:, None] == np.arange(H)).astype(np.float32),
        "head_pick": pair.astype(np.float32),
        "slot_no": np.tile(np.arange(CAP, dtype=np.float32), (P, 1)),
        "lanes": np.tile(np.arange(E, dtype=np.float32), (P, 1)),
    }
    nc = bacc.Bacc("TRN2", target_bir_lowering=False, num_devices=1)
    aps = {}
    for name, v in arrays.items():
        aps[name] = nc.dram_tensor(f"in_{name}", v.shape, mybir.dt.from_np(v.dtype), kind="ExternalInput").ap()
    out = nc.dram_tensor("out", _OUT, F32, kind="ExternalOutput").ap()
    build(nc, aps, out, PHASES)
    r = run_bass_kernel_spmd(nc, [{f"in_{k}": v for k, v in arrays.items()}], core_ids=[0])
    return r.results[0]["out"].reshape(B, N, D)


PHASES = 4
```

```python
from contextlib import ExitStack

import concourse.bass as bass
from concourse import mybir

F32 = mybir.dt.float32
BF16 = mybir.dt.bfloat16
F16 = mybir.dt.float16
U8 = mybir.dt.uint8
U32 = mybir.dt.uint32
I32 = mybir.dt.int32
ALU = mybir.AluOpType
ACT = mybir.ActivationFunctionType
AX = mybir.AxisListType

P = 128
B, N, D = 16, 256, 128
S = 64
H, DH = 16, 8
E, F = 8, 512
FC = F // P
TPB = N // P
T = B * TPB
PAIRS = H // 2
GROUPS = 4
HPG = H // GROUPS
X_LOADS = 4
CT = 4
CHUNKS = T // CT
CW = CT * P
GR = 2
TG = T // GR
CG = TG // CT
BG = B // GR
FIRST = BG + 2
SW = 256
NB = 2 * TG * P // SW + E - 1
ROWS = NB * SW
DEEP = 4
RING = 8
CAP = 2 * N // E
HB = B // 2
SCALE = float(DH) ** -0.5
EPS = 1e-5
MASKED = -1e30
LEAST = 1e-18
SPLIT = 4096.0


def wait(engine, sem, value):
    if isinstance(value, int) and value <= 0:
        return
    engine.wait_ge(sem, value)


def hold(engine, sem, value, held):
    if isinstance(value, int) and value <= 0:
        return
    engine.wait_ge(sem, value)
    engine.sem_inc(held, 1)


class Chain:

    def __init__(self, engine, sem):
        self.engine, self.sem, self.base, self.k = engine, sem, 0, 0

    def start(self, base, k=0):
        self.base, self.k = base, k

    def done(self, instruction):
        self.k += 1
        return instruction.then_inc(self.sem, 1)

    def link(self, instruction):
        self.done(instruction)
        self.engine.wait_ge(self.sem, self.base + self.k)


def build(nc, a, out, phases=4):
    with ExitStack() as ctx:
        def sb(name, shape, dt=F32):
            return ctx.enter_context(nc.sbuf_tensor(name, shape, dt))

        def sem(name):
            return ctx.enter_context(nc.semaphore(name))

        x = sb("x", [P, T, D])
        mean_var = sb("mean_var", [P, T, 2])
        rstd = sb("rstd", [P, 2, T])
        shift = sb("shift", [P, 2, T])
        ident = sb("ident", [P, P])
        head_rows = sb("head_rows", [P, H])
        head_pick = sb("head_pick", [H, PAIRS, P])
        head_pick16 = sb("head_pick16", [H, PAIRS, P], BF16)
        token_no = sb("token_no", [P, N])
        ident16 = sb("ident16", [P, P], F16)
        lanes = sb("lanes", [P, E])
        before = sb("before", [P, P])
        before16 = sb("before16", [P, P], BF16)
        all16 = sb("all16", [P, P], BF16)
        block_start = sb("block_start", [1, NB])
        ones = sb("ones", [1, P])
        ones16 = sb("ones16", [1, P], BF16)
        eps = sb("eps", [P, 1])
        gates = sb("gates", [P, 4])
        tg = sb("tg", [P, 4])
        q_w = sb("q_w", [P, D])
        kv_w = sb("kv_w", [P, 2 * D])
        proj_w = sb("proj_w", [P, D])
        wk_t = sb("wk_t", [P, D])
        wo_t = sb("wo_t", [P, D])
        route = sb("route", [P, 2, E])
        q_b = sb("q_b", [P, 1])
        q_bs = sb("q_bs", [P, 1])
        k_b = sb("k_b", [P, 1])
        bk1 = sb("bk1", [P, 1])
        v_b = sb("v_b", [P, D])
        proj_b = sb("proj_b", [1, D])
        bo1 = sb("bo1", [P, D])
        w_up1 = sb("w_up1", [P, E, F])
        w_down1 = sb("w_down1", [P, E, FC, D])
        mask4 = sb("mask4", [P, B // 4], U32)
        key_bias = sb("key_bias", [P, B])
        mask_row4 = sb("mask_row4", [1, B * S // 4], U32)
        key_row = sb("key_row", [1, B, S], BF16)
        vals0 = sb("vals0", [P, B, PAIRS, 2 * (DH + 1)])
        z = sb("z", [P, CT, D])
        zt = sb("zt", [P, N])
        q = sb("q", [P, 2, N])
        neg_max = sb("neg_max", [P, TPB, H])
        nmt = sb("nmt", [H, N], BF16)
        inv = sb("inv", [P, TPB, H])
        on = sb("on", [P, TPB, D])
        ot = sb("ot", [P, N])
        stats = sb("stats", [P, CT, 6])
        mv = sb("mv", [P, CT, 2])
        k1 = sb("k1", [P, B, S])
        v1 = sb("v1", [S, B, D])
        s1 = sb("s1", [P, TPB, S])
        nm1 = sb("nm1", [P, TPB])
        e1 = sb("e1", [P, TPB, S])
        sum1 = sb("sum1", [P, TPB])
        p1 = sb("p1", [P, TPB, S])
        pt1 = sb("pt1", [S, N])
        lg = sb("lg", [P, T, E])
        gate = sb("gate", [P, T, E])
        top8 = sb("top8", [P, T, 8])
        idx8 = sb("idx8", [P, T, 8], mybir.dt.uint32)
        pick = sb("pick", [P, 2, T])
        hot0 = sb("hot0", [P, T, E])
        hot1 = sb("hot1", [P, T, E])
        hot16 = sb("hot16", [P, T, E], BF16)
        tot = sb("tot", [P, E, TG])
        cum = sb("cum", [P, E, TG])
        ranks = sb("ranks", [P, TG, E])
        cnt = sb("cnt", [P, 4, E])
        cnt_i = sb("cnt_i", [P, 2, E], I32)
        zero_e = sb("zero_e", [P, E * TG])
        posf = sb("posf", [P, 2, T])
        pos = sb("pos", [P, 2, T], U32)
        starts = sb("starts", [1, NB, E])
        expertf = sb("expertf", [1, NB])
        expert = sb("expert", [1, GR * NB], U32)
        part = sb("part", [P, 2, T])
        scr = sb("scr", [P, T, E])
        left = sb("left", [P, 2, N])
        best = sb("best", [P, CAP])
        best_at = sb("best_at", [P, CAP], U32)
        best_no = sb("best_no", [P, CAP])
        slots = sb("slots", [P, 2, B, FC])
        o16 = sb("o16", [P, TPB, D], BF16)

        area_k = sb("area_k", [P, 4096])
        area_h = sb("area_h", [P, 4096])
        area_z = sb("area_z", [P, 4096])
        area_m = sb("area_m", [P, 3072])
        area_w = sb("area_w", [P, 8192])
        k0 = area_k[:, 0:B * S].rearrange("p (b s) -> p b s", b=B)
        k0s = area_k[:, B * S:B * S + 2 * H * S].rearrange("p (u h s) -> p u h s", u=2, h=H)
        seq_zero = area_k[:, 3072:4096].rearrange("p (b s) -> p b s", s=S)
        wb = area_w[:, 0:4096].rearrange("p (r w) -> p r w", r=DEEP)
        x_row = area_w[:, 4096:5120].rearrange("p (r t d) -> p r t d", r=DEEP, d=D)
        y_row = area_w[:, 5120:6144].rearrange("p (r t d) -> p r t d", r=DEEP, d=D)
        xt = area_w[:, 6144:6656].rearrange("p (u n) -> p u n", u=2)
        yg = area_k[:, 3072:4096].rearrange("p (r d) -> p r d", d=D)
        taken = [a[:, 0:4096].rearrange("p (e b s) -> p e b s", e=E, s=CAP) for a in (area_k, area_w)]
        ctx_t = area_h[:, 0:B * S].rearrange("p (b s) -> p b s", b=B)
        pt0 = area_h[:, 0:PAIRS * N].rearrange("p (h n) -> p h n", h=PAIRS)
        hid = area_h[:, :].rearrange("p (u f n) -> p u f n", u=2, f=FC)
        hid0 = area_h[:, 0:2 * FC * SW].rearrange("p (u f n) -> p u f n", u=2, f=FC)
        zt2 = area_h[:, 3072:4096].rearrange("p (u n) -> p u n", u=2)
        zt2d = area_h[:, 0:2 * CW].rearrange("p (u n) -> p u n", u=2)
        cell_zero = area_h[:, 2048:4096].rearrange("p (t s) -> p t s", s=S)
        z_all = area_z[:, :].rearrange("p (t d) -> p t d", d=D)
        yt = [a[:, :].rearrange("p (b e s) -> p b e s", b=HB, e=E) for a in (area_z, area_k)]
        cell = area_m[:, 0:T * S].rearrange("p (t s) -> p t s", s=S)
        seq = area_m[:, T * S:T * S + B * S].rearrange("p (b s) -> p b s", s=S)
        z_hi, z_lo = (area_m[:, 256 * k:256 * (k + 1)].bitcast(F16).rearrange("p (u j d) -> p u j d", u=2, j=TPB)
                      for k in range(2))
        y_slots = area_m[:, 512:1536].rearrange("p (u k d) -> p u k d", u=2, k=FC)
        k16 = area_w[:, 6656:7680].bitcast(F16).rearrange("p (u h s) -> p u h s", u=2, h=H)
        q16 = area_w[:, 7680:7936].bitcast(F16).rearrange("p (u n) -> p u n", u=2)
        one_hot = area_w[:, 4096:5120].bitcast(F16).rearrange("p (u k n) -> p u k n", u=2, k=FC)
        sel = area_w[:, 5120:6144].bitcast(F16).rearrange("p (u j m) -> p u j m", u=2, j=TPB)
        gated = area_w[:, 6144:8192].rearrange("p (u k n) -> p u k n", u=2, k=FC)

        bank = [ctx.enter_context(nc.psum_tensor(f"bank{i}", [P, 512], F32)) for i in range(4)]
        big = [ctx.enter_context(nc.psum_tensor(f"big{i}", [P, 1024], F32)) for i in range(2)]

        names = """ld_const ld_ctx ld_w ld_keys ld_mask ld_e1 ld_r stored
            pe_setup act_setup dve_setup pool_setup masks_ready
            a_keys16 a_keys a_z a_tz a_zt a_qm a_q16 a_q a_s a_max a_tm a_mt a_p2 a_exp a_av a_on a_to a_ot a_pj a_read
            ln_sqrt x_done dve pool held_dve held_act held_pe
            r_z r_tz r_zt r_lg r_d r_exp
            b_hot b_rank b_read b_pos xs_clear b_sc0 b_sc1 b_tx b_xt b_up b_act b_y b_yr b_add
            c_z c_tz c_zt c_s c_sub c_exp c_p c_tp c_pt c_o
            d_pr d_rows d_best d_cols d_z d_hot d_ht d_sel d_xg d_xge
            d_up d_act d_y d_yt d_gated d_ty d_ys d_out0 d_o d_out""".split()
        s = {n: sem(n) for n in names}

        def load(eng, which, dst, src):
            eng.dma_start(dst, src).then_inc(s[which], 16)

        ld_x = [sem(f"ld_x{i}") for i in range(X_LOADS)]
        gathered = [sem(f"b_gat{i}") for i in range(RING)]
        got_x, got_w, kept = ([sem(f"{k}{i}") for i in range(DEEP)] for k in ("b_ld_x", "b_ld_w", "b_st"))

        def nth(n, r):
            return 16 // DEEP * (n - r) + 16

        slots_in = [nc.dram_tensor(f"slots_in{g}", (ROWS, D), F32, kind="Internal").ap() for g in range(GR)]
        slots_out = [nc.dram_tensor(f"slots_out{g}", (ROWS, D), F32, kind="Internal").ap() for g in range(GR)]

        def block_rows(tables, g, n):
            rows = tables[g].rearrange("(n t p) d -> p n t d", p=P, t=SW // P)
            return rows[:, bass.ds(n - NB * g, 1), :, :].squeeze(1)

        LOADS = {"ld_const": 7, "ld_ctx": 1, "ld_w": 12, "ld_keys": 2, "ld_mask": 2, "ld_e1": 2, "ld_r": 2}

        def loaded(eng, which):
            eng.wait_ge(s[which], 16 * LOADS[which])

        block = ctx.enter_context(nc.Block())

        @block.sync
        def _(sp):
            x_in = a["x"].rearrange("(t p) d -> p t d", p=P)
            for i in range(X_LOADS):
                tiles = slice(T // X_LOADS * i, T // X_LOADS * (i + 1))
                sp.dma_start(x[:, tiles, :], x_in[:, tiles, :]).then_inc(ld_x[i], 16)
                if i == 0:
                    load(sp, "ld_ctx", ctx_t, a["ctx_t"])
            load(sp, "ld_w", kv_w[:, :], a["kv_w"])
            load(sp, "ld_w", k_b[:, :], a["kv_b"][0:D].rearrange("(p a) -> p a", a=1))
            load(sp, "ld_w", v_b[:, :], bcast_rows(a["kv_b"][D:2 * D]))
            load(sp, "ld_const", ident[:, :], a["ident"])
            load(sp, "ld_const", head_rows[:, :], a["head_rows"])
            load(sp, "ld_const", head_pick[:, :, :], a["head_pick"])
            load(sp, "ld_const", token_no[:, :], a["token_no"])
            load(sp, "ld_const", lanes[:, :], a["lanes"])
            load(sp, "ld_const", before[:, :], a["before"])
            load(sp, "ld_const", block_start[:, :], a["block_start"])
            load(sp, "ld_keys", mask4[:, :], a["mask_t"])
            load(sp, "ld_keys", mask_row4[:, :], a["mask_row"])
            load(sp, "ld_mask", cell, a["cell"].rearrange("(t p) s -> p t s", p=P))
            load(sp, "ld_mask", area_m[:, T * S:T * S + B * S], bcast_rows(a["seq"]))
            load(sp, "ld_w", q_w[:, :], a["q_w"])
            load(sp, "ld_w", q_b[:, :], a["q_b"].rearrange("(p a) -> p a", a=1))
            load(sp, "ld_w", proj_w[:, :], a["proj_w"])
            load(sp, "ld_w", proj_b[:, :], a["proj_b"].rearrange("(a d) -> a d", a=1))
            load(sp, "ld_w", gates[:, 0:2], bcast_rows(a["g_xattn"]))
            load(sp, "ld_w", gates[:, 2:4], bcast_rows(a["g_ffn"]))
            load(sp, "ld_w", wk_t[:, :], a["wk_t"])
            load(sp, "ld_w", wo_t[:, :], a["wo_t"])
            load(sp, "ld_w", bk1[:, :], a["b_k"].rearrange("(p a) -> p a", a=1))
            load(sp, "ld_r", bo1[:, :], bcast_rows(a["b_o"]))
            load(sp, "ld_r", route[:, :, :], a["route"])
            load(sp, "ld_e1", w_up1[:, :, :], a["w_up1"])
            load(sp, "ld_e1", w_down1[:, :, :], a["w_down1"])
            sp.wait_ge(s["pool_setup"], 1)
            for rows in slots_in:
                sp.dma_start(rows.rearrange("(p r) d -> p r d", p=P),
                             zero_e[:, 0:D].unsqueeze(1).broadcast_to([P, ROWS // P, D])).then_inc(s["xs_clear"], 16)
            if phases >= 2:
                sp.wait_ge(s["b_pos"], 1)
                def block_load(g, n, r, store_g=None):
                    e = sp.value_load(expert[0:1, bass.ds(n, 1)], min_val=0, max_val=E - 1)
                    if store_g is not None:
                        sp.wait_ge(s["b_y"], n - DEEP + 1)
                    sp.dma_start(wb[:, r, :], a["w0"][bass.ds(e, 1), :, :].squeeze(0)).then_inc(got_w[r], 16)
                    sp.dma_start(x_row[:, r, :, :], block_rows(slots_in, g, n)).then_inc(got_x[r], 16)
                    if store_g is not None:
                        block_store(store_g, n - DEEP, r)

                def block_store(g, n, r):
                    sp.wait_ge(s["b_yr"], n + 1)
                    sp.dma_start(block_rows(slots_out, g, n), y_row[:, r, :, :]).then_inc(kept[r], 16)

                sp.wait_ge(s["b_sc0"], 16 * 2 * TG)
                for n in range(DEEP):
                    block_load(0, n, n)
                with sp.Fori(DEEP, NB - DEEP + 1 - NB % DEEP, DEEP) as n:
                    for i in range(DEEP):
                        block_load(0, n + i, i, store_g=0)
                for n in range(NB - NB % DEEP, NB):
                    block_load(0, n, n % DEEP, store_g=0)
                sp.wait_ge(s["b_pos"], 2)
                sp.wait_ge(s["b_sc1"], 16 * 2 * TG)
                for n in range(NB, NB + DEEP):
                    block_load(1, n, n % DEEP, store_g=0)
                rest = (NB - DEEP) % DEEP
                with sp.Fori(NB + DEEP, 2 * NB - rest - DEEP + 1, DEEP) as n:
                    for i in range(DEEP):
                        block_load(1, n + i, (NB + i) % DEEP, store_g=1)
                for n in range(2 * NB - rest, 2 * NB):
                    block_load(1, n, n % DEEP, store_g=1)
                for n in range(2 * NB - DEEP, 2 * NB):
                    block_store(1, n, n % DEEP)
            if phases < 4:
                sp.wait_ge(s["x_done"], 1)
                sp.dma_start(out.rearrange("(t p) d -> p t d", p=P), x[:, :, :]).then_inc(s["stored"], 16)
                sp.wait_ge(s["stored"], 16)
                return
            x_out = out.rearrange("(t p) d -> p t d", p=P)
            for b in range(B):
                sp.wait_ge(s["d_out"], b + 1)
                sp.dma_start(x_out[:, TPB * b:TPB * b + TPB, :], x[:, TPB * b:TPB * b + TPB, :]).then_inc(s["stored"], 16)
            sp.wait_ge(s["stored"], 16 * B)

        @block.gpsimd
        def _(pool):
            ch = Chain(pool, s["pool"])
            ch.done(pool.memset(ones[:, :], 1.0))
            ch.done(pool.memset(ones16[:, :], 1.0))
            ch.done(pool.memset(eps[:, :], EPS))
            ch.done(pool.memset(all16[:, :], 1.0))
            ch.done(pool.memset(zero_e[:, :], 0.0))
            ch.link(pool.memset(vals0[:, :, :, :], 0.0))
            ch.done(pool.memset(vals0[0:S, :, :, DH:DH + 1], 1.0))
            pool.memset(vals0[S:P, :, :, 2 * DH + 1:2 * DH + 2], 1.0).then_inc(s["pool_setup"], 1)

            pool.wait_ge(s["pool_setup"], 1)
            loaded(pool, "ld_mask")
            ch.done(pool.tensor_scalar(cell_zero, cell, 0.0, MASKED, ALU.is_le, ALU.mult))
            ch.link(pool.tensor_scalar(seq_zero, seq, 0.0, MASKED, ALU.is_le, ALU.mult))
            ch.done(pool.tensor_scalar(cell, cell, LEAST, None, ALU.max))
            pool.tensor_scalar(seq, seq, LEAST, None, ALU.max).then_inc(s["pool_setup"], 1)

            def keys(c, u):
                if not isinstance(c, int) or c >= 2:
                    pool.wait_ge(s["a_p2"], 2 * c - 2)
                for dst, done in ((k16, "a_keys16"), (k0s, "a_keys")):
                    pool.tensor_tensor(dst[:, u, :, :], k0[:, bass.ds(c, 1), :].broadcast_to([P, H, S]),
                                       head_rows[:, :].unsqueeze(2).broadcast_to([P, H, S]), ALU.mult).then_inc(s[done], 1)

            def scatter(g, tiles):
                pool.wait_ge(s["b_pos"], g + 1)
                for t in tiles:
                    for k in range(2):
                        pool.indirect_dma_start(out=slots_in[g], out_offset=bass.IndirectOffsetOnAxis(ap=pos[:, k, t:t + 1], axis=0),
                                                in_=z_all[:, t, :], in_offset=None).then_inc(s[f"b_sc{g}"], 16)

            pool.wait_ge(s["pool_setup"], 2)
            pool.wait_ge(s["dve_setup"], 6)
            keys(0, 0)
            keys(1, 1)
            pool.wait_ge(s["masks_ready"], 2)
            ch.done(pool.tensor_tensor(cell, cell, cell_zero, ALU.add))
            ch.link(pool.tensor_tensor(seq, seq, seq_zero, ALU.add))
            cell_b = cell.rearrange("p (b t) s -> p b t s", t=TPB)
            for t in range(TPB):
                pool.wait_ge(s["pool"], ch.k)
                pool.tensor_tensor(cell_b[:, :, t, :], cell_b[:, :, t, :], seq, ALU.add).then_inc(s["pool_setup"], 1)
            with pool.Fori(2, FIRST - 1, 2) as c:
                keys(c, 0)
                keys(c + 1, 1)
            keys(FIRST, 0)
            keys(FIRST + 1, 1)
            pool.wait_ge(s["xs_clear"], 16 * GR)
            scatter(0, range(0, TG // 2))
            keys(FIRST + 2, 0)
            scatter(0, range(TG // 2, TG))
            keys(FIRST + 3, 1)
            for c in range(FIRST + 4, B):
                keys(c, c % 2)
            scatter(1, range(TG, T))
            for g in range(GR):
                for n in range(NB * (g + 1) - DEEP, NB * (g + 1)):
                    pool.wait_ge(kept[n % DEEP], nth(n, n % DEEP))
                for t in range(TG * g, TG * g + TG):
                    for k in range(2):
                        m = 2 * t + k
                        if m >= RING:
                            pool.wait_ge(s["b_add"], m - RING + 1)
                        pool.indirect_dma_start(out=yg[:, m % RING, :], out_offset=None, in_=slots_out[g],
                                                in_offset=bass.IndirectOffsetOnAxis(ap=pos[:, k, t:t + 1], axis=0))\
                            .then_inc(gathered[m % RING], 16)

        @block.scalar
        def _(act):
            act.preload_act_table(ACT.Exp)
            act.wait_ge(s["ld_w"], 16 * LOADS["ld_w"])
            act.activation(tg[:, :], gates[:, :], ACT.Tanh)
            act.activation(q_bs[:, :], q_b[:, :], ACT.Copy, scale=SCALE).then_inc(s["act_setup"], 1)

            act.wait_ge(s["pool_setup"], 2)
            act.activation(cell, cell, ACT.Ln).then_inc(s["masks_ready"], 1)
            act.activation(seq, seq, ACT.Ln).then_inc(s["masks_ready"], 1)

            def layer_rstd(n, i, tiles=slice(0, T)):
                act.wait_ge(s["ln_sqrt"], i)
                act.activation(rstd[:, 1 - n % 2, tiles], mean_var[:, tiles, 1], ACT.Sqrt, bias=eps[:, 0:1])\
                    .then_inc(s["act_setup"], 1)

            layer_rstd(1, 1)
            act.preload_act_table(ACT.Exp)

            def evac_zt(c):
                wait(act, s["a_tz"], c + 1)
                act.activation(zt[:, :], bank[0][:, 0:N], ACT.Copy).then_inc(s["a_zt"], 1)

            def evac_q(c, u):
                wait(act, s["a_qm"], c + 1)
                for dst, done in ((q16, "a_q16"), (q, "a_q")):
                    act.activation(dst[:, u, :], bank[1][:, 0:N], ACT.Identity, bias=q_bs[:, 0:1], scale=SCALE)\
                        .then_inc(s[done], 1)

            def exps(c, h):
                hold(act, s["a_p2"], 2 * c + h + 1, s["held_act"])
                act.activation(area_h[:, h * 1024:(h + 1) * 1024], big[h][:, :], ACT.Exp,
                               bias=key_bias[:, bass.ds(c, 1)]).then_inc(s["a_exp"], 1)

            def a_iter(c, u, now=True, last=True, nxt=True):
                if nxt:
                    evac_zt(c + 1)
                    evac_q(c + 1, 1 - u)
                if now:
                    wait(act, s["a_tm"], c + 1)
                    act.activation(nmt[:, :], bank[0][0:H, 0:N], ACT.Copy).then_inc(s["a_mt"], 1)
                    exps(c, 0)
                    exps(c, 1)
                if last:
                    wait(act, s["a_to"], c)
                    act.activation(ot[:, :], bank[0][:, 0:N], ACT.Copy).then_inc(s["a_ot"], 1)

            evac_zt(0)
            evac_q(0, 0)
            act.wait_ge(s["dve_setup"], 2)
            a_iter(0, 0, last=False)
            a_iter(1, 1)
            with act.Fori(2, FIRST - 1, 2) as c:
                a_iter(c, 0)
                a_iter(c + 1, 1)

            def route_evac(chunks, dst):
                for c in chunks:
                    act.wait_ge(s["r_tz"], c + 1)
                    if c - chunks[0] >= 2:
                        act.wait_ge(s["r_lg"], c - 1)
                    act.activation(dst[:, c % 2, :], bank[c % 2][:, :], ACT.Copy).then_inc(s["r_zt"], 1)

            def route_tanh(g):
                act.wait_ge(s["r_d"], g + 1)
                tiles = slice(TG * g, TG * (g + 1))
                act.activation(part[:, 0, tiles], pick[:, 0, tiles], ACT.Tanh, scale=0.5).then_inc(s["r_exp"], 1)

            layer_rstd(2, 2, slice(0, TG))
            act.preload_act_table(ACT.Exp)
            act.wait_ge(s["pool_setup"], 2 + TPB)
            route_evac(range(0, CG), zt2)
            route_tanh(0)

            with act.Fori(FIRST, B - 3, 2) as c:
                a_iter(c, 0)
                a_iter(c + 1, 1)
            a_iter(B - 2, 0)
            a_iter(B - 1, 1, nxt=False)
            a_iter(B, 0, now=False, nxt=False)

            if phases < 2:
                return

            def hidden(n, u, func, done):
                for f in range(FC):
                    act.wait_ge(s[done[0]], FC * n + f + 1)
                    src = big[f // 2][:, (f % 2) * CW:(f % 2 + 1) * CW]
                    act.activation(hid[:, u, f, :], src, func).then_inc(s[done[1]], 1)

            layer_rstd(2, 3, slice(TG, T))
            act.preload_act_table(ACT.Silu)
            route_evac(range(CG, 2 * CG), zt2)

            def b_xt(n, u):
                act.wait_ge(s["b_tx"], n + 1)
                act.activation(xt[:, u, :], bank[0][:, 0:SW], ACT.Copy).then_inc(s["b_xt"], 1)

            def b_hidden(n, u):
                act.wait_ge(s["b_up"], n + 1)
                act.activation(hid0[:, u, :, :], big[u][:, :].rearrange("p (f n) -> p f n", f=FC), ACT.Silu)\
                    .then_inc(s["b_act"], 1)

            b_xt(0, 0)
            b_xt(1, 1)
            b_hidden(0, 0)
            route_tanh(1)
            with act.Fori(0, GR * NB - 2, 2) as n:
                b_hidden(n + 1, 1)
                b_xt(n + 2, 0)
                b_hidden(n + 2, 0)
                b_xt(n + 3, 1)
            b_hidden(GR * NB - 1, 1)
            if phases < 3:
                return

            layer_rstd(3, 4, slice(0, TG))
            act.preload_act_table(ACT.Exp)

            def c_zt(c):
                act.wait_ge(s["c_tz"], c + 1)
                act.activation(zt[:, :], bank[0][:, 0:N], ACT.Copy).then_inc(s["c_zt"], 1)

            def c_iter(c, nxt=True):
                if nxt:
                    c_zt(c + 1)
                act.wait_ge(s["c_sub"], c + 1)
                act.activation(e1[:, :, :], s1[:, :, :], ACT.Exp).then_inc(s["c_exp"], 1)
                act.wait_ge(s["c_tp"], c + 1)
                act.activation(pt1[:, :], bank[1][0:S, 0:N], ACT.Copy).then_inc(s["c_pt"], 1)

            c_zt(0)
            with act.Fori(0, BG - 1) as c:
                c_iter(c)
            layer_rstd(3, 5, slice(TG, T))
            act.preload_act_table(ACT.Exp)
            with act.Fori(BG - 1, B - 1) as c:
                c_iter(c)
            c_iter(B - 1, nxt=False)
            if phases < 4:
                return

            layer_rstd(4, 6)
            act.preload_act_table(ACT.Exp)
            route_evac(range(CHUNKS, 2 * CHUNKS), zt2d)
            act.wait_ge(s["r_d"], GR + 1)
            act.activation(scr[:, :, :], lg[:, :, :], ACT.Exp).then_inc(s["r_exp"], 1)
            act.preload_act_table(ACT.Gelu_apprx_tanh)

            def select(b, u, free=True):
                act.wait_ge(s["d_ht"], b + 1)
                if free:
                    act.wait_ge(s["d_xg"], b - 1)
                act.activation(sel[:, u, :, :], bank[0][:, :].bitcast(F16).rearrange("p (j m) -> p j m", j=TPB), ACT.Copy)\
                    .then_inc(s["d_sel"], 1)

            def take(half, i):
                act.wait_ge(s["d_xg"], HB * half + i + 1)
                act.activation(taken[half][:, :, bass.ds(i, 1), :].squeeze(2),
                               bank[1][:, :].rearrange("p (e s) -> p e s", e=E), ACT.Copy, scale=1.0 / SPLIT)\
                    .then_inc(s["d_xge"], 1)

            def experts(half, e):
                hidden(E * half + e, e % 2, ACT.Gelu_apprx_tanh, ("d_up", "d_act"))

            def slots_down(b):
                act.wait_ge(s["d_ty"], b + 1)
                if b >= 2:
                    act.wait_ge(s["d_out0"], b - 1)
                act.activation(y_slots[:, b % 2, :, :], bank[0][:, :].rearrange("p (k d) -> p k d", k=FC), ACT.Copy)\
                    .then_inc(s["d_ys"], 1)

            select(0, 0, False)
            select(1, 1, False)
            take(0, 0)
            with act.Fori(2, HB - 1, 2) as b:
                select(b, 0)
                take(0, b - 1)
                select(b + 1, 1)
                take(0, b)
            take(0, HB - 1)
            experts(0, 0)
            for e in range(E):
                if e + 1 < E:
                    experts(0, e + 1)
                select(HB + e, e % 2)
                take(1, e)
            experts(1, 0)
            for e in range(E):
                if e + 1 < E:
                    experts(1, e + 1)
                slots_down(e)
            for b in range(HB, B):
                slots_down(b)

        @block.tensor
        def _(pe):
            mm = pe.matmul
            pe.wait_ge(s["ld_ctx"], 16)
            pe.wait_ge(s["ld_w"], 16 * LOADS["ld_w"])
            for h in range(2):
                mm(bank[h][:, :], kv_w[:, 0:D], ctx_t[:, 8 * h:8 * h + 8, :], start=True, stop=True)\
                    .then_inc(s["pe_setup"], 1)
            for h in range(2):
                mm(bank[2 + h][:, :], wk_t[:, :], ctx_t[:, 8 * h:8 * h + 8, :], start=True, stop=True)\
                    .then_inc(s["pe_setup"], 1)
            for b in range(B):
                for k in range(2):
                    ins = mm(big[b // 8][S * k:S * k + S, (b % 8) * D:(b % 8 + 1) * D], ctx_t[:, b, :], kv_w[:, D:2 * D],
                             start=True, stop=True)
                if b % 8 == 7:
                    ins.then_inc(s["pe_setup"], 1)
            for b in range(B):
                if b % 8 == 0:
                    pe.wait_ge(s["dve_setup"], 3 + b // 8)
                ins = mm(big[b // 8][0:S, (b % 8) * D:(b % 8 + 1) * D], ctx_t[:, b, :], wo_t[:, :], start=True, stop=True)
                if b % 8 == 7:
                    ins.then_inc(s["pe_setup"], 1)

            def transposes(dst, src, n, done, rows=P, cols=P):
                for t in range(n):
                    ins = pe.transpose(dst[0:cols, t * P:(t + 1) * P], src[:, t, :], ident[:, :])
                ins.then_inc(done, 1)

            pe.wait_ge(s["ld_const"], 16 * LOADS["ld_const"])

            def tz(c):
                wait(pe, s["a_z"], c + 1)
                wait(pe, s["a_ot"], c - 2)
                transposes(bank[0], z[:, 0:TPB, :], TPB, s["a_tz"])

            def q_product(c):
                wait(pe, s["a_zt"], c + 1)
                wait(pe, s["a_q"], c)
                mm(bank[1][:, 0:N], q_w[:, :], zt[:, :], start=True, stop=True).then_inc(s["a_qm"], 1)

            def pass1(c, u, t, between=None):
                if t == 0:
                    wait(pe, s["a_q16"], c + 1)
                    wait(pe, s["a_keys16"], c + 1)
                wait(pe, s["a_exp"], 2 * c - 1 + t)
                for g in range(GROUPS):
                    dst = big[t][:, g * HPG * S:(g + 1) * HPG * S]
                    mm(dst, q16[:, u, t * P:(t + 1) * P], k16[:, u, HPG * g:HPG * g + HPG, :], start=True, stop=False)
                    ins = mm(dst, ones16[:, :], key_row[:, bass.ds(c, 1), :].broadcast_to([1, HPG, S]),
                             start=False, stop=True)
                    if g == GROUPS - 1:
                        ins.then_inc(s["a_s"], 1)
                    if between:
                        between(g)

            def values(c, t, pairs):
                for h in pairs:
                    w = 2 * (DH + 1)
                    o = (t * PAIRS + h) * w
                    ins = mm(bank[2][:, o:o + w], pt0[:, h, t * P:(t + 1) * P], vals0[:, bass.ds(c, 1), h, :],
                             start=True, stop=True)
                if t == TPB - 1 and h == PAIRS - 1:
                    ins.then_inc(s["a_av"], 1)

            def pass2(c, u, h, between=None):
                wait(pe, s["a_max"], 2 * c + h + 1)
                wait(pe, s["a_q"], c + 1)
                wait(pe, s["a_keys"], c + 1)
                for k in range(4):
                    pair = 4 * h + k
                    dst = big[h][:, k * N:(k + 1) * N]
                    if between:
                        between(k)
                    mm(dst, k0s[:, u, 2 * pair:2 * pair + 2, :], q[:, u, :], start=True, stop=False)
                    ins = mm(dst, head_pick16[:, pair, :], nmt[:, :], start=False, stop=True)
                ins.then_inc(s["a_p2"], 1)

            def project(c):
                wait(pe, s["a_ot"], c + 1)
                wait(pe, s["a_read"], c + 1)
                for t in range(TPB):
                    dst = bank[3][:, t * P:(t + 1) * P]
                    mm(dst, ot[:, t * P:(t + 1) * P], proj_w[:, :], start=True, stop=False)
                    ins = mm(dst, ones[:, :], proj_b[:, :], start=False, stop=True)
                ins.then_inc(s["a_pj"], 1)

            def a_iter(c, u, now=True, last=True, proj=True, nxt=True):
                def first_values(g):
                    if g == 0:
                        wait(pe, s["a_exp"], 2 * c)
                    values(c - 1, 0, range(2 * g, 2 * g + 2))

                def last_values(k):
                    values(c - 1, 1, range(4 + k, 5 + k))

                if now:
                    pass1(c, u, 0)
                if nxt:
                    tz(c + 1)
                if now:
                    pass1(c, u, 1, first_values if last else None)
                elif last:
                    for g in range(4):
                        first_values(g)
                if nxt:
                    q_product(c + 1)
                if proj:
                    project(c - 2)
                if now:
                    wait(pe, s["a_max"], 2 * c + 2)
                    wait(pe, s["a_ot"], c - 1)
                    transposes(bank[0], neg_max, TPB, s["a_tm"], cols=H)
                if last:
                    values(c - 1, 1, range(0, 4))
                if now:
                    wait(pe, s["a_mt"], c + 1)
                    pass2(c, u, 0, last_values if last else None)
                    pass2(c, u, 1)
                elif last:
                    for k in range(4):
                        last_values(k)
                if last:
                    wait(pe, s["a_on"], c)
                    wait(pe, s["a_mt"], c + 1 if now else 0)
                    transposes(bank[0], on, TPB, s["a_to"])

            pe.wait_ge(s["dve_setup"], 8)
            tz(0)
            q_product(0)
            a_iter(0, 0, last=False, proj=False)
            a_iter(1, 1, proj=False)
            with pe.Fori(2, FIRST - 1, 2) as c:
                a_iter(c, 0)
                a_iter(c + 1, 1)

            def route_products(chunks, layer, rows, ztr, col):
                for c in chunks:
                    pe.wait_ge(s["r_z"], c + 1)
                    if c - chunks[0] >= 2:
                        pe.wait_ge(s["r_zt"], c - 1)
                    transposes(bank[c % 2], rows(c), CT, s["r_tz"])
                    pe.wait_ge(s["r_zt"], c + 1)
                    for t in range(CT):
                        k = col(CT * (c - chunks[0]) + t)
                        ins = mm(bank[2][:, k:k + E], ztr[:, c % 2, P * t:P * t + P], route[:, layer, :],
                                 start=True, stop=True)
                    ins.then_inc(s["r_lg"], 1)

            def route_group(g):
                route_products(range(CG * g, CG * (g + 1)), 0, lambda c: z_all[:, CT * c:CT * c + CT, :], zt2, lambda t: E * t)

            def rank_group(g):
                pe.wait_ge(s["b_hot"], g + 1)
                for k, m in enumerate((before16, all16)):
                    ins = mm(bank[1][:, k * TG * E:(k + 1) * TG * E], m[:, :], hot16[:, TG * g:TG * (g + 1), :],
                             start=True, stop=True)
                ins.then_inc(s["b_rank"], 1)

            loaded(pe, "ld_r")
            pe.wait_ge(s["a_ot"], FIRST - 1)
            pe.wait_ge(s["a_q"], FIRST + 1)
            route_group(0)
            rank_group(0)
            pe.wait_ge(s["b_read"], 1)
            with pe.Fori(FIRST, B - 3, 2) as c:
                a_iter(c, 0)
                a_iter(c + 1, 1)
            a_iter(B - 2, 0)
            a_iter(B - 1, 1, nxt=False)
            a_iter(B, 0, now=False, nxt=False)
            project(B - 1)
            if phases < 2:
                return

            def up(n, w, e, tokens, sems, free):
                for f in range(FC):
                    wait(pe, s[sems[1]], FC * (n - 1) + f + 1 if free else 0)
                    mm(big[f // 2][:, (f % 2) * CW:(f % 2 + 1) * CW], w[:, e, f * P:(f + 1) * P], tokens,
                       start=True, stop=True).then_inc(s[sems[0]], 1)

            route_group(1)

            def b_tx(n, r):
                pe.wait_ge(got_x[r], nth(n, r))
                for t in range(SW // P):
                    ins = pe.transpose(bank[0][:, t * P:(t + 1) * P], x_row[:, r, t, :], ident[:, :])
                ins.then_inc(s["b_tx"], 1)

            def b_up(n, u, r, first=False):
                pe.wait_ge(s["b_xt"], n + 1)
                pe.wait_ge(got_w[r], nth(n, r))
                if not first:
                    pe.wait_ge(s["b_act"], n - 1)
                for f in range(FC):
                    ins = mm(big[u][:, f * SW:(f + 1) * SW], wb[:, r, f * P:(f + 1) * P], xt[:, u, :], start=True, stop=True)
                ins.then_inc(s["b_up"], 1)

            def b_down(n, u, r, first=False):
                pe.wait_ge(s["b_act"], n + 1)
                if not first:
                    pe.wait_ge(s["b_yr"], n - 1)
                for t in range(SW // P):
                    for f in range(FC):
                        ins = mm(bank[2 + u][:, t * D:(t + 1) * D], hid0[:, u, f, t * P:(t + 1) * P], wb[:, r, F + f * D:F + (f + 1) * D],
                                 start=(f == 0), stop=(f == FC - 1))
                ins.then_inc(s["b_y"], 1)

            def b_tx_next(n, r):
                hold(pe, s["b_xt"], n, s["held_pe"])
                b_tx(n, r)

            def b_step(n, i):
                b_up(n + 1, (i + 1) % 2, (i + 1) % DEEP)
                b_tx_next(n + 2, (i + 2) % DEEP)
                b_down(n, i % 2, i)

            b_tx(0, 0)
            b_tx_next(1, 1)
            b_up(0, 0, 0, first=True)
            b_up(1, 1, 1, first=True)
            rank_group(1)
            b_tx_next(2, 2)
            b_down(0, 0, 0, first=True)
            b_up(2, 0, 2)
            b_tx_next(3, 3)
            b_down(1, 1, 1, first=True)
            rest = (GR * NB - 4) % DEEP
            with pe.Fori(2, GR * NB - 2 - rest - DEEP + 1, DEEP) as n:
                for i in range(DEEP):
                    b_step(n + i, (2 + i) % DEEP)
            for n in range(GR * NB - 2 - rest, GR * NB - 2):
                b_step(n, n % DEEP)
            n = GR * NB - 2
            b_up(n + 1, (n + 1) % 2, (n + 1) % DEEP)
            b_down(n, n % 2, n % DEEP)
            b_down(n + 1, (n + 1) % 2, (n + 1) % DEEP)
            if phases < 3:
                return

            def c_tz(c):
                pe.wait_ge(s["c_z"], c + 1)
                transposes(bank[0], z[:, 0:TPB, :], TPB, s["c_tz"])

            def c_scores(c, free=True):
                pe.wait_ge(s["c_zt"], c + 1)
                if free:
                    pe.wait_ge(s["c_sub"], c)
                for t in range(TPB):
                    ins = mm(bank[2][:, t * S:(t + 1) * S], zt[:, t * P:(t + 1) * P], k1[:, bass.ds(c, 1), :],
                             start=True, stop=True)
                ins.then_inc(s["c_s"], 1)

            def c_iter(c, nxt=True):
                if nxt:
                    c_tz(c + 1)
                    c_scores(c + 1)
                hold(pe, s["c_p"], c + 1, s["held_pe"])
                transposes(bank[1], p1, TPB, s["c_tp"], cols=S)
                pe.wait_ge(s["c_pt"], c + 1)
                for t in range(TPB):
                    ins = mm(bank[3][:, t * D:(t + 1) * D], pt1[:, t * P:(t + 1) * P], v1[:, bass.ds(c, 1), :],
                             start=True, stop=True)
                ins.then_inc(s["c_o"], 1)

            hold(pe, s["b_xt"], GR * NB, s["held_pe"])
            pe.wait_ge(s["b_yr"], GR * NB)
            c_tz(0)
            c_scores(0, free=False)
            with pe.Fori(0, B - 1) as c:
                c_iter(c)
            c_iter(B - 1, nxt=False)
            if phases < 4:
                return

            loaded(pe, "ld_e1")
            pe.wait_ge(s["x_done"], 1)
            route_products(range(CHUNKS, 2 * CHUNKS), 1, lambda c: z, zt2d, lambda t: (t % TPB) * B * E + t // TPB * E)
            pe.wait_ge(s["d_pr"], 1)
            for j in range(TPB):
                ins = pe.transpose(bank[0][:, j * P:(j + 1) * P], gate[:, :, :].rearrange("p (j b) e -> p j (b e)", j=TPB)[:, j, :], ident[:, :])
            ins.then_inc(s["d_rows"], 1)
            pe.wait_ge(s["d_best"], 1)
            for k, rows in enumerate((best_no, best)):
                for h in range(2):
                    ins = mm(bank[1][CAP * h:CAP * h + CAP, k * P:(k + 1) * P], rows[:, :], ident[:, :], start=True, stop=True)
            ins.then_inc(s["d_cols"], 1)

            def turn(b, u, free=True):
                pe.wait_ge(s["d_hot"], b + 1)
                if free:
                    pe.wait_ge(s["d_sel"], b)
                for j in range(TPB):
                    for k in range(FC):
                        o = (j * FC + k) * P
                        ins = pe.transpose(bank[0][:, o // 2:(o + P) // 2].bitcast(F16), one_hot[:, u, k, j * P:(j + 1) * P],
                                           ident16[:, :])
                ins.then_inc(s["d_ht"], 1)

            def pick_tokens(b, u, free=True):
                pe.wait_ge(s["d_z"], b + 1)
                pe.wait_ge(s["d_sel"], b + 1)
                if free:
                    pe.wait_ge(s["d_xge"], b)
                for j in range(TPB):
                    for part_ in (z_hi, z_lo):
                        ins = mm(bank[1][:, :], part_[:, u, j, :], sel[:, u, j, :], start=(j == 0 and part_ is z_hi),
                                 stop=(j == TPB - 1 and part_ is z_lo))
                ins.then_inc(s["d_xg"], 1)

            def d_up(half, e):
                n = E * half + e
                up(n, w_up1, e, taken[half][:, e, :, :], ("d_up", "d_act"), n > 0)

            def d_down(half, e):
                n = E * half + e
                pe.wait_ge(s["d_act"], FC * (n + 1))
                if n >= 2:
                    pe.wait_ge(s["d_yt"], n - 1)
                for f in range(FC):
                    ins = mm(bank[2 + e % 2][:, :], w_down1[:, e, f, :], hid[:, e % 2, f, :],
                             start=(f == 0), stop=(f == FC - 1))
                ins.then_inc(s["d_y"], 1)

            def turn_outputs(b):
                if b > 0:
                    pe.wait_ge(s["d_ys"], b)
                for k in range(FC):
                    ins = pe.transpose(bank[0][:, k * P:(k + 1) * P], yt[b // HB][:, b % HB, 2 * k:2 * k + 2, :], ident[:, :])
                ins.then_inc(s["d_ty"], 1)

            def give_back(b):
                pe.wait_ge(s["d_ys"], b + 1)
                pe.wait_ge(s["d_gated"], b + 1)
                if b > 0:
                    pe.wait_ge(s["d_o"], b)
                for j in range(TPB):
                    for k in range(FC):
                        ins = mm(bank[1][:, j * D:(j + 1) * D], gated[:, b % 2, k, j * P:(j + 1) * P], y_slots[:, b % 2, k, :],
                                 start=(k == 0), stop=(k == FC - 1))
                ins.then_inc(s["d_out0"], 1)

            turn(0, 0, False)
            turn(1, 1)
            pick_tokens(0, 0, False)
            with pe.Fori(2, HB - 1, 2) as b:
                turn(b, 0)
                pick_tokens(b - 1, 1)
                turn(b + 1, 1)
                pick_tokens(b, 0)
            pick_tokens(HB - 1, 1)
            pe.wait_ge(s["d_xge"], HB)
            d_up(0, 0)
            for e in range(E):
                if e + 1 < E:
                    d_up(0, e + 1)
                turn(HB + e, e % 2)
                d_down(0, e)
                pick_tokens(HB + e, e % 2)
            pe.wait_ge(s["d_xge"], B)
            pe.wait_ge(s["d_yt"], E)
            d_up(1, 0)
            for e in range(E):
                if e + 1 < E:
                    d_up(1, e + 1)
                turn_outputs(e)
                d_down(1, e)
                give_back(e)
            pe.wait_ge(s["d_yt"], 2 * E)
            turn_outputs(HB)
            for b in range(HB, B):
                if b + 1 < B:
                    turn_outputs(b + 1)
                give_back(b)

        @block.vector
        def _(dve):
            ch = Chain(dve, s["dve"])

            def tile_stats(t0, n):
                hold(dve, ch.sem, ch.base + ch.k, s["held_dve"])
                for t in range(n):
                    ch.done(dve.bn_stats(stats[:, t, :], x[:, bass.ds(t0 + t, 1), :].squeeze(1)))
                hold(dve, ch.sem, ch.base + ch.k, s["held_dve"])
                for t in range(n):
                    ch.done(dve.bn_aggr(mv[:, t, :], stats[:, t, :]))
                dve.wait_ge(ch.sem, ch.base + ch.k)
                ch.link(dve.tensor_copy(mean_var[:, bass.ds(t0, n), :], mv[:, 0:n, :]))

            def layer_norm(n, i, tiles=slice(0, T), asked=False):
                if not asked:
                    dve.drain().then_inc(s["ln_sqrt"], 1)
                dve.wait_ge(s["act_setup"], i + 1)
                of = 1 - n % 2, tiles
                ch.link(dve.reciprocal(rstd[:, *of], rstd[:, *of]))
                ch.link(dve.scalar_tensor_tensor(shift[:, *of], mean_var[:, tiles, 0], -1.0, rstd[:, *of], ALU.mult, ALU.mult))

            def normalize(layer, t0, n, done, rows=z):
                for t in range(n):
                    tile = bass.ds(t0 + t, 1)
                    ins = dve.tensor_scalar(rows[:, t, :], x[:, tile, :].squeeze(1), rstd[:, 1 - layer % 2, tile],
                                            shift[:, 1 - layer % 2, tile], ALU.mult, ALU.add)
                ins.then_inc(s[done], 1)

            for c in range(CHUNKS):
                if c % (CHUNKS // X_LOADS) == 0:
                    dve.wait_ge(ld_x[c // (CHUNKS // X_LOADS)], 16)
                tile_stats(CT * c, CT)
            dve.drain().then_inc(s["ln_sqrt"], 1)
            dve.wait_ge(s["ld_const"], 16 * LOADS["ld_const"])
            loaded(dve, "ld_keys")
            ch.done(dve.tensor_copy(before16[:, :], before[:, :]))
            ch.done(dve.tensor_copy(ident16[:, :], ident[:, :]))
            ch.done(dve.tensor_copy(head_pick16[:, :, :], head_pick[:, :, :]))
            dve.tensor_scalar(key_row[:, :, :], mask_row4[:, :].bitcast(U8).rearrange("p (b s) -> p b s", s=S), MASKED, None,
                              ALU.mult).then_inc(s["dve_setup"], 1)
            dve.tensor_scalar(key_bias[:, :], mask4[:, :].bitcast(U8), MASKED, None, ALU.mult).then_inc(s["dve_setup"], 1)
            dve.wait_ge(s["pool_setup"], 1)
            dve.wait_ge(s["ld_w"], 16 * LOADS["ld_w"])
            for h in range(2):
                dve.wait_ge(s["pe_setup"], 5 + h)
                for k in range(2):
                    r = slice(S * k, S * k + S)
                    for j in range(2):
                        v = big[h][r, 512 * j:512 * j + 512].rearrange("p (b h k d) -> p b h k d", b=4, h=PAIRS, k=2)
                        bias = v_b[r, :].rearrange("p (h k d) -> p h k d", h=PAIRS, k=2)[:, :, k, :]
                        b0 = 8 * h + 4 * j
                        ins = dve.tensor_tensor(vals0[r, b0:b0 + 4, :, k * (DH + 1):k * (DH + 1) + DH], v[:, :, :, k, :],
                                                bias.unsqueeze(1).broadcast_to([S, 4, PAIRS, DH]), ALU.add)
                        if (k, j) == (1, 1):
                            ins.then_inc(s["dve_setup"], 1)
            for h in range(2):
                dve.tensor_scalar(k0[:, 8 * h:8 * h + 8, :], bank[h][:, :].rearrange("p (b s) -> p b s", s=S),
                                  k_b[:, 0:1], None, ALU.add)\
                    .then_inc(s["dve_setup"], 1)
            dve.wait_ge(s["ld_r"], 16 * LOADS["ld_r"])
            for h in range(2):
                ins = dve.tensor_scalar(k1[:, 8 * h:8 * h + 8, :], bank[2 + h][:, :].rearrange("p (b s) -> p b s", s=S),
                                        bk1[:, 0:1], None, ALU.add)
            for h in range(2):
                dve.wait_ge(s["pe_setup"], 7 + h)
                dve.tensor_tensor(v1[:, 8 * h:8 * h + 8, :], big[h][0:S, :].rearrange("p (b d) -> p b d", d=D),
                                  bo1[0:S, :].unsqueeze(1).broadcast_to([S, 8, D]), ALU.add)\
                    .then_inc(s["dve_setup"], 1)

            dve.wait_ge(s["act_setup"], 1)
            layer_norm(1, 1, asked=True)

            def add_projected(c):
                wait(dve, s["a_pj"], c + 1)
                xs = x[:, bass.ds(TPB * c, TPB), :]
                ch.link(dve.scalar_tensor_tensor(xs, bank[3][:, 0:N].rearrange("p (t d) -> p t d", t=TPB),
                                                 tg[:, 0:1], xs, ALU.mult, ALU.add))
                dve.sem_inc(s["a_read"], 1)
                tile_stats(TPB * c, TPB)

            def a_iter(c, now=True, last=True, proj=True, nxt=True):
                if now:
                    for t in range(TPB):
                        wait(dve, s["a_s"], TPB * c + t + 1)
                        wait(dve, s["a_tm"], c)
                        dve.tensor_reduce(neg_max[:, t, :], big[t][:, :].rearrange("p (h s) -> p h s", s=S), AX.X,
                                          ALU.max, negate=True).then_inc(s["a_max"], 1)
                if nxt:
                    wait(dve, s["a_tz"], c + 2)
                    normalize(1, TPB * (c + 2), TPB, "a_z")
                if proj:
                    add_projected(c - 2)
                if last:
                    wait(dve, s["a_av"], c)
                    o = bank[2][:, 0:TPB * H * (DH + 1)].rearrange("p (t h d) -> p t h d", t=TPB, h=H)
                    ch.link(dve.reciprocal(inv[:, :, :], o[:, :, :, DH]))
                    dve.tensor_tensor(on[:, :, :].rearrange("p t (h d) -> p t h d", h=H), o[:, :, :, 0:DH],
                                      inv[:, :, :].unsqueeze(3).broadcast_to([P, TPB, H, DH]), ALU.mult)\
                        .then_inc(s["a_on"], 1)

            normalize(1, 0, TPB, "a_z")
            dve.sem_inc(s["a_read"], 1)
            dve.wait_ge(s["a_tz"], 1)
            normalize(1, TPB, TPB, "a_z")
            a_iter(0, last=False, proj=False)
            a_iter(1, proj=False)
            per = 2 + 2 * TPB + 1
            base = ch.k
            with dve.Fori(2, FIRST - 1, 2) as c:
                ch.start(base + per * (c - 2))
                a_iter(c)
                a_iter(c + 1)
                assert ch.k == 2 * per
            ch.start(0, base + per * (FIRST - 2))

            def link_all():
                dve.wait_ge(ch.sem, ch.base + ch.k)

            lanes_all = lanes[:, :].unsqueeze(1).broadcast_to([P, TG, E])

            def route_group(g):
                tiles = slice(TG * g, TG * (g + 1))
                layer_norm(2, 2 + g, tiles)
                for c in range(CG * g, CG * (g + 1)):
                    normalize(2, CT * c, CT, "r_z", z_all[:, CT * c:CT * c + CT, :])
                dve.wait_ge(s["r_lg"], CG * (g + 1))
                ch.link(dve.tensor_copy(lg[:, tiles, :], bank[2][:, 0:TG * E].rearrange("p (t e) -> p t e", e=E)))
                for t in range(TG * g, TG * (g + 1)):
                    ch.done(dve.max(top8[:, t, :], lg[:, t, :]))
                link_all()
                dve.tensor_tensor(pick[:, 0, tiles], top8[:, tiles, 0], top8[:, tiles, 1], ALU.subtract).then_inc(s["r_d"], 1)
                for t in range(TG * g, TG * (g + 1)):
                    ch.done(dve.max_index(idx8[:, t, :], top8[:, t, :], lg[:, t, :]))
                dve.wait_ge(s["r_exp"], g + 1)
                link_all()
                ch.link(dve.tensor_copy(pick[:, :, tiles], idx8[:, tiles, 0:2].rearrange("p t k -> p k t")))
                for k, dst in enumerate((hot0, hot1)):
                    ch.done(dve.tensor_tensor(dst[:, tiles, :], lanes_all, pick[:, k, tiles].unsqueeze(2).broadcast_to([P, TG, E]),
                                              ALU.is_equal))
                link_all()
                dve.tensor_tensor(hot16[:, tiles, :], hot0[:, tiles, :], hot1[:, tiles, :], ALU.add).then_inc(s["b_hot"], 1)
                for k in range(2):
                    ch.link(dve.tensor_scalar(part[:, 1 - k, tiles], part[:, 0, tiles], -0.5 if k == 0 else 0.5, 0.5,
                                              ALU.mult, ALU.add))
                ch.done(dve.tensor_scalar(part[:, :, tiles], part[:, :, tiles], tg[:, 2:3], None, ALU.mult))
                dve.wait_ge(s["b_rank"], g + 1)
                prefix = bank[1][:, 0:TG * E].rearrange("p (t e) -> p t e", e=E)
                totals = bank[1][:, TG * E:2 * TG * E].rearrange("p (t e) -> p e t", e=E)
                ch.link(dve.tensor_copy(tot[:, :, :], totals))
                flat_tot, flat_cum = tot[:, :, :].rearrange("p e t -> p (e t)"), cum[:, :, :].rearrange("p e t -> p (e t)")
                ch.done(dve.reduce_sum(cnt[:, 0, :], tot[:, :, :], AX.X))
                ch.link(dve.tensor_tensor_scan(flat_cum, flat_tot, zero_e[:, :], 0.0, ALU.add, ALU.add))
                ch.done(dve.tensor_tensor(flat_cum, flat_cum, flat_tot, ALU.subtract))
                ch.link(dve.tensor_scalar(cnt_i[:, 0, :], cnt[:, 0, :], float(SW - 1), None, ALU.add))
                ch.link(dve.tensor_scalar(cnt_i[:, 1, :], cnt_i[:, 0, :], -SW, None, ALU.bitwise_and))
                ch.link(dve.tensor_copy(cnt[:, 1, :], cnt_i[:, 1, :]))
                ch.link(dve.tensor_tensor_scan(cnt[:, 2, :], cnt[:, 1, :], zero_e[:, 0:E], 0.0, ALU.add, ALU.add))
                ch.link(dve.tensor_tensor(cnt[:, 3, :], cnt[:, 2, :], cnt[:, 1, :], ALU.subtract))
                ch.link(dve.tensor_tensor(cnt[:, 3, :], cnt[:, 3, :], cum[:, :, 0], ALU.subtract))
                ch.link(dve.tensor_tensor(cum[:, :, :], cum[:, :, :], cnt[:, 3, :].unsqueeze(2).broadcast_to([P, E, TG]), ALU.add))
                ch.link(dve.tensor_tensor(ranks[:, :, :], prefix, cum[:, :, :].rearrange("p e t -> p t e"), ALU.add))
                dve.sem_inc(s["b_read"], 1)
                for k, hot in enumerate((hot0, hot1)):
                    ch.link(dve.tensor_tensor(scr[:, TG * k:TG * (k + 1), :], hot[:, tiles, :], ranks[:, :, :], ALU.mult))
                for k in range(2):
                    ch.done(dve.reduce_sum(posf[:, k, tiles], scr[:, TG * k:TG * (k + 1), :], AX.X))
                ch.link(dve.tensor_tensor(starts[:, :, :], cnt[0:1, 2, :].unsqueeze(1).broadcast_to([1, NB, E]),
                                          block_start[:, :].unsqueeze(2).broadcast_to([1, NB, E]), ALU.is_le))
                ch.link(dve.reduce_sum(expertf[:, :], starts[:, :, :], AX.X))
                ch.link(dve.tensor_scalar(expert[:, NB * g:NB * (g + 1)], expertf[:, :], float(E - 1), None, ALU.min))
                dve.tensor_copy(pos[:, :, tiles], posf[:, :, tiles]).then_inc(s["b_pos"], 1)

            route_group(0)
            base = ch.k
            with dve.Fori(FIRST, B - 3, 2) as c:
                ch.start(base + per * (c - FIRST))
                a_iter(c)
                a_iter(c + 1)
                assert ch.k == 2 * per
            ch.start(0, base + per * (B - 2 - FIRST))
            a_iter(B - 2, nxt=False)
            a_iter(B - 1, nxt=False)
            a_iter(B, now=False, nxt=False)
            add_projected(B - 1)
            if phases < 2:
                dve.drain().then_inc(s["x_done"], 1)
                return

            route_group(1)

            def y_out(n, r, first=False):
                dve.wait_ge(s["b_y"], n + 1)
                if not first:
                    dve.wait_ge(kept[r], nth(n - DEEP, r))
                dve.tensor_copy(y_row[:, r, :, :], bank[2 + r % 2][:, 0:SW].rearrange("p (t d) -> p t d", d=D))\
                    .then_inc(s["b_yr"], 1)

            def combine(t, r):
                xs_t = x[:, bass.ds(t, 1), :].squeeze(1)
                for k in range(2):
                    dve.wait_ge(gathered[2 * r + k], 4 * (t - r) + 16)
                    dve.scalar_tensor_tensor(xs_t, yg[:, 2 * r + k, :], part[:, k, bass.ds(t, 1)], xs_t, ALU.mult, ALU.add)\
                        .then_inc(s["b_add"], 1)
                    dve.wait_ge(s["b_add"], 2 * t + k + 1)
                tile_stats(t, 1)

            for n in range(DEEP):
                y_out(n, n, first=True)
            with dve.Fori(DEEP, NB - DEEP + 1 - NB % DEEP, DEEP) as n:
                for i in range(DEEP):
                    y_out(n + i, i)
            for n in range(NB - NB % DEEP, NB + 3):
                y_out(n, n % DEEP)
            base, per = ch.k, 3
            n0 = NB + 3
            with dve.Fori(0, TG - RING // 2 + 1, RING // 2) as t:
                ch.start(base + per * t)
                for i in range(RING // 2):
                    y_out(t + n0 + i, (n0 + i) % DEEP)
                    combine(t + i, i)
                assert ch.k == per * RING // 2
            ch.start(0, base + per * TG)
            for n in range(n0 + TG, GR * NB):
                y_out(n, n % DEEP)
            layer_norm(3, 4, slice(0, TG))
            dve.wait_ge(s["pool_setup"], 2 + TPB)

            def c_iter(c, last=True, now=True, nxt=True):
                if now:
                    dve.wait_ge(s["c_s"], c + 1)
                    ch.link(dve.tensor_tensor(s1[:, :, :], bank[2][:, 0:TPB * S].rearrange("p (t s) -> p t s", t=TPB),
                                              cell[:, bass.ds(TPB * c, TPB), :], ALU.add))
                    ch.link(dve.tensor_reduce(nm1[:, :], s1[:, :, :], AX.X, ALU.max, negate=True))
                    dve.tensor_tensor(s1[:, :, :], s1[:, :, :], nm1[:, :].unsqueeze(2).broadcast_to([P, TPB, S]), ALU.add)\
                        .then_inc(s["c_sub"], 1)
                if nxt:
                    dve.wait_ge(s["c_tz"], c + 1)
                    normalize(3, TPB * (c + 1), TPB, "c_z")
                if last:
                    dve.wait_ge(s["c_o"], c)
                    xs = x[:, bass.ds(TPB * (c - 1), TPB), :]
                    ch.done(dve.scalar_tensor_tensor(xs, bank[3][:, 0:N].rearrange("p (t d) -> p t d", t=TPB),
                                                     tg[:, 1:2], xs, ALU.mult, ALU.add))
                    tile_stats(TPB * (c - 1), TPB)
                if now:
                    dve.wait_ge(s["c_exp"], c + 1)
                    ch.link(dve.reduce_sum(sum1[:, :], e1[:, :, :], AX.X))
                    ch.link(dve.reciprocal(sum1[:, :], sum1[:, :]))
                    dve.tensor_tensor(p1[:, :, :], e1[:, :, :], sum1[:, :].unsqueeze(2).broadcast_to([P, TPB, S]), ALU.mult)\
                        .then_inc(s["c_p"], 1)

            def combine_batch(c, r):
                for i in range(TPB):
                    combine(TG + TPB * c + i, r + i)

            normalize(3, 0, TPB, "c_z")
            c_iter(0, last=False)
            combine_batch(0, 0)
            base = ch.k
            per_c, per_b = 4 + 2 + 2 * TPB, TPB * per
            with dve.Fori(1, BG - 2, 2) as c:
                ch.start(base + (per_c + per_b) * (c - 1))
                for i in range(2):
                    c_iter(c + i)
                    combine_batch(c + i, (TPB * (1 + i)) % (RING // 2))
                assert ch.k == 2 * (per_c + per_b)
            ch.start(0, base + (per_c + per_b) * (BG - 2))
            combine_batch(BG - 1, (TPB * (BG - 1)) % (RING // 2))
            layer_norm(3, 5, slice(TG, T))
            base = ch.k
            with dve.Fori(BG - 1, B - 1) as c:
                ch.start(base + per_c * (c - BG + 1))
                c_iter(c)
                assert ch.k == per_c
            ch.start(0, base + per_c * (B - BG))
            c_iter(B - 1, nxt=False)
            c_iter(B, now=False, nxt=False)
            dve.drain().then_inc(s["x_done"], 1)
            if phases < 4:
                return

            layer_norm(4, 6)
            for c in range(CHUNKS):
                dve.wait_ge(s["r_tz"], CHUNKS + c)
                normalize(4, CT * c, CT, "r_z")
            dve.wait_ge(s["r_lg"], 2 * CHUNKS)
            ch.link(dve.tensor_copy(lg[:, :, :], bank[2][:, 0:T * E].rearrange("p (t e) -> p t e", e=E)))
            ch.link(dve.tensor_reduce(pick[:, 0, :], lg[:, :, :], AX.X, ALU.max, negate=True))
            dve.tensor_tensor(lg[:, :, :], lg[:, :, :], pick[:, 0, :].unsqueeze(2).broadcast_to([P, T, E]), ALU.add)\
                .then_inc(s["r_d"], 1)
            dve.wait_ge(s["r_exp"], GR + 1)
            ch.link(dve.reduce_sum(pick[:, 0, :], scr[:, :, :], AX.X))
            ch.link(dve.reciprocal(pick[:, 0, :], pick[:, 0, :]))
            dve.tensor_tensor(gate[:, :, :], scr[:, :, :], pick[:, 0, :].unsqueeze(2).broadcast_to([P, T, E]), ALU.mult)\
                .then_inc(s["d_pr"], 1)
            dve.wait_ge(s["d_rows"], 1)
            ch.link(dve.tensor_copy(left[:, 0, :], bank[0][:, 0:N]))
            for i in range(CAP // 8):
                eight = slice(8 * i, 8 * i + 8)
                ch.link(dve.max(best[:, eight], left[:, i % 2, :]))
                ch.done(dve.max_index(best_at[:, eight], best[:, eight], left[:, i % 2, :]))
                ch.link(dve.match_replace(left[:, 1 - i % 2, :], best[:, eight], left[:, i % 2, :], -1.0))
            dve.tensor_copy(best_no[:, :], best_at[:, :]).then_inc(s["d_best"], 1)
            dve.wait_ge(s["d_cols"], 1)
            for h in range(2):
                rows = slice(CAP * h, CAP * h + CAP)
                ch.done(dve.tensor_copy(slots[rows, :, :, :],
                                        bank[1][rows, 0:2 * P].rearrange("p (n b k h) -> p n b k h", n=2, b=B, k=FC)[:, :, :, :, h]))
            link_all()

            def column(n, b, k):
                return slots[:, n, bass.ds(b, 1), k:k + 1].squeeze(1)

            def mark(b, u, free=True):
                if free:
                    dve.wait_ge(s["d_ht"], b - 1)
                for k in range(FC):
                    ins = dve.tensor_scalar(one_hot[:, u, k, :], token_no[:, :], column(0, b, k), None, ALU.is_equal)
                ins.then_inc(s["d_hot"], 1)
                if free:
                    dve.wait_ge(s["d_xg"], b - 1)
                zs = z[:, TPB * u:TPB * u + TPB, :]
                for t in range(TPB):
                    tile = bass.ds(TPB * b + t, 1)
                    ch.done(dve.tensor_scalar(zs[:, t, :], x[:, tile, :].squeeze(1), rstd[:, 1, tile], shift[:, 1, tile],
                                              ALU.mult, ALU.add))
                link_all()
                ch.link(dve.tensor_scalar(z_hi[:, u, :, :], zs, SPLIT, None, ALU.mult))
                dve.scalar_tensor_tensor(z_lo[:, u, :, :], zs, SPLIT, z_hi[:, u, :, :], ALU.mult, ALU.subtract)\
                    .then_inc(s["d_z"], 1)

            def gate_slots(b):
                if b >= 2:
                    dve.wait_ge(s["d_out0"], b - 1)
                for k in range(FC):
                    ins = dve.tensor_scalar(gated[:, b % 2, k, :], token_no[:, :], column(0, b, k), column(1, b, k),
                                            ALU.is_equal, ALU.mult)
                ins.then_inc(s["d_gated"], 1)

            def keep_outputs(half, e):
                dve.wait_ge(s["d_y"], E * half + e + 1)
                dve.tensor_copy(yt[half][:, :, e, :], bank[2 + e % 2][:, :].rearrange("p (b s) -> p b s", b=HB))\
                    .then_inc(s["d_yt"], 1)

            def add_outputs(b):
                dve.wait_ge(s["d_out0"], b + 1)
                if b > 0:
                    dve.wait_ge(s["d_out"], b)
                ch.link(dve.tensor_copy(o16[:, :, :], bank[1][:, 0:N].rearrange("p (t d) -> p t d", t=TPB)))
                dve.sem_inc(s["d_o"], 1)
                xs = x[:, TPB * b:TPB * b + TPB, :]
                dve.scalar_tensor_tensor(xs, o16[:, :, :], tg[:, 3:4], xs, ALU.mult, ALU.add).then_inc(s["d_out"], 1)

            mark(0, 0, free=False)
            mark(1, 1, free=False)
            base, per = ch.k, TPB + 1
            with dve.Fori(2, HB - 1, 2) as b:
                ch.start(base + per * (b - 2))
                mark(b, 0)
                mark(b + 1, 1)
                assert ch.k == 2 * per
            ch.start(0, base + per * (HB - 2))
            mark(HB, 0)
            for e in range(E):
                if e + 1 < E:
                    mark(HB + e + 1, (e + 1) % 2)
                keep_outputs(0, e)
            gate_slots(0)
            for e in range(E):
                gate_slots(e + 1)
                keep_outputs(1, e)
                add_outputs(e)
            for b in range(HB, B):
                if b + 1 < B:
                    gate_slots(b + 1)
                add_outputs(b)


def bcast_rows(src):
    n = src.shape[0]
    return src.rearrange("(a n) -> a n", a=1).broadcast_to([P, n])


_OUT = (B * N, D)


def kernel(**inputs):
    import numpy as np
    import concourse.bacc as bacc
    from concourse.bass_utils import run_bass_kernel_spmd

    g = {k: np.asarray(v) for k, v in inputs.items()}
    flat = np.ascontiguousarray
    mask = g["mask_BxS2_bk0"].view(np.uint8)
    pair = np.arange(H)[:, None, None] == 2 * np.arange(PAIRS)[None, :, None] + (np.arange(P) // S)[None, None, :]
    arrays = {
        "x": flat(g["x"].reshape(B * N, D)),
        "ctx_t": flat(g["ctx_1024"].transpose(2, 0, 1)),
        "mask_t": flat(np.concatenate([mask.T, mask.T])).view(np.uint32),
        "mask_row": flat(mask.reshape(1, B * S)).view(np.uint32),
        "cell": flat(g["mask_BxSxS2_ff1"].reshape(B * N, S)),
        "seq": flat(g["mask_BxS2_ff1"].reshape(B * S)),
        "g_xattn": flat(g["g_xattn"]),
        "g_ffn": flat(g["g_ffn"]),
        "q_w": flat(g["L0_xattn_q_w"]),
        "q_b": flat(g["L0_xattn_q_b"]),
        "kv_w": flat(g["L0_xattn_kv_w"]),
        "kv_b": flat(g["L0_xattn_kv_b"]),
        "proj_w": flat(g["L0_xattn_proj_w"]),
        "proj_b": flat(g["L0_xattn_proj_b"]),
        "wk_t": flat(g["L1_xattn_W_k"].T),
        "b_k": flat(g["L1_xattn_b_k"]),
        "wo_t": flat(g["L1_xattn_W_o"].T),
        "b_o": flat(g["L1_xattn_b_o"]),
        "route": flat(np.stack([g["L0_ffn_Wg"].T, g["L1_ffn_gate_w"]], axis=1)),
        "w0": flat(np.concatenate([
            g["L0_ffn_W1"], g["L0_ffn_W2"].reshape(E, FC, P, D).transpose(0, 2, 1, 3).reshape(E, P, F),
        ], axis=2)),
        "w_up1": flat(g["L1_ffn_w1"].transpose(1, 0, 2)),
        "w_down1": flat(g["L1_ffn_w2"].reshape(E, FC, P, D).transpose(2, 0, 1, 3)),
        "ident": np.eye(P, dtype=np.float32),
        "head_rows": ((np.arange(P) // DH)[:, None] == np.arange(H)).astype(np.float32),
        "head_pick": pair.astype(np.float32),
        "token_no": np.tile(np.arange(N, dtype=np.float32), (P, 1)),
        "before": np.triu(np.ones((P, P), np.float32), 1),
        "block_start": np.arange(NB, dtype=np.float32)[None] * SW,
        "lanes": np.tile(np.arange(E, dtype=np.float32), (P, 1)),
    }
    nc = bacc.Bacc("TRN2", target_bir_lowering=False, num_devices=1)
    aps = {}
    for name, v in arrays.items():
        aps[name] = nc.dram_tensor(f"in_{name}", v.shape, mybir.dt.from_np(v.dtype), kind="ExternalInput").ap()
    out = nc.dram_tensor("out", _OUT, F32, kind="ExternalOutput").ap()
    build(nc, aps, out, PHASES)
    r = run_bass_kernel_spmd(nc, [{f"in_{k}": v for k, v in arrays.items()}], core_ids=[0])
    return r.results[0]["out"].reshape(B, N, D)


PHASES = 4
```

```python
from contextlib import ExitStack

import concourse.bass as bass
from concourse import mybir

F32 = mybir.dt.float32
BF16 = mybir.dt.bfloat16
F16 = mybir.dt.float16
U8 = mybir.dt.uint8
U32 = mybir.dt.uint32
I32 = mybir.dt.int32
ALU = mybir.AluOpType
ACT = mybir.ActivationFunctionType
AX = mybir.AxisListType

P = 128
B, N, D = 16, 256, 128
S = 64
H, DH = 16, 8
E, F = 8, 512
FC = F // P
TPB = N // P
T = B * TPB
PAIRS = H // 2
GROUPS = 4
HPG = H // GROUPS
X_LOADS = 8
CT = 4
CHUNKS = T // CT
CW = CT * P
GR = 2
TG = T // GR
CG = TG // CT
BG = B // GR
FIRST = BG + 2
SW = 256
NB = 2 * TG * P // SW + E - 1
ROWS = NB * SW
DEEP = 4
RING = 8
CAP = 2 * N // E
HB = B // 2
SCALE = float(DH) ** -0.5
EPS = 1e-5
MASKED = -1e30
LEAST = 1e-18
SPLIT = 4096.0


def wait(engine, sem, value):
    if isinstance(value, int) and value <= 0:
        return
    engine.wait_ge(sem, value)


def hold(engine, sem, value, held):
    if isinstance(value, int) and value <= 0:
        return
    engine.wait_ge(sem, value)
    engine.sem_inc(held, 1)


class Chain:

    def __init__(self, engine, sem):
        self.engine, self.sem, self.base, self.k = engine, sem, 0, 0

    def start(self, base, k=0):
        self.base, self.k = base, k

    def done(self, instruction):
        self.k += 1
        return instruction.then_inc(self.sem, 1)

    def link(self, instruction):
        self.done(instruction)
        self.engine.wait_ge(self.sem, self.base + self.k)


def build(nc, a, out):
    with ExitStack() as ctx:
        def sb(name, shape, dt=F32):
            return ctx.enter_context(nc.sbuf_tensor(name, shape, dt))

        def sem(name):
            return ctx.enter_context(nc.semaphore(name))

        x = sb("x", [P, T, D])
        mean_var = sb("mean_var", [P, T, 2])
        rstd = sb("rstd", [P, 2, T])
        shift = sb("shift", [P, 2, T])
        ident = sb("ident", [P, P])
        head_rows = sb("head_rows", [P, H])
        head_pick = sb("head_pick", [H, PAIRS, P])
        head_pick16 = sb("head_pick16", [H, PAIRS, P], BF16)
        token_no = sb("token_no", [P, N])
        ident16 = sb("ident16", [P, P], F16)
        lanes = sb("lanes", [P, E])
        before = sb("before", [P, P])
        before16 = sb("before16", [P, P], BF16)
        all16 = sb("all16", [P, P], BF16)
        block_start = sb("block_start", [1, NB])
        ones = sb("ones", [1, P])
        ones16 = sb("ones16", [1, P], BF16)
        eps = sb("eps", [P, 1])
        gates = sb("gates", [P, 4])
        tg = sb("tg", [P, 4])
        q_w = sb("q_w", [P, D])
        kv_w = sb("kv_w", [P, 2 * D])
        proj_w = sb("proj_w", [P, D])
        wk_t = sb("wk_t", [P, D])
        wo_t = sb("wo_t", [P, D])
        route = sb("route", [P, 2, E])
        q_b = sb("q_b", [P, 1])
        q_bs = sb("q_bs", [P, 1])
        k_b = sb("k_b", [P, 1])
        bk1 = sb("bk1", [P, 1])
        v_b = sb("v_b", [P, D])
        proj_b = sb("proj_b", [1, D])
        bo1 = sb("bo1", [P, D])
        w_up1 = sb("w_up1", [P, E, F])
        w_down1 = sb("w_down1", [P, E, FC, D])
        mask4 = sb("mask4", [P, B // 4], U32)
        key_bias = sb("key_bias", [P, B])
        mask_row4 = sb("mask_row4", [1, B * S // 4], U32)
        key_row = sb("key_row", [1, B, S], BF16)
        vals0 = sb("vals0", [P, B, PAIRS, 2 * (DH + 1)])
        z = sb("z", [P, CT, D])
        zt = sb("zt", [P, N])
        q = sb("q", [P, 2, N])
        neg_max = sb("neg_max", [P, TPB, H])
        nmt = sb("nmt", [H, N], BF16)
        inv = sb("inv", [P, TPB, H])
        on = sb("on", [P, TPB, D])
        ot = sb("ot", [P, N])
        stats = sb("stats", [P, CT, 6])
        mv = sb("mv", [P, CT, 2])
        k1 = sb("k1", [P, B, S])
        v1 = sb("v1", [S, B, D])
        nm1 = sb("nm1", [P, 2, TPB])
        e1 = sb("e1", [P, 2, TPB, S])
        sum1 = sb("sum1", [P, 2, TPB])
        inv1 = sb("inv1", [P, 2, TPB])
        pt1 = sb("pt1", [S, N])
        lg = sb("lg", [P, T, E])
        gate = sb("gate", [P, T, E])
        top8 = sb("top8", [P, T, 8])
        idx8 = sb("idx8", [P, T, 8], mybir.dt.uint32)
        pick = sb("pick", [P, 2, T])
        hot0 = sb("hot0", [P, T, E])
        hot1 = sb("hot1", [P, T, E])
        hot16 = sb("hot16", [P, T, E], BF16)
        tot = sb("tot", [P, E, TG])
        cum = sb("cum", [P, E, TG])
        ranks = sb("ranks", [P, TG, E])
        cnt = sb("cnt", [P, 4, E])
        cnt_i = sb("cnt_i", [P, 2, E], I32)
        zero_e = sb("zero_e", [P, E * TG])
        posf = sb("posf", [P, 2, T])
        pos = sb("pos", [P, 2, T], U32)
        starts = sb("starts", [1, NB, E])
        expertf = sb("expertf", [1, NB])
        expert = sb("expert", [1, GR * NB], U32)
        part = sb("part", [P, 2, T])
        scr = sb("scr", [P, T, E])
        left = sb("left", [P, 2, N])
        best = sb("best", [P, CAP])
        best_at = sb("best_at", [P, CAP], U32)
        best_no = sb("best_no", [P, CAP])
        slots = sb("slots", [P, 2, B, FC])
        o16 = sb("o16", [P, TPB, D], BF16)

        area_k = sb("area_k", [P, 4096])
        area_h = sb("area_h", [P, 4096])
        area_z = sb("area_z", [P, 4096])
        area_m = sb("area_m", [P, 3072])
        area_w = sb("area_w", [P, 8192])
        k0 = area_k[:, 0:B * S].rearrange("p (b s) -> p b s", b=B)
        k0s = area_k[:, B * S:B * S + 2 * H * S].rearrange("p (u h s) -> p u h s", u=2, h=H)
        seq_zero = area_k[:, 3072:4096].rearrange("p (b s) -> p b s", s=S)
        wb = area_w[:, 0:4096].rearrange("p (r w) -> p r w", r=DEEP)
        x_row = area_w[:, 4096:5120].rearrange("p (r t d) -> p r t d", r=DEEP, d=D)
        y_row = area_w[:, 5120:6144].rearrange("p (r t d) -> p r t d", r=DEEP, d=D)
        xt = area_w[:, 6144:6656].rearrange("p (u n) -> p u n", u=2)
        k16 = area_w[:, 6656:7680].bitcast(F16).rearrange("p (u h s) -> p u h s", u=2, h=H)
        q16 = area_w[:, 7680:7936].bitcast(F16).rearrange("p (u n) -> p u n", u=2)
        one_hot = area_w[:, 4096:5120].bitcast(F16).rearrange("p (u k n) -> p u k n", u=2, k=FC)
        sel = area_w[:, 5120:6144].bitcast(F16).rearrange("p (u j m) -> p u j m", u=2, j=TPB)
        gated = area_w[:, 6144:8192].rearrange("p (u k n) -> p u k n", u=2, k=FC)
        yg = area_k[:, 3072:4096].rearrange("p (r d) -> p r d", d=D)
        taken = [area[:, 0:4096].rearrange("p (e b s) -> p e b s", e=E, s=CAP) for area in (area_k, area_w)]
        ctx_t = area_h[:, 0:B * S].rearrange("p (b s) -> p b s", b=B)
        pt0 = area_h[:, :].rearrange("p (u h n) -> p u h n", u=2, h=PAIRS)
        hid = area_h[:, :].rearrange("p (u f n) -> p u f n", u=2, f=FC)
        hid0 = area_h[:, 0:2 * FC * SW].rearrange("p (u f n) -> p u f n", u=2, f=FC)
        zt2 = [area_w[:, o:o + 2 * CW].rearrange("p (u n) -> p u n", u=2) for o in (0, 6656)]
        zt2d = area_h[:, 0:2 * CW].rearrange("p (u n) -> p u n", u=2)
        cell_zero = area_z[:, 2048:4096].rearrange("p (t s) -> p t s", s=S)
        z_all = area_z[:, :].rearrange("p (t d) -> p t d", d=D)
        yt = [area[:, :].rearrange("p (b e s) -> p b e s", b=HB, e=E) for area in (area_z, area_k)]
        cell = area_m[:, 0:T * S].rearrange("p (t s) -> p t s", s=S)
        seq = area_m[:, T * S:T * S + B * S].rearrange("p (b s) -> p b s", s=S)
        z_hi, z_lo = (area_m[:, 256 * k:256 * (k + 1)].bitcast(F16).rearrange("p (u j d) -> p u j d", u=2, j=TPB)
                      for k in range(2))
        y_slots = area_m[:, 512:1536].rearrange("p (u k d) -> p u k d", u=2, k=FC)

        bank = [ctx.enter_context(nc.psum_tensor(f"bank{i}", [P, 512], F32)) for i in range(4)]
        big = [ctx.enter_context(nc.psum_tensor(f"big{i}", [P, 1024], F32)) for i in range(2)]

        names = """ld_const ld_ctx ld_kv ld_w ld_keys ld_mask ld_e1 ld_r stored
            pe_setup act_setup dve_setup pool_setup masks_ready
            a_keys16 a_keys a_z a_tz a_zt a_qm a_q16 a_q a_s a_max a_tm a_mt a_p2 a_exp a_av a_on a_to a_ot a_pj a_read
            ln_sqrt x_done dve pool held_dve held_act held_pe
            r_z r_tz r_zt r_lg r_d r_exp
            b_hot b_rank b_read b_pos xs_clear b_sc0 b_sc1 b_tx b_xt b_up b_act b_y b_yr b_add
            c_z c_tz c_zt c_s c_max c_exp c_tp c_pt c_o c_read
            d_pr d_rows d_best d_cols d_z d_hot d_ht d_sel d_xg d_xge
            d_up d_act d_y d_yt d_gated d_ty d_ys d_out0 d_o d_out""".split()
        s = {n: sem(n) for n in names}

        def load(eng, which, dst, src):
            eng.dma_start(dst, src).then_inc(s[which], 16)

        ld_x = [sem(f"ld_x{i}") for i in range(X_LOADS)]
        gathered = [sem(f"b_gat{i}") for i in range(RING)]
        got_x, got_w, kept = ([sem(f"{k}{i}") for i in range(DEEP)] for k in ("b_ld_x", "b_ld_w", "b_st"))

        def nth(n, r):
            return 16 // DEEP * (n - r) + 16

        slots_in = [nc.dram_tensor(f"slots_in{g}", (ROWS, D), F32, kind="Internal").ap() for g in range(GR)]
        slots_out = [nc.dram_tensor(f"slots_out{g}", (ROWS, D), F32, kind="Internal").ap() for g in range(GR)]

        def block_rows(tables, g, n):
            rows = tables[g].rearrange("(n t p) d -> p n t d", p=P, t=SW // P)
            return rows[:, bass.ds(n - NB * g, 1), :, :].squeeze(1)

        LOADS = {"ld_const": 7, "ld_ctx": 1, "ld_kv": 5, "ld_w": 7, "ld_keys": 2, "ld_mask": 2, "ld_e1": 2, "ld_r": 2}

        def loaded(eng, which):
            eng.wait_ge(s[which], 16 * LOADS[which])

        block = ctx.enter_context(nc.Block())

        @block.sync
        def _(sp):
            load(sp, "ld_ctx", ctx_t, a["ctx_t"])
            load(sp, "ld_kv", kv_w[:, :], a["kv_w"])
            x_in = a["x"].rearrange("(t p) d -> p t d", p=P)
            for i in range(X_LOADS):
                tiles = slice(T // X_LOADS * i, T // X_LOADS * (i + 1))
                sp.dma_start(x[:, tiles, :], x_in[:, tiles, :]).then_inc(ld_x[i], 16)
            load(sp, "ld_kv", k_b[:, :], a["kv_b"][0:D].rearrange("(p a) -> p a", a=1))
            load(sp, "ld_kv", v_b[:, :], bcast_rows(a["kv_b"][D:2 * D]))
            load(sp, "ld_kv", wk_t[:, :], a["wk_t"])
            load(sp, "ld_kv", wo_t[:, :], a["wo_t"])
            load(sp, "ld_const", ident[:, :], a["ident"])
            load(sp, "ld_const", head_rows[:, :], a["head_rows"])
            load(sp, "ld_const", head_pick[:, :, :], a["head_pick"])
            load(sp, "ld_const", token_no[:, :], a["token_no"])
            load(sp, "ld_const", lanes[:, :], a["lanes"])
            load(sp, "ld_const", before[:, :], a["before"])
            load(sp, "ld_const", block_start[:, :], a["block_start"])
            load(sp, "ld_keys", mask4[:, :], a["mask_t"])
            load(sp, "ld_keys", mask_row4[:, :], a["mask_row"])
            load(sp, "ld_mask", cell, a["cell"].rearrange("(t p) s -> p t s", p=P))
            load(sp, "ld_mask", area_m[:, T * S:T * S + B * S], bcast_rows(a["seq"]))
            load(sp, "ld_w", q_w[:, :], a["q_w"])
            load(sp, "ld_w", q_b[:, :], a["q_b"].rearrange("(p a) -> p a", a=1))
            load(sp, "ld_w", proj_w[:, :], a["proj_w"])
            load(sp, "ld_w", proj_b[:, :], a["proj_b"].rearrange("(a d) -> a d", a=1))
            load(sp, "ld_w", gates[:, 0:2], bcast_rows(a["g_xattn"]))
            load(sp, "ld_w", gates[:, 2:4], bcast_rows(a["g_ffn"]))
            load(sp, "ld_w", bk1[:, :], a["b_k"].rearrange("(p a) -> p a", a=1))
            load(sp, "ld_r", bo1[:, :], bcast_rows(a["b_o"]))
            load(sp, "ld_r", route[:, :, :], a["route"])
            load(sp, "ld_e1", w_up1[:, :, :], a["w_up1"])
            load(sp, "ld_e1", w_down1[:, :, :], a["w_down1"])
            sp.wait_ge(s["pool_setup"], 1)
            for rows in slots_in:
                sp.dma_start(rows.rearrange("(p r) d -> p r d", p=P),
                             zero_e[:, 0:D].unsqueeze(1).broadcast_to([P, ROWS // P, D])).then_inc(s["xs_clear"], 16)
            sp.wait_ge(s["b_pos"], 1)
            def block_load(g, n, r, store_g=None):
                e = sp.value_load(expert[0:1, bass.ds(n, 1)], min_val=0, max_val=E - 1)
                if store_g is not None:
                    sp.wait_ge(s["b_y"], n - DEEP + 1)
                sp.dma_start(wb[:, r, :], a["w0"][bass.ds(e, 1), :, :].squeeze(0)).then_inc(got_w[r], 16)
                sp.dma_start(x_row[:, r, :, :], block_rows(slots_in, g, n)).then_inc(got_x[r], 16)
                if store_g is not None:
                    block_store(store_g, n - DEEP, r)

            def block_store(g, n, r):
                sp.wait_ge(s["b_yr"], n + 1)
                sp.dma_start(block_rows(slots_out, g, n), y_row[:, r, :, :]).then_inc(kept[r], 16)

            sp.wait_ge(s["b_sc0"], 16 * 2 * TG)
            for n in range(DEEP):
                block_load(0, n, n)
            with sp.Fori(DEEP, NB - DEEP + 1 - NB % DEEP, DEEP) as n:
                for i in range(DEEP):
                    block_load(0, n + i, i, store_g=0)
            for n in range(NB - NB % DEEP, NB):
                block_load(0, n, n % DEEP, store_g=0)
            sp.wait_ge(s["b_pos"], 2)
            sp.wait_ge(s["b_sc1"], 16 * 2 * TG)
            for n in range(NB, NB + DEEP):
                block_load(1, n, n % DEEP, store_g=0)
            rest = (NB - DEEP) % DEEP
            with sp.Fori(NB + DEEP, 2 * NB - rest - DEEP + 1, DEEP) as n:
                for i in range(DEEP):
                    block_load(1, n + i, (NB + i) % DEEP, store_g=1)
            for n in range(2 * NB - rest, 2 * NB):
                block_load(1, n, n % DEEP, store_g=1)
            for n in range(2 * NB - DEEP, 2 * NB):
                block_store(1, n, n % DEEP)
            x_out = out.rearrange("(t p) d -> p t d", p=P)
            for b in range(B):
                sp.wait_ge(s["d_out"], b + 1)
                sp.dma_start(x_out[:, TPB * b:TPB * b + TPB, :], x[:, TPB * b:TPB * b + TPB, :]).then_inc(s["stored"], 16)
            sp.wait_ge(s["stored"], 16 * B)

        @block.gpsimd
        def _(pool):
            ch = Chain(pool, s["pool"])
            ch.done(pool.memset(ones[:, :], 1.0))
            ch.done(pool.memset(ones16[:, :], 1.0))
            ch.done(pool.memset(eps[:, :], EPS))
            ch.done(pool.memset(all16[:, :], 1.0))
            ch.done(pool.memset(zero_e[:, :], 0.0))
            ch.link(pool.memset(vals0[:, :, :, :], 0.0))
            ch.done(pool.memset(vals0[0:S, :, :, DH:DH + 1], 1.0))
            pool.memset(vals0[S:P, :, :, 2 * DH + 1:2 * DH + 2], 1.0).then_inc(s["pool_setup"], 1)

            def keys(c, u):
                if not isinstance(c, int) or c >= 2:
                    pool.wait_ge(s["a_p2"], 2 * c - 2)
                for dst, done in ((k16, "a_keys16"), (k0s, "a_keys")):
                    pool.tensor_tensor(dst[:, u, :, :], k0[:, bass.ds(c, 1), :].broadcast_to([P, H, S]),
                                       head_rows[:, :].unsqueeze(2).broadcast_to([P, H, S]), ALU.mult).then_inc(s[done], 1)

            def scatter(g, tiles):
                pool.wait_ge(s["b_pos"], g + 1)
                for t in tiles:
                    for k in range(2):
                        pool.indirect_dma_start(out=slots_in[g], out_offset=bass.IndirectOffsetOnAxis(ap=pos[:, k, t:t + 1], axis=0),
                                                in_=z_all[:, t, :], in_offset=None).then_inc(s[f"b_sc{g}"], 16)

            pool.wait_ge(s["pool_setup"], 1)
            pool.wait_ge(s["dve_setup"], 4)
            keys(0, 0)
            keys(1, 1)
            pool.wait_ge(s["a_keys"], 2)
            loaded(pool, "ld_mask")
            ch.done(pool.tensor_scalar(cell_zero, cell, 0.0, MASKED, ALU.is_le, ALU.mult))
            ch.link(pool.tensor_scalar(seq_zero, seq, 0.0, MASKED, ALU.is_le, ALU.mult))
            ch.done(pool.tensor_scalar(cell, cell, LEAST, None, ALU.max))
            pool.tensor_scalar(seq, seq, LEAST, None, ALU.max).then_inc(s["pool_setup"], 1)

            pool.wait_ge(s["pool_setup"], 2)
            with pool.Fori(2, FIRST - 1, 2) as c:
                keys(c, 0)
                keys(c + 1, 1)
            keys(FIRST, 0)
            keys(FIRST + 1, 1)
            pool.wait_ge(s["xs_clear"], 16 * GR)
            scatter(0, range(0, TG // 2))
            keys(FIRST + 2, 0)
            scatter(0, range(TG // 2, TG))
            keys(FIRST + 3, 1)
            for c in range(FIRST + 4, B):
                keys(c, c % 2)
            pool.wait_ge(s["a_keys"], B)
            pool.wait_ge(s["masks_ready"], 2)
            ch.done(pool.tensor_tensor(cell, cell, cell_zero, ALU.add))
            ch.link(pool.tensor_tensor(seq, seq, seq_zero, ALU.add))
            cell_b = cell.rearrange("p (b t) s -> p b t s", t=TPB)
            for t in range(TPB):
                pool.wait_ge(s["pool"], ch.k)
                pool.tensor_tensor(cell_b[:, :, t, :], cell_b[:, :, t, :], seq, ALU.add).then_inc(s["pool_setup"], 1)
            scatter(1, range(TG, T))
            for g in range(GR):
                for n in range(NB * (g + 1) - DEEP, NB * (g + 1)):
                    pool.wait_ge(kept[n % DEEP], nth(n, n % DEEP))
                for m in range(2 * TG * g, 2 * TG * (g + 1)):
                    k, t = m % 4 // 2, m // 4 * 2 + m % 2
                    if m >= RING:
                        pool.wait_ge(s["b_add"], m - RING + 1)
                    pool.indirect_dma_start(out=yg[:, m % RING, :], out_offset=None, in_=slots_out[g],
                                            in_offset=bass.IndirectOffsetOnAxis(ap=pos[:, k, t:t + 1], axis=0))\
                        .then_inc(gathered[m % RING], 16)

        @block.scalar
        def _(act):
            act.preload_act_table(ACT.Exp)
            act.wait_ge(s["ld_w"], 16 * LOADS["ld_w"])
            act.activation(tg[:, :], gates[:, :], ACT.Tanh)
            act.activation(q_bs[:, :], q_b[:, :], ACT.Copy, scale=SCALE).then_inc(s["act_setup"], 1)

            def layer_rstd(n, i, tiles=slice(0, T)):
                act.wait_ge(s["ln_sqrt"], i)
                act.activation(rstd[:, 1 - n % 2, tiles], mean_var[:, tiles, 1], ACT.Sqrt, bias=eps[:, 0:1])\
                    .then_inc(s["act_setup"], 1)

            act.wait_ge(s["pool_setup"], 1)
            layer_rstd(1, 1)
            act.preload_act_table(ACT.Exp)

            def evac_zt(c):
                wait(act, s["a_tz"], c + 1)
                act.activation(zt[:, :], bank[0][:, 0:N], ACT.Copy).then_inc(s["a_zt"], 1)

            def evac_q(c, u):
                wait(act, s["a_qm"], c + 1)
                for dst, done in ((q16, "a_q16"), (q, "a_q")):
                    act.activation(dst[:, u, :], bank[1][:, 0:N], ACT.Identity, bias=q_bs[:, 0:1], scale=SCALE)\
                        .then_inc(s[done], 1)

            def exps(c, u, h):
                hold(act, s["a_p2"], 2 * c + h + 1, s["held_act"])
                act.activation(area_h[:, (2 * u + h) * 1024:(2 * u + h + 1) * 1024], big[h][:, :], ACT.Exp,
                               bias=key_bias[:, bass.ds(c, 1)]).then_inc(s["a_exp"], 1)

            def a_iter(c, u, now=True, last=True, nxt=True):
                if nxt:
                    evac_zt(c + 1)
                    evac_q(c + 1, 1 - u)
                if now:
                    wait(act, s["a_tm"], c + 1)
                    act.activation(nmt[:, :], bank[0][0:H, 0:N], ACT.Copy).then_inc(s["a_mt"], 1)
                    exps(c, u, 0)
                    exps(c, u, 1)
                if last:
                    wait(act, s["a_to"], c)
                    act.activation(ot[:, :], bank[0][:, 0:N], ACT.Copy).then_inc(s["a_ot"], 1)

            evac_zt(0)
            evac_q(0, 0)
            act.wait_ge(s["dve_setup"], 2)
            a_iter(0, 0, last=False)
            a_iter(1, 1)
            with act.Fori(2, FIRST - 1, 2) as c:
                a_iter(c, 0)
                a_iter(c + 1, 1)

            def route_evac(chunks, dst):
                for c in chunks:
                    act.wait_ge(s["r_tz"], c + 1)
                    if c - chunks[0] >= 2:
                        act.wait_ge(s["r_lg"], c - 1)
                    act.activation(dst[:, c % 2, :], bank[c % 2][:, :], ACT.Copy).then_inc(s["r_zt"], 1)

            def route_tanh(g):
                act.wait_ge(s["r_d"], g + 1)
                tiles = slice(TG * g, TG * (g + 1))
                act.activation(part[:, 0, tiles], pick[:, 0, tiles], ACT.Tanh, scale=0.5).then_inc(s["r_exp"], 1)

            layer_rstd(2, 2, slice(0, TG))
            act.preload_act_table(ACT.Exp)
            route_evac(range(0, CG), zt2[0])
            route_tanh(0)
            act.wait_ge(s["pool_setup"], 2)
            act.activation(cell, cell, ACT.Ln).then_inc(s["masks_ready"], 1)
            act.activation(seq, seq, ACT.Ln).then_inc(s["masks_ready"], 1)

            act.preload_act_table(ACT.Exp)

            with act.Fori(FIRST, B - 3, 2) as c:
                a_iter(c, 0)
                a_iter(c + 1, 1)
            a_iter(B - 2, 0)
            a_iter(B - 1, 1, nxt=False)
            a_iter(B, 0, now=False, nxt=False)

            def hidden(n, u, func, done):
                for f in range(FC):
                    act.wait_ge(s[done[0]], FC * n + f + 1)
                    src = big[f // 2][:, (f % 2) * CW:(f % 2 + 1) * CW]
                    act.activation(hid[:, u, f, :], src, func).then_inc(s[done[1]], 1)

            def b_xt(n, u):
                act.wait_ge(s["b_tx"], n + 1)
                act.activation(xt[:, u, :], bank[0][:, 0:SW], ACT.Copy).then_inc(s["b_xt"], 1)

            def b_hidden(n, u):
                act.wait_ge(s["b_up"], n + 1)
                act.activation(hid0[:, u, :, :], big[u][:, :].rearrange("p (f n) -> p f n", f=FC), ACT.Silu)\
                    .then_inc(s["b_act"], 1)

            b_xt(0, 0)
            b_xt(1, 1)
            layer_rstd(2, 3, slice(TG, T))
            act.preload_act_table(ACT.Silu)
            b_hidden(0, 0)
            route_evac(range(CG, 2 * CG), zt2[1])
            route_tanh(1)
            with act.Fori(0, GR * NB - 2, 2) as n:
                b_hidden(n + 1, 1)
                b_xt(n + 2, 0)
                b_hidden(n + 2, 0)
                b_xt(n + 3, 1)
            b_hidden(GR * NB - 1, 1)
            layer_rstd(3, 4, slice(0, TG))
            act.preload_act_table(ACT.Exp)

            def c_zt(c, u):
                act.wait_ge(s["c_tz"], c + 1)
                act.activation(q[:, u, :], bank[0][:, 0:N], ACT.Copy).then_inc(s["c_zt"], 1)

            def c_exp(c, u):
                act.wait_ge(s["c_max"], c + 1)
                for t in range(TPB):
                    ins = act.activation(e1[:, u, t, :], big[u][:, t * S:(t + 1) * S], ACT.Exp, bias=nm1[:, u, t:t + 1],
                                         accum_out=sum1[:, u, t:t + 1])
                ins.then_inc(s["c_exp"], 1)

            def c_iter(c, u, ahead=2):
                act.wait_ge(s["c_tp"], c + 1)
                act.activation(pt1[:, :], bank[1][0:S, 0:N], ACT.Copy).then_inc(s["c_pt"], 1)
                if ahead >= 1:
                    c_exp(c + 1, 1 - u)
                if ahead >= 2:
                    c_zt(c + 2, u)

            c_zt(0, 0)
            c_zt(1, 1)
            c_exp(0, 0)
            c_iter(0, 0)
            with act.Fori(1, BG - 4, 2) as c:
                c_iter(c, 1)
                c_iter(c + 1, 0)
            c_iter(BG - 3, 1)
            layer_rstd(3, 5, slice(TG, T))
            act.preload_act_table(ACT.Exp)
            c_iter(BG - 2, 0)
            with act.Fori(BG - 1, B - 4, 2) as c:
                c_iter(c, 1)
                c_iter(c + 1, 0)
            c_iter(B - 3, 1)
            c_iter(B - 2, 0, ahead=1)
            c_iter(B - 1, 1, ahead=0)
            layer_rstd(4, 6)
            act.preload_act_table(ACT.Exp)
            route_evac(range(CHUNKS, 2 * CHUNKS), zt2d)
            act.wait_ge(s["r_d"], GR + 1)
            act.activation(scr[:, :, :], lg[:, :, :], ACT.Exp).then_inc(s["r_exp"], 1)
            act.preload_act_table(ACT.Gelu_apprx_tanh)

            def select(b, u, free=True):
                act.wait_ge(s["d_ht"], b + 1)
                if free:
                    act.wait_ge(s["d_xg"], b - 1)
                act.activation(sel[:, u, :, :], bank[0][:, :].bitcast(F16).rearrange("p (j m) -> p j m", j=TPB), ACT.Copy)\
                    .then_inc(s["d_sel"], 1)

            def take(half, i):
                act.wait_ge(s["d_xg"], HB * half + i + 1)
                act.activation(taken[half][:, :, bass.ds(i, 1), :].squeeze(2),
                               bank[1][:, :].rearrange("p (e s) -> p e s", e=E), ACT.Copy, scale=1.0 / SPLIT)\
                    .then_inc(s["d_xge"], 1)

            def experts(half, e):
                hidden(E * half + e, e % 2, ACT.Gelu_apprx_tanh, ("d_up", "d_act"))

            def slots_down(b):
                act.wait_ge(s["d_ty"], b + 1)
                if b >= 2:
                    act.wait_ge(s["d_out0"], b - 1)
                act.activation(y_slots[:, b % 2, :, :], bank[0][:, :].rearrange("p (k d) -> p k d", k=FC), ACT.Copy)\
                    .then_inc(s["d_ys"], 1)

            select(0, 0, False)
            select(1, 1, False)
            take(0, 0)
            with act.Fori(2, HB - 1, 2) as b:
                select(b, 0)
                take(0, b - 1)
                select(b + 1, 1)
                take(0, b)
            take(0, HB - 1)
            experts(0, 0)
            for e in range(E):
                if e + 1 < E:
                    experts(0, e + 1)
                select(HB + e, e % 2)
                take(1, e)
            experts(1, 0)
            for e in range(E):
                if e + 1 < E:
                    experts(1, e + 1)
                slots_down(e)
            for b in range(HB, B):
                slots_down(b)

        @block.tensor
        def _(pe):
            mm = pe.matmul
            pe.wait_ge(s["ld_ctx"], 16)
            loaded(pe, "ld_kv")
            for h in range(2):
                mm(bank[h][:, :], kv_w[:, 0:D], ctx_t[:, 8 * h:8 * h + 8, :], start=True, stop=True)\
                    .then_inc(s["pe_setup"], 1)
            for h in range(2):
                mm(bank[2 + h][:, :], wk_t[:, :], ctx_t[:, 8 * h:8 * h + 8, :], start=True, stop=True)\
                    .then_inc(s["pe_setup"], 1)
            for b in range(B):
                for k in range(2):
                    ins = mm(big[b // 8][S * k:S * k + S, (b % 8) * D:(b % 8 + 1) * D], ctx_t[:, b, :], kv_w[:, D:2 * D],
                             start=True, stop=True)
                if b % 8 == 7:
                    ins.then_inc(s["pe_setup"], 1)
            for b in range(B):
                if b % 8 == 0:
                    pe.wait_ge(s["dve_setup"], 5 + b // 8)
                ins = mm(big[b // 8][0:S, (b % 8) * D:(b % 8 + 1) * D], ctx_t[:, b, :], wo_t[:, :], start=True, stop=True)
                if b % 8 == 7:
                    ins.then_inc(s["pe_setup"], 1)

            def transposes(dst, src, n, done, rows=P, cols=P):
                for t in range(n):
                    ins = pe.transpose(dst[0:cols, t * P:(t + 1) * P], src[:, t, :], ident[:, :])
                ins.then_inc(done, 1)

            pe.wait_ge(s["ld_const"], 16 * LOADS["ld_const"])

            def tz(c):
                wait(pe, s["a_z"], c + 1)
                wait(pe, s["a_ot"], c - 2)
                transposes(bank[0], z[:, 0:TPB, :], TPB, s["a_tz"])

            def q_product(c):
                wait(pe, s["a_zt"], c + 1)
                wait(pe, s["a_q"], c)
                mm(bank[1][:, 0:N], q_w[:, :], zt[:, :], start=True, stop=True).then_inc(s["a_qm"], 1)

            def pass1(c, u, t):
                if t == 0:
                    wait(pe, s["a_q16"], c + 1)
                    wait(pe, s["a_keys16"], c + 1)
                wait(pe, s["a_exp"], 2 * c - 1 + t)
                for g in range(GROUPS):
                    dst = big[t][:, g * HPG * S:(g + 1) * HPG * S]
                    mm(dst, q16[:, u, t * P:(t + 1) * P], k16[:, u, HPG * g:HPG * g + HPG, :], start=True, stop=False)
                    ins = mm(dst, ones16[:, :], key_row[:, bass.ds(c, 1), :].broadcast_to([1, HPG, S]),
                             start=False, stop=True)
                ins.then_inc(s["a_s"], 1)

            def values(c, u, parts):
                for place in parts:
                    t, h = divmod(place, PAIRS)
                    w = 2 * (DH + 1)
                    ins = mm(bank[2][:, place * w:(place + 1) * w], pt0[:, u, h, t * P:(t + 1) * P],
                             vals0[:, bass.ds(c, 1), h, :], start=True, stop=True)
                if place == TPB * PAIRS - 1:
                    ins.then_inc(s["a_av"], 1)

            def pass2(c, u, h, parts=None):
                wait(pe, s["a_max"], 2 * c + h + 1)
                wait(pe, s["a_q"], c + 1)
                wait(pe, s["a_keys"], c + 1)
                for k in range(4):
                    pair = 4 * h + k
                    dst = big[h][:, k * N:(k + 1) * N]
                    mm(dst, k0s[:, u, 2 * pair:2 * pair + 2, :], q[:, u, :], start=True, stop=False)
                    ins = mm(dst, head_pick16[:, pair, :], nmt[:, :], start=False, stop=True)
                    if k == 3:
                        ins.then_inc(s["a_p2"], 1)
                    if parts and parts[k] < parts[k + 1]:
                        values(c - 1, 1 - u, range(parts[k], parts[k + 1]))

            def project(c):
                wait(pe, s["a_ot"], c + 1)
                wait(pe, s["a_read"], c + 1)
                for t in range(TPB):
                    dst = bank[3][:, t * P:(t + 1) * P]
                    mm(dst, ot[:, t * P:(t + 1) * P], proj_w[:, :], start=True, stop=False)
                    ins = mm(dst, ones[:, :], proj_b[:, :], start=False, stop=True)
                ins.then_inc(s["a_pj"], 1)

            def a_iter(c, u, now=True, last=True, proj=True, nxt=True):
                if now:
                    pass1(c, u, 0)
                    pass1(c, u, 1)
                if nxt:
                    tz(c + 1)
                if proj:
                    project(c - 2)
                if nxt:
                    q_product(c + 1)
                if now:
                    wait(pe, s["a_max"], 2 * c + 2)
                    wait(pe, s["a_ot"], c - 1)
                    transposes(bank[0], neg_max, TPB, s["a_tm"], cols=H)
                if last:
                    wait(pe, s["a_exp"], 2 * c)
                    values(c - 1, 1 - u, range(0, 7))
                if now:
                    wait(pe, s["a_mt"], c + 1)
                    pass2(c, u, 0, [7, 10, 13, 16, 16] if last else None)
                    pass2(c, u, 1)
                elif last:
                    values(c - 1, 1 - u, range(7, TPB * PAIRS))
                if last:
                    wait(pe, s["a_on"], c)
                    transposes(bank[0], on, TPB, s["a_to"])

            tz(0)
            loaded(pe, "ld_w")
            q_product(0)
            pe.wait_ge(s["dve_setup"], 8)
            a_iter(0, 0, last=False, proj=False)
            a_iter(1, 1, proj=False)
            with pe.Fori(2, FIRST - 1, 2) as c:
                a_iter(c, 0)
                a_iter(c + 1, 1)

            def route_products(chunks, layer, rows, ztr, logits, col):
                def turn(c):
                    pe.wait_ge(s["r_z"], c + 1)
                    if c - chunks[0] >= 2:
                        pe.wait_ge(s["r_zt"], c - 1)
                    transposes(bank[c % 2], rows(c), CT, s["r_tz"])

                turn(chunks[0])
                for c in chunks:
                    if c < chunks[-1]:
                        turn(c + 1)
                    pe.wait_ge(s["r_zt"], c + 1)
                    for t in range(CT):
                        k = col(CT * (c - chunks[0]) + t)
                        ins = mm(logits[:, k:k + E], ztr[:, c % 2, P * t:P * t + P], route[:, layer, :],
                                 start=True, stop=True)
                    ins.then_inc(s["r_lg"], 1)

            def route_group(g):
                route_products(range(CG * g, CG * (g + 1)), 0, lambda c: z_all[:, CT * c:CT * c + CT, :], zt2[g],
                               bank[2 + g], lambda t: E * t)

            def rank_group(g):
                pe.wait_ge(s["b_hot"], g + 1)
                for k, m in enumerate((before16, all16)):
                    ins = mm(bank[1][:, k * TG * E:(k + 1) * TG * E], m[:, :], hot16[:, TG * g:TG * (g + 1), :],
                             start=True, stop=True)
                ins.then_inc(s["b_rank"], 1)

            loaded(pe, "ld_r")
            pe.wait_ge(s["a_ot"], FIRST - 1)
            pe.wait_ge(s["a_q"], FIRST + 1)
            route_group(0)
            rank_group(0)
            pe.wait_ge(s["b_read"], 1)
            with pe.Fori(FIRST, B - 3, 2) as c:
                a_iter(c, 0)
                a_iter(c + 1, 1)
            a_iter(B - 2, 0)
            a_iter(B - 1, 1, nxt=False)
            a_iter(B, 0, now=False, nxt=False)
            project(B - 1)
            def up(n, w, e, tokens, sems, free):
                for f in range(FC):
                    wait(pe, s[sems[1]], FC * (n - 1) + f + 1 if free else 0)
                    mm(big[f // 2][:, (f % 2) * CW:(f % 2 + 1) * CW], w[:, e, f * P:(f + 1) * P], tokens,
                       start=True, stop=True).then_inc(s[sems[0]], 1)

            def b_tx(n, r):
                pe.wait_ge(got_x[r], nth(n, r))
                for t in range(SW // P):
                    ins = pe.transpose(bank[0][:, t * P:(t + 1) * P], x_row[:, r, t, :], ident[:, :])
                ins.then_inc(s["b_tx"], 1)

            def b_up(n, u, r, first=False):
                pe.wait_ge(s["b_xt"], n + 1)
                pe.wait_ge(got_w[r], nth(n, r))
                if not first:
                    pe.wait_ge(s["b_act"], n - 1)
                for f in range(FC):
                    ins = mm(big[u][:, f * SW:(f + 1) * SW], wb[:, r, f * P:(f + 1) * P], xt[:, u, :], start=True, stop=True)
                ins.then_inc(s["b_up"], 1)

            def b_down(n, u, r, first=False):
                pe.wait_ge(s["b_act"], n + 1)
                if not first:
                    pe.wait_ge(s["b_yr"], n - 1)
                for t in range(SW // P):
                    for f in range(FC):
                        ins = mm(bank[2 + u][:, t * D:(t + 1) * D], hid0[:, u, f, t * P:(t + 1) * P], wb[:, r, F + f * D:F + (f + 1) * D],
                                 start=(f == 0), stop=(f == FC - 1))
                ins.then_inc(s["b_y"], 1)

            def b_tx_next(n, r):
                hold(pe, s["b_xt"], n, s["held_pe"])
                b_tx(n, r)

            def b_step(n, i):
                b_up(n + 1, (i + 1) % 2, (i + 1) % DEEP)
                b_tx_next(n + 2, (i + 2) % DEEP)
                b_down(n, i % 2, i)

            b_tx(0, 0)
            b_tx_next(1, 1)
            b_up(0, 0, 0, first=True)
            b_up(1, 1, 1, first=True)
            hold(pe, s["b_xt"], 2, s["held_pe"])
            route_group(1)
            b_tx_next(2, 2)
            b_down(0, 0, 0, first=True)
            rank_group(1)
            b_up(2, 0, 2)
            b_tx_next(3, 3)
            b_down(1, 1, 1, first=True)
            rest = (GR * NB - 4) % DEEP
            with pe.Fori(2, GR * NB - 2 - rest - DEEP + 1, DEEP) as n:
                for i in range(DEEP):
                    b_step(n + i, (2 + i) % DEEP)
            for n in range(GR * NB - 2 - rest, GR * NB - 2):
                b_step(n, n % DEEP)
            n = GR * NB - 2
            b_up(n + 1, (n + 1) % 2, (n + 1) % DEEP)
            b_down(n, n % 2, n % DEEP)
            b_down(n + 1, (n + 1) % 2, (n + 1) % DEEP)
            def c_tz(c, u):
                pe.wait_ge(s["c_z"], c + 1)
                transposes(bank[0], z[:, TPB * u:TPB * u + TPB, :], TPB, s["c_tz"])

            def c_scores(c, u):
                pe.wait_ge(s["c_zt"], c + 1)
                for t in range(TPB):
                    dst = big[u][:, t * S:(t + 1) * S]
                    mm(dst, q[:, u, t * P:(t + 1) * P], k1[:, bass.ds(c, 1), :], start=True, stop=False)
                    ins = mm(dst, ident[:, :], cell[:, bass.ds(TPB * c + t, 1), :], start=False, stop=True)
                ins.then_inc(s["c_s"], 1)

            def c_iter(c, u, ahead=2, free=True):
                hold(pe, s["c_exp"], c + 1, s["held_pe"])
                transposes(bank[1], e1[:, u, :, :], TPB, s["c_tp"], cols=S)
                if ahead >= 1:
                    c_scores(c + 1, 1 - u)
                pe.wait_ge(s["c_pt"], c + 1)
                if free:
                    pe.wait_ge(s["c_read"], c)
                for t in range(TPB):
                    ins = mm(bank[3][:, t * D:(t + 1) * D], pt1[:, t * P:(t + 1) * P], v1[:, bass.ds(c, 1), :],
                             start=True, stop=True)
                ins.then_inc(s["c_o"], 1)
                if ahead >= 2:
                    c_tz(c + 2, u)

            hold(pe, s["b_xt"], GR * NB, s["held_pe"])
            pe.wait_ge(s["b_yr"], GR * NB)
            pe.wait_ge(s["b_act"], GR * NB)
            pe.wait_ge(s["pool_setup"], 2 + TPB)
            c_tz(0, 0)
            c_scores(0, 0)
            c_tz(1, 1)
            c_iter(0, 0, free=False)
            with pe.Fori(1, BG - 4, 2) as c:
                c_iter(c, 1)
                c_iter(c + 1, 0)
            c_iter(BG - 3, 1)
            c_iter(BG - 2, 0)
            with pe.Fori(BG - 1, B - 4, 2) as c:
                c_iter(c, 1)
                c_iter(c + 1, 0)
            c_iter(B - 3, 1)
            c_iter(B - 2, 0, ahead=1)
            c_iter(B - 1, 1, ahead=0)
            loaded(pe, "ld_e1")
            pe.wait_ge(s["x_done"], 1)
            route_products(range(CHUNKS, 2 * CHUNKS), 1,
                           lambda c: z_all[:, CT * (c - CHUNKS):CT * (c - CHUNKS) + CT, :], zt2d, bank[2],
                           lambda t: (t % TPB) * B * E + t // TPB * E)
            pe.wait_ge(s["d_pr"], 1)
            for j in range(TPB):
                ins = pe.transpose(bank[0][:, j * P:(j + 1) * P], gate[:, :, :].rearrange("p (j b) e -> p j (b e)", j=TPB)[:, j, :], ident[:, :])
            ins.then_inc(s["d_rows"], 1)
            pe.wait_ge(s["d_best"], 1)
            for k, rows in enumerate((best_no, best)):
                for h in range(2):
                    ins = mm(bank[1][CAP * h:CAP * h + CAP, k * P:(k + 1) * P], rows[:, :], ident[:, :], start=True, stop=True)
            ins.then_inc(s["d_cols"], 1)

            def turn(b, u, free=True):
                pe.wait_ge(s["d_hot"], b + 1)
                if free:
                    pe.wait_ge(s["d_sel"], b)
                for j in range(TPB):
                    for k in range(FC):
                        o = (j * FC + k) * P
                        ins = pe.transpose(bank[0][:, o // 2:(o + P) // 2].bitcast(F16), one_hot[:, u, k, j * P:(j + 1) * P],
                                           ident16[:, :])
                ins.then_inc(s["d_ht"], 1)

            def pick_tokens(b, u, free=True):
                pe.wait_ge(s["d_z"], b + 1)
                pe.wait_ge(s["d_sel"], b + 1)
                if free:
                    pe.wait_ge(s["d_xge"], b)
                for j in range(TPB):
                    for piece in (z_hi, z_lo):
                        ins = mm(bank[1][:, :], piece[:, u, j, :], sel[:, u, j, :], start=(j == 0 and piece is z_hi),
                                 stop=(j == TPB - 1 and piece is z_lo))
                ins.then_inc(s["d_xg"], 1)

            def d_up(half, e):
                n = E * half + e
                up(n, w_up1, e, taken[half][:, e, :, :], ("d_up", "d_act"), n > 0)

            def d_down(half, e):
                n = E * half + e
                pe.wait_ge(s["d_act"], FC * (n + 1))
                if n >= 2:
                    pe.wait_ge(s["d_yt"], n - 1)
                for f in range(FC):
                    ins = mm(bank[2 + e % 2][:, :], w_down1[:, e, f, :], hid[:, e % 2, f, :],
                             start=(f == 0), stop=(f == FC - 1))
                ins.then_inc(s["d_y"], 1)

            def turn_outputs(b):
                if b > 0:
                    pe.wait_ge(s["d_ys"], b)
                for k in range(FC):
                    ins = pe.transpose(bank[0][:, k * P:(k + 1) * P], yt[b // HB][:, b % HB, 2 * k:2 * k + 2, :], ident[:, :])
                ins.then_inc(s["d_ty"], 1)

            def give_back(b):
                pe.wait_ge(s["d_ys"], b + 1)
                pe.wait_ge(s["d_gated"], b + 1)
                if b > 0:
                    pe.wait_ge(s["d_o"], b)
                for j in range(TPB):
                    for k in range(FC):
                        ins = mm(bank[1][:, j * D:(j + 1) * D], gated[:, b % 2, k, j * P:(j + 1) * P], y_slots[:, b % 2, k, :],
                                 start=(k == 0), stop=(k == FC - 1))
                ins.then_inc(s["d_out0"], 1)

            turn(0, 0, False)
            turn(1, 1)
            pick_tokens(0, 0, False)
            with pe.Fori(2, HB - 1, 2) as b:
                turn(b, 0)
                pick_tokens(b - 1, 1)
                turn(b + 1, 1)
                pick_tokens(b, 0)
            pick_tokens(HB - 1, 1)
            pe.wait_ge(s["d_xge"], HB)
            d_up(0, 0)
            for e in range(E):
                if e + 1 < E:
                    d_up(0, e + 1)
                turn(HB + e, e % 2)
                d_down(0, e)
                pick_tokens(HB + e, e % 2)
            pe.wait_ge(s["d_xge"], B)
            pe.wait_ge(s["d_yt"], E)
            d_up(1, 0)
            for e in range(E):
                if e + 1 < E:
                    d_up(1, e + 1)
                turn_outputs(e)
                d_down(1, e)
                give_back(e)
            pe.wait_ge(s["d_yt"], 2 * E)
            turn_outputs(HB)
            for b in range(HB, B):
                if b + 1 < B:
                    turn_outputs(b + 1)
                give_back(b)

        @block.vector
        def _(dve):
            ch = Chain(dve, s["dve"])

            def stats_of(t0, n):
                hold(dve, ch.sem, ch.base + ch.k, s["held_dve"])
                for t in range(n):
                    ch.done(dve.bn_stats(stats[:, t, :], x[:, bass.ds(t0 + t, 1), :].squeeze(1)))

            def stats_merged(n):
                hold(dve, ch.sem, ch.base + ch.k, s["held_dve"])
                for t in range(n):
                    ch.done(dve.bn_aggr(mv[:, t, :], stats[:, t, :]))

            def stats_kept(t0, n):
                dve.wait_ge(ch.sem, ch.base + ch.k)
                ch.done(dve.tensor_copy(mean_var[:, bass.ds(t0, n), :], mv[:, 0:n, :]))

            def tile_stats(t0, n):
                stats_of(t0, n)
                stats_merged(n)
                stats_kept(t0, n)
                dve.wait_ge(ch.sem, ch.base + ch.k)

            def layer_norm(n, i, tiles=slice(0, T), asked=False):
                if not asked:
                    dve.drain().then_inc(s["ln_sqrt"], 1)
                dve.wait_ge(s["act_setup"], i + 1)
                of = 1 - n % 2, tiles
                ch.link(dve.reciprocal(rstd[:, *of], rstd[:, *of]))
                ch.link(dve.scalar_tensor_tensor(shift[:, *of], mean_var[:, tiles, 0], -1.0, rstd[:, *of], ALU.mult, ALU.mult))

            def normalize(layer, t0, n, done, rows=z):
                for t in range(n):
                    tile = bass.ds(t0 + t, 1)
                    ins = dve.tensor_scalar(rows[:, t, :], x[:, tile, :].squeeze(1), rstd[:, 1 - layer % 2, tile],
                                            shift[:, 1 - layer % 2, tile], ALU.mult, ALU.add)
                ins.then_inc(s[done], 1)

            for c in range(CHUNKS):
                if c % (CHUNKS // X_LOADS) == 0:
                    dve.wait_ge(ld_x[c // (CHUNKS // X_LOADS)], 16)
                tile_stats(CT * c, CT)
            dve.drain().then_inc(s["ln_sqrt"], 1)
            dve.wait_ge(s["ld_const"], 16 * LOADS["ld_const"])
            loaded(dve, "ld_keys")
            loaded(dve, "ld_kv")
            for h in range(2):
                dve.wait_ge(s["pe_setup"], 1 + h)
                dve.tensor_scalar(k0[:, 8 * h:8 * h + 8, :], bank[h][:, :].rearrange("p (b s) -> p b s", s=S),
                                  k_b[:, 0:1], None, ALU.add)\
                    .then_inc(s["dve_setup"], 1)
            ch.done(dve.tensor_copy(before16[:, :], before[:, :]))
            ch.done(dve.tensor_copy(ident16[:, :], ident[:, :]))
            ch.done(dve.tensor_copy(head_pick16[:, :, :], head_pick[:, :, :]))
            dve.tensor_scalar(key_row[:, :, :], mask_row4[:, :].bitcast(U8).rearrange("p (b s) -> p b s", s=S), MASKED, None,
                              ALU.mult).then_inc(s["dve_setup"], 1)
            dve.tensor_scalar(key_bias[:, :], mask4[:, :].bitcast(U8), MASKED, None, ALU.mult).then_inc(s["dve_setup"], 1)
            dve.wait_ge(s["act_setup"], 1)
            layer_norm(1, 1, asked=True)

            def add_projected(c):
                wait(dve, s["a_pj"], c + 1)
                xs = x[:, bass.ds(TPB * c, TPB), :]
                ch.link(dve.scalar_tensor_tensor(xs, bank[3][:, 0:N].rearrange("p (t d) -> p t d", t=TPB),
                                                 tg[:, 0:1], xs, ALU.mult, ALU.add))
                dve.sem_inc(s["a_read"], 1)
                tile_stats(TPB * c, TPB)

            def a_iter(c, now=True, last=True, proj=True, nxt=True):
                if now:
                    for t in range(TPB):
                        wait(dve, s["a_s"], TPB * c + t + 1)
                        wait(dve, s["a_tm"], c)
                        dve.tensor_reduce(neg_max[:, t, :], big[t][:, :].rearrange("p (h s) -> p h s", s=S), AX.X,
                                          ALU.max, negate=True).then_inc(s["a_max"], 1)
                if nxt:
                    wait(dve, s["a_tz"], c + 2)
                    normalize(1, TPB * (c + 2), TPB, "a_z")
                if proj:
                    add_projected(c - 2)
                if last:
                    wait(dve, s["a_av"], c)
                    o = bank[2][:, 0:TPB * H * (DH + 1)].rearrange("p (t h d) -> p t h d", t=TPB, h=H)
                    ch.link(dve.reciprocal(inv[:, :, :], o[:, :, :, DH]))
                    dve.tensor_tensor(on[:, :, :].rearrange("p t (h d) -> p t h d", h=H), o[:, :, :, 0:DH],
                                      inv[:, :, :].unsqueeze(3).broadcast_to([P, TPB, H, DH]), ALU.mult)\
                        .then_inc(s["a_on"], 1)

            normalize(1, 0, TPB, "a_z")
            dve.wait_ge(s["pool_setup"], 1)
            for h in range(2):
                dve.wait_ge(s["pe_setup"], 5 + h)
                for k in range(2):
                    r = slice(S * k, S * k + S)
                    for j in range(2):
                        v = big[h][r, 512 * j:512 * j + 512].rearrange("p (b h k d) -> p b h k d", b=4, h=PAIRS, k=2)
                        bias = v_b[r, :].rearrange("p (h k d) -> p h k d", h=PAIRS, k=2)[:, :, k, :]
                        b0 = 8 * h + 4 * j
                        ins = dve.tensor_tensor(vals0[r, b0:b0 + 4, :, k * (DH + 1):k * (DH + 1) + DH], v[:, :, :, k, :],
                                                bias.unsqueeze(1).broadcast_to([S, 4, PAIRS, DH]), ALU.add)
                        if (k, j) == (1, 1):
                            ins.then_inc(s["dve_setup"], 1)
            dve.wait_ge(s["ld_r"], 16 * LOADS["ld_r"])
            loaded(dve, "ld_w")
            for h in range(2):
                dve.wait_ge(s["pe_setup"], 3 + h)
                ins = dve.tensor_scalar(k1[:, 8 * h:8 * h + 8, :], bank[2 + h][:, :].rearrange("p (b s) -> p b s", s=S),
                                        bk1[:, 0:1], None, ALU.add)
            for h in range(2):
                dve.wait_ge(s["pe_setup"], 7 + h)
                dve.tensor_tensor(v1[:, 8 * h:8 * h + 8, :], big[h][0:S, :].rearrange("p (b d) -> p b d", d=D),
                                  bo1[0:S, :].unsqueeze(1).broadcast_to([S, 8, D]), ALU.add)\
                    .then_inc(s["dve_setup"], 1)

            dve.sem_inc(s["a_read"], 1)
            dve.wait_ge(s["a_tz"], 1)
            normalize(1, TPB, TPB, "a_z")
            a_iter(0, last=False, proj=False)
            a_iter(1, proj=False)
            per = 2 + 2 * TPB + 1
            base = ch.k
            with dve.Fori(2, FIRST - 1, 2) as c:
                ch.start(base + per * (c - 2))
                a_iter(c)
                a_iter(c + 1)
                assert ch.k == 2 * per
            ch.start(0, base + per * (FIRST - 2))

            def link_all():
                dve.wait_ge(ch.sem, ch.base + ch.k)

            lanes_all = lanes[:, :].unsqueeze(1).broadcast_to([P, TG, E])

            def route_group(g):
                tiles = slice(TG * g, TG * (g + 1))
                layer_norm(2, 2 + g, tiles)
                if g == 1:
                    dve.wait_ge(s["pool_setup"], 2 + TPB)
                for c in range(CG * g, CG * (g + 1)):
                    normalize(2, CT * c, CT, "r_z", z_all[:, CT * c:CT * c + CT, :])
                dve.wait_ge(s["r_lg"], CG * (g + 1))
                ch.link(dve.tensor_copy(lg[:, tiles, :], bank[2 + g][:, 0:TG * E].rearrange("p (t e) -> p t e", e=E)))
                for t in range(TG * g, TG * (g + 1)):
                    ch.done(dve.max(top8[:, t, :], lg[:, t, :]))
                link_all()
                dve.tensor_tensor(pick[:, 0, tiles], top8[:, tiles, 0], top8[:, tiles, 1], ALU.subtract).then_inc(s["r_d"], 1)
                for t in range(TG * g, TG * (g + 1)):
                    ch.done(dve.max_index(idx8[:, t, :], top8[:, t, :], lg[:, t, :]))
                dve.wait_ge(s["r_exp"], g + 1)
                link_all()
                ch.link(dve.tensor_copy(pick[:, :, tiles], idx8[:, tiles, 0:2].rearrange("p t k -> p k t")))
                for k, dst in enumerate((hot0, hot1)):
                    ch.done(dve.tensor_tensor(dst[:, tiles, :], lanes_all, pick[:, k, tiles].unsqueeze(2).broadcast_to([P, TG, E]),
                                              ALU.is_equal))
                link_all()
                dve.tensor_tensor(hot16[:, tiles, :], hot0[:, tiles, :], hot1[:, tiles, :], ALU.add).then_inc(s["b_hot"], 1)
                for k in range(2):
                    ch.link(dve.tensor_scalar(part[:, 1 - k, tiles], part[:, 0, tiles], -0.5 if k == 0 else 0.5, 0.5,
                                              ALU.mult, ALU.add))
                ch.done(dve.tensor_scalar(part[:, :, tiles], part[:, :, tiles], tg[:, 2:3], None, ALU.mult))
                dve.wait_ge(s["b_rank"], g + 1)
                prefix = bank[1][:, 0:TG * E].rearrange("p (t e) -> p t e", e=E)
                totals = bank[1][:, TG * E:2 * TG * E].rearrange("p (t e) -> p e t", e=E)
                ch.link(dve.tensor_copy(tot[:, :, :], totals))
                flat_tot, flat_cum = tot[:, :, :].rearrange("p e t -> p (e t)"), cum[:, :, :].rearrange("p e t -> p (e t)")
                ch.done(dve.reduce_sum(cnt[:, 0, :], tot[:, :, :], AX.X))
                ch.link(dve.tensor_tensor_scan(flat_cum, flat_tot, zero_e[:, :], 0.0, ALU.add, ALU.add))
                ch.done(dve.tensor_tensor(flat_cum, flat_cum, flat_tot, ALU.subtract))
                ch.link(dve.tensor_scalar(cnt_i[:, 0, :], cnt[:, 0, :], float(SW - 1), None, ALU.add))
                ch.link(dve.tensor_scalar(cnt_i[:, 1, :], cnt_i[:, 0, :], -SW, None, ALU.bitwise_and))
                ch.link(dve.tensor_copy(cnt[:, 1, :], cnt_i[:, 1, :]))
                ch.link(dve.tensor_tensor_scan(cnt[:, 2, :], cnt[:, 1, :], zero_e[:, 0:E], 0.0, ALU.add, ALU.add))
                ch.link(dve.tensor_tensor(cnt[:, 3, :], cnt[:, 2, :], cnt[:, 1, :], ALU.subtract))
                ch.link(dve.tensor_tensor(cnt[:, 3, :], cnt[:, 3, :], cum[:, :, 0], ALU.subtract))
                ch.link(dve.tensor_tensor(cum[:, :, :], cum[:, :, :], cnt[:, 3, :].unsqueeze(2).broadcast_to([P, E, TG]), ALU.add))
                ch.link(dve.tensor_tensor(ranks[:, :, :], prefix, cum[:, :, :].rearrange("p e t -> p t e"), ALU.add))
                dve.sem_inc(s["b_read"], 1)
                for k, hot in enumerate((hot0, hot1)):
                    ch.link(dve.tensor_tensor(scr[:, TG * k:TG * (k + 1), :], hot[:, tiles, :], ranks[:, :, :], ALU.mult))
                for k in range(2):
                    ch.done(dve.reduce_sum(posf[:, k, tiles], scr[:, TG * k:TG * (k + 1), :], AX.X))
                ch.link(dve.tensor_tensor(starts[:, :, :], cnt[0:1, 2, :].unsqueeze(1).broadcast_to([1, NB, E]),
                                          block_start[:, :].unsqueeze(2).broadcast_to([1, NB, E]), ALU.is_le))
                ch.link(dve.reduce_sum(expertf[:, :], starts[:, :, :], AX.X))
                ch.link(dve.tensor_scalar(expert[:, NB * g:NB * (g + 1)], expertf[:, :], float(E - 1), None, ALU.min))
                dve.tensor_copy(pos[:, :, tiles], posf[:, :, tiles]).then_inc(s["b_pos"], 1)

            route_group(0)
            base = ch.k
            with dve.Fori(FIRST, B - 3, 2) as c:
                ch.start(base + per * (c - FIRST))
                a_iter(c)
                a_iter(c + 1)
                assert ch.k == 2 * per
            ch.start(0, base + per * (B - 2 - FIRST))
            a_iter(B - 2, nxt=False)
            a_iter(B - 1, nxt=False)
            a_iter(B, now=False, nxt=False)
            add_projected(B - 1)
            route_group(1)

            def y_out(n, r, first=False):
                dve.wait_ge(s["b_y"], n + 1)
                if not first:
                    dve.wait_ge(kept[r], nth(n - DEEP, r))
                dve.tensor_copy(y_row[:, r, :, :], bank[2 + r % 2][:, 0:SW].rearrange("p (t d) -> p t d", d=D))\
                    .then_inc(s["b_yr"], 1)

            def combine(t0, r):
                for k in range(2):
                    for i in range(2):
                        xs_t = x[:, bass.ds(t0 + i, 1), :].squeeze(1)
                        dve.wait_ge(gathered[2 * r + 2 * k + i], 4 * (t0 - r) + 16)
                        if k:
                            dve.wait_ge(s["b_add"], 2 * t0 + i + 1)
                        dve.scalar_tensor_tensor(xs_t, yg[:, 2 * r + 2 * k + i, :], part[:, k, bass.ds(t0 + i, 1)], xs_t,
                                                 ALU.mult, ALU.add).then_inc(s["b_add"], 1)
                dve.wait_ge(s["b_add"], 2 * t0 + 4)
                tile_stats(t0, 2)

            for n in range(DEEP):
                y_out(n, n, first=True)
            with dve.Fori(DEEP, NB - DEEP + 1 - NB % DEEP, DEEP) as n:
                for i in range(DEEP):
                    y_out(n + i, i)
            for n in range(NB - NB % DEEP, NB + 3):
                y_out(n, n % DEEP)
            base, per = ch.k, 5
            n0 = NB + 3
            with dve.Fori(0, TG // (RING // 2)) as lap:
                t = RING // 2 * lap
                ch.start(base + per * RING // 4 * lap)
                for i in range(0, RING // 2, 2):
                    for j in range(2):
                        y_out(t + n0 + i + j, (n0 + i + j) % DEEP)
                    combine(t + i, i)
                assert ch.k == per * RING // 4
            ch.start(0, base + per * TG // 2)
            for n in range(n0 + TG, GR * NB):
                y_out(n, n % DEEP)
            layer_norm(3, 4, slice(0, TG))
            dve.wait_ge(s["pool_setup"], 2 + TPB)

            def c_norm(c, u):
                normalize(3, TPB * c, TPB, "c_z", z[:, TPB * u:TPB * u + TPB, :])

            def c_max(c, u):
                dve.wait_ge(s["c_s"], c + 1)
                dve.tensor_reduce(nm1[:, u, :], big[u][:, 0:TPB * S].rearrange("p (t s) -> p t s", t=TPB), AX.X, ALU.max,
                                  negate=True).then_inc(s["c_max"], 1)

            def c_iter(c, u, ahead=2, stats_too=True):
                if ahead >= 2:
                    dve.wait_ge(s["c_tz"], c + 1)
                    c_norm(c + 2, u)
                if stats_too:
                    stats_of(TPB * (c - 1), TPB)
                if ahead >= 1:
                    c_max(c + 1, 1 - u)
                if stats_too:
                    stats_merged(TPB)
                dve.wait_ge(s["c_o"], c + 1)
                ch.done(dve.reciprocal(inv1[:, u, :], sum1[:, u, :]))
                if stats_too:
                    stats_kept(TPB * (c - 1), TPB)
                link_all()
                ch.link(dve.tensor_scalar(inv1[:, u, :], inv1[:, u, :], tg[:, 1:2], None, ALU.mult))
                for t in range(TPB):
                    xs = x[:, bass.ds(TPB * c + t, 1), :].squeeze(1)
                    ch.done(dve.scalar_tensor_tensor(xs, bank[3][:, t * D:(t + 1) * D], inv1[:, u, t:t + 1], xs,
                                                     ALU.mult, ALU.add))
                link_all()
                dve.sem_inc(s["c_read"], 1)

            c_norm(0, 0)
            c_norm(1, 1)
            c_max(0, 0)
            c_iter(0, 0, stats_too=False)
            combine(TG, 0)
            base = ch.k
            per_c, per_b = 2 + TPB + 2 * TPB + 1, per
            with dve.Fori(1, BG - 4, 2) as c:
                ch.start(base + (per_c + per_b) * (c - 1))
                for i in range(2):
                    c_iter(c + i, 1 - i)
                    combine(TG + TPB * (c + i), (TPB * (1 + i)) % (RING // 2))
                assert ch.k == 2 * (per_c + per_b)
            ch.start(0, base + (per_c + per_b) * (BG - 4))
            c_iter(BG - 3, 1)
            for c in range(BG - 3, BG):
                combine(TG + TPB * c, (TPB * c) % (RING // 2))
            layer_norm(3, 5, slice(TG, T))
            c_iter(BG - 2, 0)
            base = ch.k
            with dve.Fori(BG - 1, B - 4, 2) as c:
                ch.start(base + per_c * (c - BG + 1))
                c_iter(c, 1)
                c_iter(c + 1, 0)
                assert ch.k == 2 * per_c
            ch.start(0, base + per_c * (B - 3 - (BG - 1)))
            c_iter(B - 3, 1)
            c_iter(B - 2, 0, ahead=1)
            c_iter(B - 1, 1, ahead=0)
            tile_stats(TPB * (B - 1), TPB)
            dve.drain().then_inc(s["x_done"], 1)
            layer_norm(4, 6)
            for c in range(CHUNKS):
                normalize(4, CT * c, CT, "r_z", z_all[:, CT * c:CT * c + CT, :])
            dve.wait_ge(s["r_lg"], 2 * CHUNKS)
            ch.link(dve.tensor_copy(lg[:, :, :], bank[2][:, 0:T * E].rearrange("p (t e) -> p t e", e=E)))
            ch.link(dve.tensor_reduce(pick[:, 0, :], lg[:, :, :], AX.X, ALU.max, negate=True))
            dve.tensor_tensor(lg[:, :, :], lg[:, :, :], pick[:, 0, :].unsqueeze(2).broadcast_to([P, T, E]), ALU.add)\
                .then_inc(s["r_d"], 1)
            dve.wait_ge(s["r_exp"], GR + 1)
            ch.link(dve.reduce_sum(pick[:, 0, :], scr[:, :, :], AX.X))
            ch.link(dve.reciprocal(pick[:, 0, :], pick[:, 0, :]))
            dve.tensor_tensor(gate[:, :, :], scr[:, :, :], pick[:, 0, :].unsqueeze(2).broadcast_to([P, T, E]), ALU.mult)\
                .then_inc(s["d_pr"], 1)
            dve.wait_ge(s["d_rows"], 1)
            ch.link(dve.tensor_copy(left[:, 0, :], bank[0][:, 0:N]))
            for i in range(CAP // 8):
                eight = slice(8 * i, 8 * i + 8)
                ch.link(dve.max(best[:, eight], left[:, i % 2, :]))
                ch.done(dve.max_index(best_at[:, eight], best[:, eight], left[:, i % 2, :]))
                ch.link(dve.match_replace(left[:, 1 - i % 2, :], best[:, eight], left[:, i % 2, :], -1.0))
            dve.tensor_copy(best_no[:, :], best_at[:, :]).then_inc(s["d_best"], 1)
            dve.wait_ge(s["d_cols"], 1)
            for h in range(2):
                rows = slice(CAP * h, CAP * h + CAP)
                ch.done(dve.tensor_copy(slots[rows, :, :, :],
                                        bank[1][rows, 0:2 * P].rearrange("p (n b k h) -> p n b k h", n=2, b=B, k=FC)[:, :, :, :, h]))
            link_all()

            def column(n, b, k):
                return slots[:, n, bass.ds(b, 1), k:k + 1].squeeze(1)

            def mark(b, u, free=True, again=False):
                if free:
                    dve.wait_ge(s["d_ht"], b - 1)
                for k in range(FC):
                    ins = dve.tensor_scalar(one_hot[:, u, k, :], token_no[:, :], column(0, b, k), None, ALU.is_equal)
                ins.then_inc(s["d_hot"], 1)
                if free:
                    dve.wait_ge(s["d_xg"], b - 1)
                if again:
                    zs = z[:, TPB * u:TPB * u + TPB, :]
                    for t in range(TPB):
                        tile = bass.ds(TPB * b + t, 1)
                        ch.done(dve.tensor_scalar(zs[:, t, :], x[:, tile, :].squeeze(1), rstd[:, 1, tile], shift[:, 1, tile],
                                                  ALU.mult, ALU.add))
                    link_all()
                else:
                    zs = z_all[:, bass.ds(TPB * b, TPB), :]
                ch.link(dve.tensor_scalar(z_hi[:, u, :, :], zs, SPLIT, None, ALU.mult))
                dve.scalar_tensor_tensor(z_lo[:, u, :, :], zs, SPLIT, z_hi[:, u, :, :], ALU.mult, ALU.subtract)\
                    .then_inc(s["d_z"], 1)

            def gate_slots(b):
                if b >= 2:
                    dve.wait_ge(s["d_out0"], b - 1)
                for k in range(FC):
                    ins = dve.tensor_scalar(gated[:, b % 2, k, :], token_no[:, :], column(0, b, k), column(1, b, k),
                                            ALU.is_equal, ALU.mult)
                ins.then_inc(s["d_gated"], 1)

            def keep_outputs(half, e):
                dve.wait_ge(s["d_y"], E * half + e + 1)
                dve.tensor_copy(yt[half][:, :, e, :], bank[2 + e % 2][:, :].rearrange("p (b s) -> p b s", b=HB))\
                    .then_inc(s["d_yt"], 1)

            def add_outputs(b):
                dve.wait_ge(s["d_out0"], b + 1)
                if b > 0:
                    dve.wait_ge(s["d_out"], b)
                ch.link(dve.tensor_copy(o16[:, :, :], bank[1][:, 0:N].rearrange("p (t d) -> p t d", t=TPB)))
                dve.sem_inc(s["d_o"], 1)
                xs = x[:, TPB * b:TPB * b + TPB, :]
                dve.scalar_tensor_tensor(xs, o16[:, :, :], tg[:, 3:4], xs, ALU.mult, ALU.add).then_inc(s["d_out"], 1)

            mark(0, 0, free=False)
            mark(1, 1, free=False)
            base, per = ch.k, 1
            with dve.Fori(2, HB - 1, 2) as b:
                ch.start(base + per * (b - 2))
                mark(b, 0)
                mark(b + 1, 1)
                assert ch.k == 2 * per
            ch.start(0, base + per * (HB - 2))
            mark(HB, 0, again=True)
            for e in range(E):
                if e + 1 < E:
                    mark(HB + e + 1, (e + 1) % 2, again=True)
                keep_outputs(0, e)
            gate_slots(0)
            for e in range(E):
                gate_slots(e + 1)
                keep_outputs(1, e)
                add_outputs(e)
            for b in range(HB, B):
                if b + 1 < B:
                    gate_slots(b + 1)
                add_outputs(b)


def bcast_rows(src):
    n = src.shape[0]
    return src.rearrange("(a n) -> a n", a=1).broadcast_to([P, n])


_OUT = (B * N, D)


def kernel(**inputs):
    import numpy as np
    import concourse.bacc as bacc
    from concourse.bass_utils import run_bass_kernel_spmd

    g = {k: np.asarray(v) for k, v in inputs.items()}
    flat = np.ascontiguousarray
    mask = g["mask_BxS2_bk0"].view(np.uint8)
    pair = np.arange(H)[:, None, None] == 2 * np.arange(PAIRS)[None, :, None] + (np.arange(P) // S)[None, None, :]
    arrays = {
        "x": flat(g["x"].reshape(B * N, D)),
        "ctx_t": flat(g["ctx_1024"].transpose(2, 0, 1)),
        "mask_t": flat(np.concatenate([mask.T, mask.T])).view(np.uint32),
        "mask_row": flat(mask.reshape(1, B * S)).view(np.uint32),
        "cell": flat(g["mask_BxSxS2_ff1"].reshape(B * N, S)),
        "seq": flat(g["mask_BxS2_ff1"].reshape(B * S)),
        "g_xattn": flat(g["g_xattn"]),
        "g_ffn": flat(g["g_ffn"]),
        "q_w": flat(g["L0_xattn_q_w"]),
        "q_b": flat(g["L0_xattn_q_b"]),
        "kv_w": flat(g["L0_xattn_kv_w"]),
        "kv_b": flat(g["L0_xattn_kv_b"]),
        "proj_w": flat(g["L0_xattn_proj_w"]),
        "proj_b": flat(g["L0_xattn_proj_b"]),
        "wk_t": flat(g["L1_xattn_W_k"].T),
        "b_k": flat(g["L1_xattn_b_k"]),
        "wo_t": flat(g["L1_xattn_W_o"].T),
        "b_o": flat(g["L1_xattn_b_o"]),
        "route": flat(np.stack([g["L0_ffn_Wg"].T, g["L1_ffn_gate_w"]], axis=1)),
        "w0": flat(np.concatenate([
            g["L0_ffn_W1"], g["L0_ffn_W2"].reshape(E, FC, P, D).transpose(0, 2, 1, 3).reshape(E, P, F),
        ], axis=2)),
        "w_up1": flat(g["L1_ffn_w1"].transpose(1, 0, 2)),
        "w_down1": flat(g["L1_ffn_w2"].reshape(E, FC, P, D).transpose(2, 0, 1, 3)),
        "ident": np.eye(P, dtype=np.float32),
        "head_rows": ((np.arange(P) // DH)[:, None] == np.arange(H)).astype(np.float32),
        "head_pick": pair.astype(np.float32),
        "token_no": np.tile(np.arange(N, dtype=np.float32), (P, 1)),
        "before": np.triu(np.ones((P, P), np.float32), 1),
        "block_start": np.arange(NB, dtype=np.float32)[None] * SW,
        "lanes": np.tile(np.arange(E, dtype=np.float32), (P, 1)),
    }
    nc = bacc.Bacc("TRN2", target_bir_lowering=False, num_devices=1)
    aps = {}
    for name, v in arrays.items():
        aps[name] = nc.dram_tensor(f"in_{name}", v.shape, mybir.dt.from_np(v.dtype), kind="ExternalInput").ap()
    out = nc.dram_tensor("out", _OUT, F32, kind="ExternalOutput").ap()
    build(nc, aps, out)
    r = run_bass_kernel_spmd(nc, [{f"in_{k}": v for k, v in arrays.items()}], core_ids=[0])
    return r.results[0]["out"].reshape(B, N, D)
```
